# Optimizing a Trainium2 kernel written in Bass

```python
import numpy as np
import jax
import jax.numpy as jnp

def _softmax(x, axis=-1):
    return jax.nn.softmax(x, axis=axis)

def _gelu(x):
    return jax.nn.gelu(x, approximate=True)

def _silu(x):
    return jax.nn.silu(x)

def _sigmoid(x):
    return jax.nn.sigmoid(x)

def _layernorm(x, axis=-1, eps=1e-05):
    m = jnp.mean(x, axis=axis, keepdims=True)
    v = jnp.var(x, axis=axis, keepdims=True)
    return (x - m) / jnp.sqrt(v + eps)

def _scatter_add(tgt, idx, src, axis=0):
    return tgt.at[idx].add(src)

def _segment_sum(src, seg, n):
    return jax.ops.segment_sum(src, seg, n)
kernel_name = 'mk_flamingo_gated_d2_seqx_r4_679b9d'

def setup_inputs(seed: int=0):
    np.random.seed(seed)
    _w = jnp.asarray

    def _rec_inputs():
        import jax
        import jax.numpy as jnp
        _rk = jax.random.key(seed)
        x = 7.22e-05 + 1 * jax.random.normal(jax.random.fold_in(_rk, 1), (4, 1024, 256), jnp.float32)
        _lenS = 1024 - jax.random.randint(jax.random.fold_in(_rk, 7), (4,), 0, max(1, 1024 // 4) + 1, jnp.int32)
        _lenS2 = 77 - jax.random.randint(jax.random.fold_in(_rk, 8), (4,), 0, max(1, 77 // 4) + 1, jnp.int32)
        _ctx_768P = jax.random.normal(jax.random.fold_in(_rk, 11), (4, 16, 192), jnp.float32)
        _ctx_768c = jax.random.dirichlet(jax.random.fold_in(_rk, 511), 0.3 * jnp.ones((16,), jnp.float32), (4, 77))
        _ctx_768t = jnp.einsum('bsk,bkd->bsd', _ctx_768c, _ctx_768P)
        _ctx_768t = _ctx_768t * jax.lax.rsqrt(jnp.mean(jnp.square(_ctx_768t)) + 1e-12) * 0.953939
        ctx_768 = -0.000191848 + 0.999787 * (_ctx_768t + 0.3 * jax.random.normal(jax.random.fold_in(_rk, 611), (4, 77, 192), jnp.float32))
        _g = jax.random.normal(jax.random.fold_in(_rk, 9001), (2, 2), jnp.float32)
        _g = jnp.sign(_g) * jnp.maximum(jnp.abs(_g), 1.0) + (_g == 0) * 1.0
        g_xattn = _g[0]
        g_ffn = _g[1]
        return (x, ctx_768, g_xattn, g_ffn)
    x, ctx_768, g_xattn, g_ffn = _rec_inputs()

    def _L0_xattn_setup():
        import jax, jax.numpy as jnp
        import numpy as np
        NUM_HEADS = 16
        CLAMP = 10000.0
        key = jax.random.key(seed)
        ks = jax.random.split(key, 8)
        B, Nq, Nkv, Cq, Ckv = (4, 512, 512, 256, 192)
        s_q = 1.0 / np.sqrt(Cq)
        s_kv = 1.0 / np.sqrt(Ckv)
        return {'query': jax.random.normal(ks[0], (B, Nq, Cq), jnp.float32), 'key_value': jax.random.normal(ks[1], (B, Nkv, Ckv), jnp.float32), 'Wq': jax.random.normal(ks[2], (Cq, Cq), jnp.float32) * s_q, 'bq': jnp.zeros((Cq,), jnp.float32), 'Wk': jax.random.normal(ks[3], (Ckv, Cq), jnp.float32) * s_kv, 'bk': jnp.zeros((Cq,), jnp.float32), 'Wv': jax.random.normal(ks[4], (Ckv, Cq), jnp.float32) * s_kv, 'bv': jnp.zeros((Cq,), jnp.float32), 'Wo': jax.random.normal(ks[5], (Cq, Cq), jnp.float32) * s_q, 'bo': jnp.zeros((Cq,), jnp.float32)}
    _L0_xattn_all = _L0_xattn_setup()
    _L0_xattn_in = {k: v for k, v in _L0_xattn_all.items() if k in ('Wq', 'bq', 'Wk', 'bk', 'Wv', 'bv', 'Wo', 'bo')}
    del _L0_xattn_all

    def _L0_ffn_setup():
        import jax, jax.numpy as jnp
        import numpy as np
        TOP_K = 2
        key = jax.random.key(seed)
        ks = jax.random.split(key, 6)
        B, L, D, E, F = (2, 512, 256, 8, 1024)
        x = jax.random.normal(ks[0], (B, L, D), dtype=jnp.float32)
        Wg = jax.random.normal(ks[1], (D, E), dtype=jnp.float32) * D ** (-0.5)
        W1 = jax.random.normal(ks[2], (E, D, F), dtype=jnp.float32) * D ** (-0.5)
        b1 = jnp.zeros((E, F), dtype=jnp.float32)
        W2 = jax.random.normal(ks[3], (E, F, D), dtype=jnp.float32) * F ** (-0.5)
        b2 = jnp.zeros((E, D), dtype=jnp.float32)
        return {'x': x, 'Wg': Wg, 'W1': W1, 'b1': b1, 'W2': W2, 'b2': b2}
    _L0_ffn_all = _L0_ffn_setup()
    _L0_ffn_in = {k: v for k, v in _L0_ffn_all.items() if k in ('Wg', 'W1', 'b1', 'W2', 'b2')}
    del _L0_ffn_all

    def _L1_xattn_setup():
        import jax, jax.numpy as jnp
        import numpy as np
        NUM_HEADS = 16
        HEAD_DIM = 64
        INNER = NUM_HEADS * HEAD_DIM
        QUERY_DIM = 256
        CONTEXT_DIM = 192
        SCALE = HEAD_DIM ** (-0.5)
        key = jax.random.key(seed)
        ks = jax.random.split(key, 6)
        B, NQ, NKV = (8, 256, 512)
        query = jax.random.normal(ks[0], (B, NQ, QUERY_DIM), dtype=jnp.float32)
        context = jax.random.normal(ks[1], (B, NKV, CONTEXT_DIM), dtype=jnp.float32)
        w_q = jax.random.normal(ks[2], (QUERY_DIM, INNER), dtype=jnp.float32) * QUERY_DIM ** (-0.5)
        w_kv = jax.random.normal(ks[3], (CONTEXT_DIM, 2 * INNER), dtype=jnp.float32) * CONTEXT_DIM ** (-0.5)
        w_out = jax.random.normal(ks[4], (INNER, QUERY_DIM), dtype=jnp.float32) * INNER ** (-0.5)
        b_out = jax.random.normal(ks[5], (QUERY_DIM,), dtype=jnp.float32) * 0.01
        return {'query': query, 'context': context, 'w_q': w_q, 'w_kv': w_kv, 'w_out': w_out, 'b_out': b_out}
    _L1_xattn_all = _L1_xattn_setup()
    _L1_xattn_in = {k: v for k, v in _L1_xattn_all.items() if k in ('w_q', 'w_kv', 'w_out', 'b_out')}
    del _L1_xattn_all

    def _L1_ffn_setup():
        import jax, jax.numpy as jnp
        import numpy as np

        def _ste(w, w_q):
            return w + jax.lax.stop_gradient(w_q - w)

        def quantize_w8_per(w, axis):
            amax = jnp.clip(jnp.max(jnp.abs(w), axis=axis, keepdims=True), 1e-08, None)
            scale = 127.0 / amax
            w_q = jnp.clip(jnp.round(w * scale), -128.0, 127.0) / scale
            return _ste(w, w_q)

        def quantize_a16(x):
            amax = jnp.clip(jnp.max(jnp.abs(x)), 1e-08, None)
            scale = 32767.0 / amax
            x_q = jnp.clip(jnp.round(x * scale), -32768.0, 32767.0) / scale
            return _ste(x, x_q)
        key = jax.random.key(seed)
        k1, k2, k3 = jax.random.split(key, 3)
        d_model, d_ff = (256, 1024)
        x = jax.random.normal(k1, (4, 512, d_model), dtype=jnp.float32)
        W_in = jax.random.normal(k2, (d_model, d_ff), dtype=jnp.float32) / np.sqrt(d_model)
        b_in = jnp.zeros((d_ff,), dtype=jnp.float32)
        W_out = jax.random.normal(k3, (d_ff, d_model), dtype=jnp.float32) / np.sqrt(d_ff)
        b_out = jnp.zeros((d_model,), dtype=jnp.float32)
        return {'x': x, 'W_in': W_in, 'b_in': b_in, 'W_out': W_out, 'b_out': b_out}
    _L1_ffn_all = _L1_ffn_setup()
    _L1_ffn_in = {k: v for k, v in _L1_ffn_all.items() if k in ('W_in', 'b_in', 'W_out', 'b_out')}
    del _L1_ffn_all
    return {'x': x, 'ctx_768': ctx_768, 'g_xattn': g_xattn, 'g_ffn': g_ffn, 'L0_xattn_Wq': _L0_xattn_in['Wq'], 'L0_xattn_bq': _L0_xattn_in['bq'], 'L0_xattn_Wk': _L0_xattn_in['Wk'], 'L0_xattn_bk': _L0_xattn_in['bk'], 'L0_xattn_Wv': _L0_xattn_in['Wv'], 'L0_xattn_bv': _L0_xattn_in['bv'], 'L0_xattn_Wo': _L0_xattn_in['Wo'], 'L0_xattn_bo': _L0_xattn_in['bo'], 'L0_ffn_Wg': _L0_ffn_in['Wg'], 'L0_ffn_W1': _L0_ffn_in['W1'], 'L0_ffn_b1': _L0_ffn_in['b1'], 'L0_ffn_W2': _L0_ffn_in['W2'], 'L0_ffn_b2': _L0_ffn_in['b2'], 'L1_xattn_w_q': _L1_xattn_in['w_q'], 'L1_xattn_w_kv': _L1_xattn_in['w_kv'], 'L1_xattn_w_out': _L1_xattn_in['w_out'], 'L1_xattn_b_out': _L1_xattn_in['b_out'], 'L1_ffn_W_in': _L1_ffn_in['W_in'], 'L1_ffn_b_in': _L1_ffn_in['b_in'], 'L1_ffn_W_out': _L1_ffn_in['W_out'], 'L1_ffn_b_out': _L1_ffn_in['b_out']}

def reference(x, ctx_768, g_xattn, g_ffn, L0_xattn_Wq, L0_xattn_bq, L0_xattn_Wk, L0_xattn_bk, L0_xattn_Wv, L0_xattn_bv, L0_xattn_Wo, L0_xattn_bo, L0_ffn_Wg, L0_ffn_W1, L0_ffn_b1, L0_ffn_W2, L0_ffn_b2, L1_xattn_w_q, L1_xattn_w_kv, L1_xattn_w_out, L1_xattn_b_out, L1_ffn_W_in, L1_ffn_b_in, L1_ffn_W_out, L1_ffn_b_out):
    import jax
    import jax.numpy as jnp

    def _L0_xattn_ref(query, key_value, Wq, bq, Wk, bk, Wv, bv, Wo, bo):
        import jax, jax.numpy as jnp
        import numpy as np
        NUM_HEADS = 16
        CLAMP = 10000.0
        B, Nq, Cq = query.shape
        Nkv = key_value.shape[1]
        H = NUM_HEADS
        D = Cq // H
        scale = D ** (-0.5)
        q = (query @ Wq + bq).reshape(B, Nq, H, D).transpose(0, 2, 1, 3)
        k = (key_value @ Wk + bk).reshape(B, Nkv, H, D).transpose(0, 2, 1, 3)
        v = (key_value @ Wv + bv).reshape(B, Nkv, H, D).transpose(0, 2, 1, 3)
        attn = jnp.einsum('bhqd,bhkd->bhqk', q, k) * scale
        attn = jnp.clip(attn, -CLAMP, CLAMP)
        attn = jax.nn.softmax(attn, axis=-1)
        attn = jnp.where(jnp.any(jnp.isnan(attn)), jnp.asarray(1.0 / Nkv, attn.dtype), attn)
        x = jnp.einsum('bhqk,bhkd->bqhd', attn, v).reshape(B, Nq, Cq)
        return x @ Wo + bo

    def _L0_ffn_ref(x, Wg, W1, b1, W2, b2):
        import jax, jax.numpy as jnp
        import numpy as np
        TOP_K = 2
        b, l, d = x.shape
        E = Wg.shape[1]
        xt = x.reshape(b * l, d)
        N = xt.shape[0]
        S = jax.nn.sigmoid(xt @ Wg)
        G, I = jax.lax.top_k(S, TOP_K)
        h = jax.nn.gelu(jnp.einsum('nd,edf->enf', xt, W1) + b1[:, None, :])
        y = jnp.einsum('enf,efd->end', h, W2) + b2[:, None, :]
        combine = jnp.zeros((N, E), dtype=x.dtype).at[jnp.arange(N)[:, None], I].add(G)
        out = jnp.einsum('ne,end->nd', combine, y)
        return out.reshape(b, l, d)

    def _L1_xattn_ref(query, context, w_q, w_kv, w_out, b_out):
        import jax, jax.numpy as jnp
        import numpy as np
        NUM_HEADS = 16
        HEAD_DIM = 64
        INNER = NUM_HEADS * HEAD_DIM
        QUERY_DIM = 256
        CONTEXT_DIM = 192
        SCALE = HEAD_DIM ** (-0.5)
        B, NQ, _ = query.shape
        NKV = context.shape[1]
        q = query @ w_q
        kv = context @ w_kv
        k, v = jnp.split(kv, 2, axis=-1)
        q = q.reshape(B, NQ, NUM_HEADS, HEAD_DIM).transpose(0, 2, 1, 3)
        k = k.reshape(B, NKV, NUM_HEADS, HEAD_DIM).transpose(0, 2, 1, 3)
        v = v.reshape(B, NKV, NUM_HEADS, HEAD_DIM).transpose(0, 2, 1, 3)
        scores = jnp.einsum('bhqd,bhkd->bhqk', q, k) * SCALE
        attn = jax.nn.softmax(scores, axis=-1)
        out = jnp.einsum('bhqk,bhkd->bhqd', attn, v)
        out = out.transpose(0, 2, 1, 3).reshape(B, NQ, INNER)
        return out @ w_out + b_out

    def _L1_ffn_ref(x, W_in, b_in, W_out, b_out):
        import jax, jax.numpy as jnp
        import numpy as np

        def _ste(w, w_q):
            return w + jax.lax.stop_gradient(w_q - w)

        def quantize_w8_per(w, axis):
            amax = jnp.clip(jnp.max(jnp.abs(w), axis=axis, keepdims=True), 1e-08, None)
            scale = 127.0 / amax
            w_q = jnp.clip(jnp.round(w * scale), -128.0, 127.0) / scale
            return _ste(w, w_q)

        def quantize_a16(x):
            amax = jnp.clip(jnp.max(jnp.abs(x)), 1e-08, None)
            scale = 32767.0 / amax
            x_q = jnp.clip(jnp.round(x * scale), -32768.0, 32767.0) / scale
            return _ste(x, x_q)
        W_in_sim = quantize_w8_per(W_in, axis=0)
        W_out_sim = quantize_w8_per(W_out, axis=1)
        x_sim = quantize_a16(x)
        hidden = jax.nn.gelu(x_sim @ W_in_sim + b_in, approximate=False)
        hidden_sim = quantize_a16(hidden)
        out = hidden_sim @ W_out_sim + b_out
        return out
    x = x + jnp.tanh(g_xattn[0]) * _L0_xattn_ref(_layernorm(x, axis=-1), ctx_768, L0_xattn_Wq, L0_xattn_bq, L0_xattn_Wk, L0_xattn_bk, L0_xattn_Wv, L0_xattn_bv, L0_xattn_Wo, L0_xattn_bo)
    x = x + jnp.tanh(g_ffn[0]) * _L0_ffn_ref(_layernorm(x, axis=-1), L0_ffn_Wg, L0_ffn_W1, L0_ffn_b1, L0_ffn_W2, L0_ffn_b2)
    x = x + jnp.tanh(g_xattn[1]) * _L1_xattn_ref(_layernorm(x, axis=-1), ctx_768, L1_xattn_w_q, L1_xattn_w_kv, L1_xattn_w_out, L1_xattn_b_out)
    x = x + jnp.tanh(g_ffn[1]) * _L1_ffn_ref(_layernorm(x, axis=-1), L1_ffn_W_in, L1_ffn_b_in, L1_ffn_W_out, L1_ffn_b_out)
    return x

_drawn_inputs = setup_inputs


def setup_inputs(seed=0):
    import zlib

    import numpy as np

    out = dict(_drawn_inputs(seed))
    spreads = {'g_ffn': (-1.0, 0.2),
     'L0_xattn_bq': (0.0, 0.1),
     'L0_xattn_bk': (0.0, 0.8),
     'L0_xattn_bv': (0.0, 0.1),
     'L0_xattn_bo': (0.0, 0.1),
     'L0_ffn_b1': (0.0, 0.1),
     'L0_ffn_b2': (0.0, 0.1),
     'L1_ffn_b_in': (0.0, 0.1),
     'L1_ffn_b_out': (0.0, 0.1)}
    factors = {'L1_xattn_b_out': 7.419}
    for name, (base, spread) in spreads.items():
        noise = np.random.default_rng([zlib.crc32(name.encode()), seed]).standard_normal(out[name].shape)
        drawn = base * np.exp(spread * noise) if base else spread * noise
        out[name] = jnp.asarray(drawn.astype(out[name].dtype))
    for name, factor in factors.items():
        out[name] = (out[name] * factor).astype(out[name].dtype)
    return out
```

```python
from contextlib import ExitStack

import concourse.bass as bass
from concourse import mybir

F32 = mybir.dt.float32
BF16 = mybir.dt.bfloat16
I32 = mybir.dt.int32
U32 = mybir.dt.uint32
ALU = mybir.AluOpType
ACT = mybir.ActivationFunctionType
AX = mybir.AxisListType.X
RMAX = bass.bass_isa.ReduceOp.max

P = 128
B, N, D = 4, 1024, 256
KEYS, DC = 77, 192
TILES = B * N // P
TPB = N // P
KD = D // P
HEADS = 16
ROWS = HEADS * KEYS
RCH = -(-ROWS // P)
CTX_K = [(0, P), (P, DC - P)]
REPS = 3
HPB = 6
SB = [(j * HPB, min(HEADS, (j + 1) * HPB)) for j in range(-(-HEADS // HPB))]
E, F, TOPK = 8, 1024, 2
FCH = F // P
SLOT_T = 256
SUB = SLOT_T // P
NST = (B * N * TOPK + E * (SLOT_T - 1)) // SLOT_T
NSUB = NST * SUB
EPS = 1e-5
CLAMP = 10000.0
MAGIC = 1.5 * 2.0 ** 23


def wait(eng, sem, value):
    if isinstance(value, int) and value <= 0:
        return
    eng.wait_ge(sem, value)


def counted(eng, value):
    return value if isinstance(value, int) else eng.snap(eng.to_reg(value))


class Mem:

    def __init__(self, nc, ctx, sems, tag):
        self.nc, self.ctx, self.sems, self.tag = nc, ctx, sems, tag

    def sb(self, name, shape, dt=F32):
        return self.ctx.enter_context(self.nc.sbuf_tensor(f"{self.tag}_{name}", shape, dt))

    def ps(self, name, shape, dt=F32):
        return self.ctx.enter_context(self.nc.psum_tensor(f"{self.tag}_{name}", shape, dt))

    def sem(self, name):
        self.sems.append(self.nc.alloc_semaphore(name=f"{self.tag}_{name}"))
        return self.sems[-1]


def clear_semaphores(nc, C):
    nc.clear_and_free_semaphores(C.sems)
    nc.all_engine_barrier()
    C.sems.clear()


def blocks_of(hpg):
    out = []
    for g in range(HEADS // hpg):
        lo, hi = g * hpg * KEYS, (g + 1) * hpg * KEYS
        out += [(c, g) for c in range(RCH) if c * P < hi and (c + 1) * P > lo]
    return out


def pieces_of(hpg):
    out = []
    for j, (a, z) in enumerate(SB):
        for g in range(HEADS // hpg):
            lo, hi = max(a, g * hpg), min(z, (g + 1) * hpg)
            if lo < hi:
                out.append((j, g, lo, hi))
    return out


def prologue(nc, io, C):
    with ExitStack() as ctx:
        m = Mem(nc, ctx, C.sems, "pro")
        ctx_rows = m.sb("ctx_rows", [KEYS, B, DC])
        g_row = m.sb("g_row", [P, 4])
        ps = m.ps("ps", [P, 2, 512])
        loaded, ones_set, ident_set, turned, copied = (m.sem(x) for x in ("loaded", "ones", "ident", "turned", "copied"))
        tanh_done = m.sem("tanh_done")
        block = ctx.enter_context(nc.Block())

        @block.sync
        def _(sp):
            sp.dma_start(ctx_rows[:, :, :], io["ctx_768"].rearrange("b k d -> k b d")).then_inc(loaded, 16)
            sp.dma_start(g_row[:, 0:2], io["g_xattn"].partition_broadcast(P)).then_inc(loaded, 16)
            sp.dma_start(g_row[:, 2:4], io["g_ffn"].partition_broadcast(P)).then_inc(loaded, 16)

        @block.gpsimd
        def _(pool):
            pool.memset(C.ident[:, :], 0.0).then_inc(ones_set, 1)
            pool.memset(C.ones[:, :], 1.0).then_inc(ones_set, 1)
            pool.memset(C.half[:, :], -0.5).then_inc(ones_set, 1)
            pool.wait_ge(ones_set, 1)
            pool.affine_select(out=C.ident[:, :], in_=C.ident[:, :], compare_op=ALU.not_equal, fill=1.0, base=0,
                               pattern=[[-1, P]], channel_multiplier=1).then_inc(ident_set, 1)
            pool.wait_ge(ones_set, 3)

        @block.tensor
        def _(pe):
            pe.wait_ge(loaded, 48)
            pe.wait_ge(ident_set, 1)
            for b in range(B):
                if b >= 2:
                    pe.wait_ge(copied, 2 * (b - 1))
                for k, (at, n) in enumerate(CTX_K):
                    pe.transpose(ps[0:n, b % 2, k * KEYS:(k + 1) * KEYS], ctx_rows[:, b, at:at + n],
                                 C.ident[0:KEYS, 0:KEYS]).then_inc(turned, 1)

        @block.vector
        def _(dve):
            for b in range(B):
                dve.wait_ge(turned, 2 * (b + 1))
                for k, (at, n) in enumerate(CTX_K):
                    src = ps[0:n, b % 2, k * KEYS:(k + 1) * KEYS].unsqueeze(1).broadcast_to((n, REPS, KEYS))
                    dve.tensor_copy(C.ctxT[0:n, k, b, :].rearrange("p (r k) -> p r k", r=REPS), src).then_inc(copied, 1)
            dve.wait_ge(copied, 2 * B)

        @block.scalar
        def _(act):
            act.wait_ge(loaded, 48)
            act.activation(C.gate[:, :], g_row[:, :], ACT.Tanh).then_inc(tanh_done, 1)
            act.wait_ge(tanh_done, 1)


def attention(nc, tag, C, x_in, x_out, w, hpg, gate_col, clamp, split=None):
    dh = P // hpg
    ng = HEADS // hpg
    blocks, pieces = blocks_of(hpg), pieces_of(hpg)
    scale = float(dh) ** -0.5
    vgroups = [blocks[i:i + 4] for i in range(0, len(blocks), 4)]
    kgroups = [(g, min(ng, g + 4)) for g in range(0, ng, 4)]
    qgroups = kgroups
    RING = 8
    with ExitStack() as ctx:
        m = Mem(nc, ctx, C.sems, tag)
        wq = m.sb("wq", [P, KD, ng * P])
        wk = m.sb("wk", [P, 2, ng * P])
        wv = m.sb("wv", [P, 2, ng * P])
        wo = m.sb("wo", [P, ng, D])
        bq = m.sb("bq", [P, ng])
        bk = m.sb("bk", [1, ng * P])
        bv = m.sb("bv", [1, ng * P])
        gbo = m.sb("gbo", [P, D])
        kmask = m.sb("kmask", [P, hpg])
        vmask = m.sb("vmask", [P, len(blocks), hpg])
        kblk = m.sb("kblk", [P, ng, hpg * KEYS])
        vblk = m.sb("vblk", [P, len(blocks), P])
        x = m.sb("x", [P, RING, D])
        stats = m.sb("stats", [P, 2, 6])
        mv = m.sb("mv", [P, 2, 2])
        veps = m.sb("veps", [P, 2])
        rstd = m.sb("rstd", [P, 2])
        xn = m.sb("xn", [P, D])
        xnT = m.sb("xnT", [P, KD, P])
        qT = m.sb("qT", [P, ng, P])
        mx = m.sb("mx", [P, HEADS])
        z = m.sb("z", [P, 2, ROWS])
        ssum = m.sb("ssum", [P, HEADS])
        rsum = m.sb("rsum", [P, 2, HEADS])
        pT = m.sb("pT", [P, RCH, P])
        attnT = m.sb("attnT", [P, ng, P])
        x1 = m.sb("x1", [P, 2, D])
        ps_sc = m.ps("ps_sc", [P, len(SB), 512])
        ps_xo = m.ps("ps_xo", [P, 512])
        ps_q = m.ps("ps_q", [P, 2, 512])
        ps_pv = m.ps("ps_pv", [P, 2, 512])
        ps_x, ps_o = ps_xo[:, 0:D], ps_q[:, 1, 0:D]
        if split:
            stage = m.sb("stage", [P, 2, 2, 512])
            piece_in = [m.sem(f"piece_in{i}") for i in range(2)]
            hi_done, lo_done = m.sem("hi_done"), m.sem("lo_done")

        weights_in, masks_done, gbo_done = m.sem("weights_in"), m.sem("masks_done"), m.sem("gbo_done")
        x_loaded = [m.sem(f"x_loaded{i}") for i in range(RING)]
        x_stored = [m.sem(f"x_stored{i}") for i in range(2)]
        names = ("stats_done", "mean_done", "veps_done", "rstd_done", "xn_done", "turned_x", "xnT_done", "q_done",
                 "qT_done", "k_proj", "k_done", "v_proj", "v_done", "scores_done", "max_done", "z_done", "zc_done",
                 "exp_done", "sum_done", "rsum_done", "norm_done", "turned_p", "pT_act", "pT_dve", "pv_done",
                 "attn_act", "attn_dve", "o_done", "x1_done", "xb_done", "mask_step", "ctx_done")
        s = {n: m.sem(n) for n in names}
        n_weights = 7 + (3 if w.get("bq") is not None else 0)
        block = ctx.enter_context(nc.Block())

        def run(eng, slot):
            for t in range(TPB + 2):
                slot(t, t % TPB, t // TPB)
            with eng.Fori(1, B - 1) as b:
                for t in range(2, TPB + 2):
                    slot(b * TPB + t, t % TPB, b + t // TPB)
            for t in range(2, TPB + 2):
                slot((B - 1) * TPB + t, t % TPB, B - 1 + t // TPB)

        def front(t_slot):
            return not isinstance(t_slot, int) or t_slot < TILES

        def back(t_slot):
            return not isinstance(t_slot, int) or t_slot >= 2

        @block.sync
        def _(sp):
            sp.dma_start(wq[:, :, :], w["wq"].rearrange("(k p) n -> p k n", p=P)).then_inc(weights_in, 16)
            for dst, name in ((wk, "wk"), (wv, "wv")):
                for k, (at, n) in enumerate(CTX_K):
                    sp.dma_start(dst[0:n, k, :], w[name][at:at + n, :]).then_inc(weights_in, 16)
            sp.dma_start(wo[:, :, :], w["wo"].rearrange("(g p) n -> p g n", p=P)).then_inc(weights_in, 16)
            sp.dma_start(gbo[:, :], w["bo"].partition_broadcast(P)).then_inc(weights_in, 16)
            if w.get("bq") is not None:
                with nc.allow_non_contiguous_dma(reason="a short bias, one element to a partition"):
                    sp.dma_start(bq[:, :], w["bq"].rearrange("(g p) -> p g", p=P)).then_inc(weights_in, 16)
                sp.dma_start(bk[:, :], w["bk"].unsqueeze(0)).then_inc(weights_in, 16)
                sp.dma_start(bv[:, :], w["bv"].unsqueeze(0)).then_inc(weights_in, 16)

            def load_x(tile, at):
                sp.dma_start(x[:, at, :], x_in[bass.ds(tile * P, P), :]).then_inc(x_loaded[at], 16)

            for t in range(RING - 2):
                load_x(t, t)

            def slot(T, t, b):
                if split and front(T):
                    wait(sp, hi_done, 2 * (T - 1))
                    wait(sp, lo_done, 2 * (T - 1))
                    sp.dma_start(stage[:, t % 2, 0, :],
                                 split["w1"].rearrange("e (c p) f -> (e c) p f", p=P)
                                 [bass.ds(b * (TPB // 2) + t // 2, 1), :, t % 2 * 512:(t % 2 + 1) * 512]
                                 .rearrange("o p f -> p (o f)")).then_inc(piece_in[t % 2], 16)
                    sp.dma_start(stage[:, t % 2, 1, :].rearrange("p (g d) -> p g d", d=D),
                                 split["w2"].rearrange("e (g p) d -> p (e g) d", p=P)
                                 [:, bass.ds(T * 2, 2), :]).then_inc(piece_in[t % 2], 16)
                if back(T):
                    sp.wait_ge(s["x1_done"], T - 1)
                    sp.dma_start(x_out[bass.ds((T - 2) * P, P), :], x1[:, t % 2, :]).then_inc(x_stored[t % 2], 16)
                    if not isinstance(T, int) or T + RING - 2 - 2 < TILES:
                        load_x(T + RING - 4, (t + RING - 4) % RING)

            run(sp, slot)
            for i in range(2):
                sp.wait_ge(x_stored[i], 16 * TILES // 2)

        @block.gpsimd
        def _(pool):
            pool.memset(kmask[:, :], 1.0).then_inc(s["mask_step"], 1)
            pool.memset(vmask[:, :, :], 1.0).then_inc(s["mask_step"], 1)
            pool.wait_ge(s["mask_step"], 2)
            pool.affine_select(out=kmask[:, :], in_=kmask[:, :], compare_op=ALU.is_ge, fill=0.0, base=0,
                               pattern=[[-dh, hpg]], channel_multiplier=1).then_inc(s["mask_step"], 1)
            pool.wait_ge(s["mask_step"], 3)
            pool.affine_select(out=kmask[:, :], in_=kmask[:, :], compare_op=ALU.is_ge, fill=0.0, base=dh - 1,
                               pattern=[[dh, hpg]], channel_multiplier=-1).then_inc(s["mask_step"], 1)
            for i, (c, g) in enumerate(blocks):
                at = c * P - g * hpg * KEYS
                pool.affine_select(out=vmask[:, i, :], in_=vmask[:, i, :], compare_op=ALU.is_ge, fill=0.0, base=at,
                                   pattern=[[-KEYS, hpg]], channel_multiplier=1).then_inc(s["mask_step"], 1)
            pool.wait_ge(s["mask_step"], 4 + len(blocks))
            for i, (c, g) in enumerate(blocks):
                at = c * P - g * hpg * KEYS
                pool.affine_select(out=vmask[:, i, :], in_=vmask[:, i, :], compare_op=ALU.is_ge, fill=0.0,
                                   base=KEYS - 1 - at, pattern=[[KEYS, hpg]],
                                   channel_multiplier=-1).then_inc(s["mask_step"], 1)
            pool.wait_ge(weights_in, 16 * n_weights)
            pool.tensor_scalar(gbo[:, :], gbo[:, :], C.gate[:, gate_col:gate_col + 1], None,
                               ALU.mult).then_inc(gbo_done, 1)
            pool.wait_ge(gbo_done, 1)

            def power(tile, at):
                pool.wait_ge(s["veps_done"], tile + 1)
                pool.tensor_tensor(rstd[:, at:at + 1], veps[:, at:at + 1], C.half[:, 0:1],
                                   ALU.pow).then_inc(s["rstd_done"], 1)

            power(0, 0)
            power(1, 1)

            def slot(T, t, b):
                if not front(T):
                    return
                if not isinstance(T, int) or T + 2 < TILES:
                    power(T + 2, t % 2)
                if split:
                    pool.wait_ge(hi_done, 2 * T + 2)
                    w1h, w1l, w2 = split["w1h"], split["w1l"], split["w2s"]
                    at = bass.ds(b * (TPB // 2) + t // 2, 1)
                    cols = slice(t % 2 * 512, (t % 2 + 1) * 512)
                    pool.tensor_tensor(w1l[:, at, cols].rearrange("p o f -> p (o f)"), stage[:, t % 2, 0, :],
                                       w1h[:, at, cols].rearrange("p o f -> p (o f)"),
                                       ALU.subtract).then_inc(lo_done, 1)
                    pool.tensor_tensor(w2[:, bass.ds(T * 2, 2), D:2 * D],
                                       stage[:, t % 2, 1, :].rearrange("p (g d) -> p g d", d=D),
                                       w2[:, bass.ds(T * 2, 2), 0:D], ALU.subtract).then_inc(lo_done, 1)
                pool.wait_ge(s["xn_done"], T + 1)
                pool.tensor_tensor(x[:, t, :], x[:, t, :], gbo[:, :], ALU.add).then_inc(s["xb_done"], 1)
                pool.wait_ge(s["rsum_done"], T + 1)
                zt = z[:, t % 2, :].rearrange("p (h k) -> p h k", k=KEYS)
                pool.tensor_tensor(zt, zt, rsum[:, t % 2, :].unsqueeze(2).broadcast_to((P, HEADS, KEYS)),
                                   ALU.mult).then_inc(s["norm_done"], 1)

            run(pool, slot)

        @block.tensor
        def _(pe):
            pe.wait_ge(weights_in, 16 * n_weights)

            def keys(T, b):
                wait(pe, s["qT_done"], T * len(qgroups))
                for j, (g0, g1) in enumerate(kgroups):
                    if j == 1:
                        wait(pe, s["x1_done"], T - 2)
                    for g in range(g0, g1):
                        out = ps_q[:, j, (g - g0) * KEYS:(g - g0 + 1) * KEYS]
                        if w.get("bk") is not None:
                            pe.matmul(out, bk[:, g * P:(g + 1) * P], C.ones[0:1, 0:KEYS], start=True, stop=False)
                        for k, (at, n) in enumerate(CTX_K):
                            mm = pe.matmul(out, wk[0:n, k, g * P:(g + 1) * P], C.ctxT_now[0:n, k, 0:KEYS],
                                           start=(k == 0 and w.get("bk") is None), stop=(k == 1))
                    mm.then_inc(s["k_proj"], 1)

            def values(T, b):
                wait(pe, s["attn_act"], T - 2)
                wait(pe, s["attn_dve"], T - 2)
                for j, group in enumerate(vgroups):
                    if j >= 2:
                        pe.wait_ge(s["v_done"], b * len(vgroups) + j - 1)
                    for i, (c, g) in enumerate(group):
                        out = ps_pv[:, j % 2, i * P:(i + 1) * P]
                        at0 = c * P % KEYS
                        if w.get("bv") is not None:
                            pe.matmul(out, C.ones[0:1, :], bv[:, g * P:(g + 1) * P], start=True, stop=False)
                        for k, (at, n) in enumerate(CTX_K):
                            mm = pe.matmul(out, C.ctxT_now[0:n, k, at0:at0 + P], wv[0:n, k, g * P:(g + 1) * P],
                                           start=(k == 0 and w.get("bv") is None), stop=(k == 1))
                    mm.then_inc(s["v_proj"], 1)

            def turn_p(T, t, parts):
                for j in parts:
                    c0, c1 = 4 * j, min(RCH, 4 * j + 4)
                    if j == 0:
                        pe.wait_ge(s["norm_done"], T - 1)
                        if not isinstance(T, int) or T > 2:
                            pe.wait_ge(s["attn_act"], T - 2)
                            pe.wait_ge(s["attn_dve"], T - 2)
                        if t == 2:
                            pe.wait_ge(s["v_done"], (T - 2) // TPB * len(vgroups) + len(vgroups)
                                       if isinstance(T, int) else v_all(T))
                    if j == 2:
                        pe.wait_ge(s["pT_act"], 2 * (T - 2) + 1)
                    for c in range(c0, c1):
                        n = min(P, ROWS - c * P)
                        mm = pe.transpose(ps_pv[0:n, j % 2, (c - c0) * P:(c - c0 + 1) * P],
                                          z[:, t % 2, c * P:c * P + n], C.ident[:, :])
                    mm.then_inc(s["turned_p"], 1)

            state = {}

            def v_all(T):
                return state["b"] * len(vgroups) + len(vgroups)

            def slot(T, t, b):
                state["b"] = b
                if front(T):
                    if t == 0:
                        pe.wait_ge(s["ctx_done"], b + 1)
                        keys(T, b)
                    pe.wait_ge(s["xn_done"], T + 1)
                    wait(pe, s["xnT_done"], T)
                    for k in range(KD):
                        mm = pe.transpose(ps_x[:, k * P:(k + 1) * P], xn[:, k * P:(k + 1) * P], C.ident[:, :])
                    mm.then_inc(s["turned_x"], 1)
                if t == 2 and back(T):
                    values(T, b)
                if back(T):
                    turn_p(T, t, (0, 1))
                if front(T):
                    pe.wait_ge(s["xnT_done"], T + 1)
                    if t == 0:
                        pe.wait_ge(s["k_done"], (b + 1) * len(kgroups))
                    wait(pe, s["qT_done"], T * len(qgroups))
                    for j, (g0, g1) in enumerate(qgroups):
                        if j == 1:
                            wait(pe, s["x1_done"], T - 2)
                        for g in range(g0, g1):
                            for k in range(KD):
                                mm = pe.matmul(ps_q[:, j, (g - g0) * P:(g - g0 + 1) * P], wq[:, k, g * P:(g + 1) * P],
                                               xnT[:, k, :], start=(k == 0), stop=(k == KD - 1))
                        mm.then_inc(s["q_done"], 1)
                if back(T):
                    turn_p(T, t, (2,))
                    pe.wait_ge(s["pT_act"], 2 * (T - 2) + 2)
                    pe.wait_ge(s["pT_dve"], T - 1)
                    half = -(-ng // 2)
                    for j in range(2):
                        for g in range(j * half, min(ng, (j + 1) * half)):
                            mine = [i for i, (c, gg) in enumerate(blocks) if gg == g]
                            for i in mine:
                                c = blocks[i][0]
                                n = min(P, ROWS - c * P)
                                mm = pe.matmul(ps_pv[:, j, (g - j * half) * P:(g - j * half + 1) * P],
                                               vblk[0:n, i, :], pT[0:n, c, :],
                                               start=(i == mine[0]), stop=(i == mine[-1]))
                        mm.then_inc(s["pv_done"], 1)
                if front(T):
                    pe.wait_ge(s["qT_done"], (T + 1) * len(qgroups))
                    for j in range(len(SB)):
                        if not isinstance(T, int) or T > 0:
                            pe.wait_ge(s["z_done"], (T - 1) * len(SB) + j + 1)
                        for jj, g, h0, h1 in pieces:
                            if jj == j:
                                a = SB[j][0]
                                mm = pe.matmul(ps_sc[:, j, (h0 - a) * KEYS:(h1 - a) * KEYS], qT[:, g, :],
                                               kblk[:, g, (h0 - g * hpg) * KEYS:(h1 - g * hpg) * KEYS],
                                               start=True, stop=True)
                        mm.then_inc(s["scores_done"], 1)
                if back(T):
                    pe.wait_ge(s["attn_act"], T - 1)
                    pe.wait_ge(s["attn_dve"], T - 1)
                    wait(pe, s["x1_done"], T - 2)
                    for g in range(ng):
                        mm = pe.matmul(ps_o, attnT[:, g, :], wo[:, g, :], start=(g == 0), stop=(g == ng - 1))
                    mm.then_inc(s["o_done"], 1)

            run(pe, slot)

        @block.scalar
        def _(act):
            act.wait_ge(weights_in, 16 * n_weights)

            def slot(T, t, b):
                if front(T):
                    if t == 0:
                        if not isinstance(T, int) or T > 0:
                            act.wait_ge(s["v_proj"], b * len(vgroups))
                            act.wait_ge(s["k_proj"], b * len(kgroups))
                        act.activation(C.ctxT_now[:, 0, :], C.ctxT[:, 0, bass.ds(b, 1), :].rearrange("p o k -> p (o k)"), ACT.Copy)
                        act.activation(C.ctxT_now[0:DC - P, 1, :],
                                       C.ctxT[0:DC - P, 1, bass.ds(b, 1), :].rearrange("p o k -> p (o k)"),
                                       ACT.Copy).then_inc(s["ctx_done"], 1)
                    act.wait_ge(s["turned_x"], T + 1)
                    wait(act, s["q_done"], T * len(qgroups))
                    act.activation(xnT[:, :, :].rearrange("p k t -> p (k t)"), ps_x, ACT.Copy).then_inc(s["xnT_done"], 1)
                    if split:
                        act.wait_ge(piece_in[t % 2], 32 * (b * (TPB // 2) + t // 2 + 1))
                        act.activation(split["w1h"][:, bass.ds(b * (TPB // 2) + t // 2, 1),
                                                    t % 2 * 512:(t % 2 + 1) * 512].rearrange("p o f -> p (o f)"),
                                       stage[:, t % 2, 0, :], ACT.Copy).then_inc(hi_done, 1)
                        act.activation(split["w2s"][:, bass.ds(T * 2, 2), 0:D],
                                       stage[:, t % 2, 1, :].rearrange("p (g d) -> p g d", d=D),
                                       ACT.Copy).then_inc(hi_done, 1)
                if back(T):
                    wait(act, s["pv_done"], 2 * (T - 2))
                    act.wait_ge(s["turned_p"], 3 * (T - 2) + 1)
                    act.activation(pT[:, 0:4, :].rearrange("p c t -> p (c t)"), ps_pv[:, 0, :],
                                   ACT.Copy).then_inc(s["pT_act"], 1)
                if front(T):
                    for j, (g0, g1) in enumerate(qgroups):
                        act.wait_ge(s["q_done"], T * len(qgroups) + j + 1)
                        if j == 0:
                            wait(act, s["scores_done"], T * len(SB))
                        if w.get("bq") is None:
                            act.activation(qT[:, g0:g1, :].rearrange("p g t -> p (g t)"), ps_q[:, j, 0:(g1 - g0) * P],
                                           ACT.Copy).then_inc(s["qT_done"], 1)
                        else:
                            for g in range(g0, g1):
                                ins = act.activation(qT[:, g, :], ps_q[:, j, (g - g0) * P:(g - g0 + 1) * P],
                                                     ACT.Identity, bias=bq[:, g:g + 1])
                            ins.then_inc(s["qT_done"], 1)
                if back(T):
                    act.wait_ge(s["turned_p"], 3 * (T - 2) + 3)
                    last = ROWS - 9 * P
                    act.activation(pT[:, 8, :], ps_pv[:, 0, 0:P], ACT.Copy)
                    act.activation(pT[0:last, 9, :], ps_pv[0:last, 0, P:2 * P], ACT.Copy).then_inc(s["pT_act"], 1)
                    act.wait_ge(s["pv_done"], 2 * (T - 2) + 1)
                    wait(act, s["o_done"], T - 2)
                    half = -(-ng // 2)
                    act.activation(attnT[:, 0:half, :].rearrange("p g t -> p (g t)"), ps_pv[:, 0, 0:half * P],
                                   ACT.Copy).then_inc(s["attn_act"], 1)
                if front(T):
                    if clamp:
                        act.wait_ge(s["zc_done"], T + 1)
                    else:
                        act.wait_ge(s["z_done"], (T + 1) * len(SB))
                    act.activation(z[:, t % 2, :], z[:, t % 2, :], ACT.Exp, scale=scale).then_inc(s["exp_done"], 1)

            run(act, slot)

        @block.vector
        def _(dve):
            def ln_stats(tile, at, r, turn):
                dve.wait_ge(x_loaded[r], 16 * (turn + 1))
                dve.bn_stats(stats[:, at, :], x[:, r, :]).then_inc(s["stats_done"], 1)
                dve.wait_ge(s["stats_done"], tile + 1)

            def ln_mean(tile, at):
                dve.bn_aggr(mv[:, at, :], stats[:, at, :]).then_inc(s["mean_done"], 1)
                dve.wait_ge(s["mean_done"], tile + 1)
                dve.tensor_scalar(veps[:, at:at + 1], mv[:, at, 1:2], EPS, None, ALU.add).then_inc(s["veps_done"], 1)

            def ln(tile, at, r):
                dve.wait_ge(s["rstd_done"], tile + 1)
                wait(dve, s["turned_x"], tile)
                dve.tensor_scalar(xn[:, :], x[:, r, :], mv[:, at, 0:1], rstd[:, at:at + 1], ALU.subtract,
                                  ALU.mult).then_inc(s["xn_done"], 1)

            ln_stats(0, 0, 0, 0)
            ln_mean(0, 0)
            ln_stats(1, 1, 1, 0)
            ln_mean(1, 1)
            ln(0, 0, 0)

            def slot(T, t, b):
                if front(T):
                    if t == 0:
                        for j, (g0, g1) in enumerate(kgroups):
                            dve.wait_ge(s["k_proj"], b * len(kgroups) + j + 1)
                            if j == 0:
                                dve.wait_ge(s["mask_step"], 4 + 2 * len(blocks))
                                wait(dve, s["scores_done"], T * len(SB))
                            n = g1 - g0
                            for h in range(hpg):
                                ins = dve.tensor_scalar(
                                    kblk[:, g0:g1, h * KEYS:(h + 1) * KEYS],
                                    ps_q[:, j, 0:n * KEYS].rearrange("p (g k) -> p g k", k=KEYS),
                                    kmask[:, h:h + 1], None, ALU.mult)
                            ins.then_inc(s["k_done"], 1)
                if t == 2 and back(T):
                    for j, group in enumerate(vgroups):
                        dve.wait_ge(s["v_proj"], b * len(vgroups) + j + 1)
                        if j == 0:
                            wait(dve, s["pv_done"], 2 * (T - 2))
                        n = len(group)
                        dve.tensor_tensor(
                            vblk[:, 4 * j:4 * j + n, :].rearrange("p i (h d) -> p (i h) d", d=dh),
                            ps_pv[:, j % 2, 0:n * P].rearrange("p (i d) -> p i d", d=dh),
                            vmask[:, 4 * j:4 * j + n, :].rearrange("p i h -> p (i h)").unsqueeze(2)
                            .broadcast_to((P, n * hpg, dh)), ALU.mult).then_inc(s["v_done"], 1)
                if back(T):
                    wait(dve, s["pv_done"], 2 * (T - 2))
                    dve.wait_ge(s["turned_p"], 3 * (T - 2) + 2)
                    dve.tensor_copy(pT[:, 4:8, :].rearrange("p c t -> p (c t)"), ps_pv[:, 1, :]).then_inc(s["pT_dve"], 1)
                more = not isinstance(T, int) or T + 2 < TILES
                if more:
                    ln_stats(T + 2, t % 2, (t + 2) % RING, b + (t + 2) // RING)
                if not isinstance(T, int) or T + 1 < TILES:
                    ln(T + 1, (t + 1) % 2, (t + 1) % RING)
                if more:
                    ln_mean(T + 2, t % 2)
                if back(T):
                    half = -(-ng // 2)
                    dve.wait_ge(s["pv_done"], 2 * (T - 2) + 2)
                    wait(dve, s["o_done"], T - 2)
                    dve.tensor_copy(attnT[:, half:ng, :].rearrange("p g t -> p (g t)"),
                                    ps_pv[:, 1, 0:(ng - half) * P]).then_inc(s["attn_dve"], 1)
                if front(T):
                    for j, (h0, h1) in enumerate(SB):
                        n = h1 - h0
                        sc = ps_sc[:, j, 0:n * KEYS].rearrange("p (h k) -> p h k", k=KEYS)
                        dve.wait_ge(s["scores_done"], T * len(SB) + j + 1)
                        dve.tensor_reduce(mx[:, h0:h1], sc, AX, ALU.max).then_inc(s["max_done"], 1)
                        if clamp:
                            dve.wait_ge(s["max_done"], 2 * len(SB) * T + 2 * j + 1)
                            dve.tensor_scalar(mx[:, h0:h1], mx[:, h0:h1], -clamp / scale, clamp / scale, ALU.max,
                                              ALU.min).then_inc(s["max_done"], 1)
                if back(T):
                    dve.wait_ge(s["o_done"], T - 1)
                    dve.wait_ge(s["xb_done"], T - 1)
                    if not isinstance(T, int) or T >= 4:
                        dve.wait_ge(x_stored[t % 2], 16 * (b * (TPB // 2) + t // 2 - 1))
                    dve.scalar_tensor_tensor(out=x1[:, t % 2, :], in0=ps_o, scalar=C.gate[:, gate_col:gate_col + 1],
                                             in1=x[:, (t - 2) % RING, :], op0=ALU.mult,
                                             op1=ALU.add).then_inc(s["x1_done"], 1)
                if front(T):
                    per = 2 if clamp else 1
                    dve.wait_ge(s["max_done"], per * len(SB) * (T + 1))
                    if back(T):
                        dve.wait_ge(s["turned_p"], 3 * (T - 2) + 3)
                    for j, (h0, h1) in enumerate(SB):
                        n = h1 - h0
                        sc = ps_sc[:, j, 0:n * KEYS].rearrange("p (h k) -> p h k", k=KEYS)
                        zj = z[:, t % 2, h0 * KEYS:h1 * KEYS].rearrange("p (h k) -> p h k", k=KEYS)
                        mb = mx[:, h0:h1].unsqueeze(2).broadcast_to((P, n, KEYS))
                        if clamp:
                            dve.scalar_tensor_tensor(out=zj, in0=sc, scalar=-clamp / scale, in1=mb, op0=ALU.max,
                                                     op1=ALU.subtract).then_inc(s["z_done"], 1)
                        else:
                            dve.tensor_tensor(zj, sc, mb, ALU.subtract).then_inc(s["z_done"], 1)
                    if clamp:
                        dve.wait_ge(s["z_done"], len(SB) * (T + 1))
                        dve.tensor_scalar(z[:, t % 2, :], z[:, t % 2, :], 0.0, None, ALU.min).then_inc(s["zc_done"], 1)
                if front(T):
                    dve.wait_ge(s["exp_done"], T + 1)
                    dve.tensor_reduce(ssum[:, :], z[:, t % 2, :].rearrange("p (h k) -> p h k", k=KEYS), AX,
                                      ALU.add).then_inc(s["sum_done"], 1)
                    dve.wait_ge(s["sum_done"], T + 1)
                    if back(T):
                        dve.wait_ge(s["norm_done"], T - 1)
                    dve.reciprocal(rsum[:, t % 2, :], ssum[:, :]).then_inc(s["rsum_done"], 1)

            run(dve, slot)


def routing(nc, C, x1_dram, xn_dram, wg):
    with ExitStack() as ctx:
        m = Mem(nc, ctx, C.sems, "route")
        x = m.sb("x", [P, TILES, D])
        wg_sb = m.sb("wg", [P, KD, E])
        stats = m.sb("stats", [P, TPB, 6])
        mv = m.sb("mv", [P, TILES, 2])
        veps = m.sb("veps", [P, TILES])
        rstd = m.sb("rstd", [P, TILES])
        xT = m.sb("xT", [P, 2, KD * P])
        lower = m.sb("lower", [P, P])
        iota_i = m.sb("iota_i", [P, P], I32)
        iota = m.sb("iota", [P, P])
        token_i = m.sb("token_i", [P, TILES], I32)
        token = m.sb("token", [P, TILES])
        rank_i = m.sb("rank_i", [P, E], I32)
        rank = m.sb("rank", [P, E])
        sig = m.sb("sig", [P, TILES, E])
        big = [m.sb(f"big{i}", [P, TILES, E]) for i in range(2)]
        hot = m.sb("hot", [P, TOPK, TILES, E])
        top = m.sb("top", [P, TOPK, TILES])
        first = m.sb("first", [P, TILES])
        both = m.sb("both", [P, TILES, E])
        run_n = [m.sb(f"run_n{i}", [P, E, TILES]) for i in range(2)]
        tiles_f = m.sb("tiles_f", [P, E])
        tiles_i = m.sb("tiles_i", [P, E], I32)
        ends = [m.sb(f"ends{i}", [P, E]) for i in range(2)]
        starts = m.sb("starts", [P, E])
        slot_f = m.sb("slot_f", [P, TOPK, TILES])
        part_i = m.sb("part_i", [P, 2, TOPK, TILES], I32)
        part = m.sb("part", [P, 2, TOPK, TILES])
        expert_f = m.sb("expert_f", [P, NST])
        past = m.sb("past", [P, NST, E])
        low_hot = m.sb("low_hot", [P, TOPK, P])
        high_tok = m.sb("high_tok", [P, TOPK, NSUB])
        ps_x = m.ps("ps_x", [P, 2, 512])
        ps_l = m.ps("ps_l", [P, 512])
        ps_n = m.ps("ps_n", [P, 2, TILES * E])
        ps_inv = m.ps("ps_inv", [P, 512])
        names = ("const_step", "wg_in", "stats_done", "mean_done", "veps_done", "rstd_done", "xn_done", "turned", "xT_done",
                 "logits_done", "exp_done", "step", "both_done", "counted", "low_done", "high_done", "inv_done", "xn_stored")
        s = {n: m.sem(n) for n in names}
        C.rows_stored = s["xn_stored"]
        x_in = [m.sem(f"x_in{b}") for b in range(B)]
        block = ctx.enter_context(nc.Block())
        x1_v = x1_dram.rearrange("(b t p) d -> b p t d", t=TPB, p=P)
        xn_v = xn_dram.rearrange("(b t p) d -> b p t d", t=TPB, p=P)

        @block.sync
        def _(sp):
            for b in range(B):
                sp.dma_start(x[:, b * TPB:(b + 1) * TPB, :], x1_v[b]).then_inc(x_in[b], 16)
            sp.dma_start(wg_sb[:, :, :], wg.rearrange("(k p) e -> p k e", p=P)).then_inc(s["wg_in"], 16)
            for b in range(B):
                sp.wait_ge(s["xn_done"], (b + 1) * TPB)
                sp.dma_start(xn_v[b], x[:, b * TPB:(b + 1) * TPB, :]).then_inc(s["xn_stored"], 16)
            sp.wait_ge(s["xn_stored"], 16 * B)

        @block.gpsimd
        def _(pool):
            pool.memset(lower[:, :], 1.0).then_inc(s["const_step"], 1)
            pool.iota(iota_i[:, :], pattern=[[1, P]], base=0, channel_multiplier=0).then_inc(s["const_step"], 1)
            pool.iota(token_i[:, :], pattern=[[P, TILES]], base=0, channel_multiplier=1).then_inc(s["const_step"], 1)
            pool.iota(rank_i[:, :], pattern=[[-1, E]], base=E, channel_multiplier=0).then_inc(s["const_step"], 1)
            pool.wait_ge(s["const_step"], 4)
            pool.affine_select(out=lower[:, :], in_=lower[:, :], compare_op=ALU.is_ge, fill=0.0, base=-1,
                               pattern=[[1, P]], channel_multiplier=-1).then_inc(s["const_step"], 1)
            pool.tensor_copy(iota[:, :], iota_i[:, :]).then_inc(s["const_step"], 1)
            pool.tensor_copy(token[:, :], token_i[:, :]).then_inc(s["const_step"], 1)
            pool.tensor_copy(rank[:, :], rank_i[:, :]).then_inc(s["const_step"], 1)
            for b in range(B):
                pool.wait_ge(s["veps_done"], b + 1)
                a = b * TPB
                pool.tensor_tensor(rstd[:, a:a + TPB], veps[:, a:a + TPB], C.half[:, 0:TPB],
                                   ALU.pow).then_inc(s["rstd_done"], 1)

        @block.tensor
        def _(pe):
            def turn(T, u):
                pe.wait_ge(s["xn_done"], T + 1)
                wait(pe, s["xT_done"], T - 1)
                for k in range(KD):
                    mm = pe.transpose(ps_x[:, u, k * P:(k + 1) * P], x[:, T, k * P:(k + 1) * P], C.ident[:, :])
                mm.then_inc(s["turned"], 1)

            def logits(T, u):
                pe.wait_ge(s["xT_done"], T + 1)
                for k in range(KD):
                    mm = pe.matmul(ps_l[:, T * E:(T + 1) * E], xT[:, u, k * P:(k + 1) * P], wg_sb[:, k, :],
                                   start=(k == 0), stop=(k == KD - 1))
                mm.then_inc(s["logits_done"], 1)

            pe.wait_ge(s["wg_in"], 16)
            for T in range(TILES):
                turn(T, T % 2)
                if T >= 1:
                    logits(T - 1, (T - 1) % 2)
            logits(TILES - 1, (TILES - 1) % 2)
            pe.wait_ge(s["both_done"], 1)
            pe.wait_ge(s["const_step"], 8)
            flat = both[:, :, :].rearrange("p t e -> p (t e)")
            pe.matmul(ps_n[:, 0, :], lower[:, :], flat, start=True, stop=True)
            pe.matmul(ps_n[:, 1, :], C.ones[:, :], flat, start=True, stop=True).then_inc(s["counted"], 1)

            def invert(T, c, start, stop):
                pe.wait_ge(s["low_done"], T * TOPK + c + 1)
                pe.wait_ge(s["high_done"], T * TOPK + c + 1)
                pe.matmul(ps_inv[:, 0:NSUB], low_hot[:, c, :], high_tok[:, c, :], start=start, stop=stop,
                          skip_group_check=True).then_inc(s["inv_done"], 1)

            invert(0, 0, True, False)
            invert(0, 1, False, False)
            with pe.Fori(1, TILES - 1) as T:
                for c in range(TOPK):
                    invert(T, c, False, False)
            invert(TILES - 1, 0, False, False)
            invert(TILES - 1, 1, False, True)

        @block.scalar
        def _(act):
            for T in range(TILES):
                act.wait_ge(s["turned"], T + 1)
                wait(act, s["logits_done"], T - 1)
                act.activation(xT[:, T % 2, :], ps_x[:, T % 2, 0:KD * P], ACT.Copy).then_inc(s["xT_done"], 1)
            act.wait_ge(s["logits_done"], TILES)
            act.activation(sig[:, :, :].rearrange("p t e -> p (t e)"), ps_l[:, 0:TILES * E], ACT.Exp,
                           scale=-1.0).then_inc(s["exp_done"], 1)

        @block.vector
        def _(dve):
            for b in range(B):
                dve.wait_ge(x_in[b], 16)
                if b:
                    dve.wait_ge(s["mean_done"], b * TPB)
                for t in range(TPB):
                    dve.bn_stats(stats[:, t, :], x[:, b * TPB + t, :]).then_inc(s["stats_done"], 1)
                for t in range(TPB):
                    dve.wait_ge(s["stats_done"], b * TPB + t + 1)
                    dve.bn_aggr(mv[:, b * TPB + t, :], stats[:, t, :]).then_inc(s["mean_done"], 1)
                dve.wait_ge(s["mean_done"], (b + 1) * TPB)
                dve.tensor_scalar(veps[:, b * TPB:(b + 1) * TPB], mv[:, b * TPB:(b + 1) * TPB, 1], EPS, None,
                                  ALU.add).then_inc(s["veps_done"], 1)
                dve.wait_ge(s["rstd_done"], b + 1)
                for t in range(TPB):
                    T = b * TPB + t
                    dve.tensor_scalar(x[:, T, :], x[:, T, :], mv[:, T, 0:1], rstd[:, T:T + 1], ALU.subtract,
                                      ALU.mult).then_inc(s["xn_done"], 1)

            steps = [0]

            def link(ins):
                steps[0] += 1
                ins.then_inc(s["step"], 1)
                dve.wait_ge(s["step"], steps[0])

            def over(ap, n):
                return ap.unsqueeze(2).broadcast_to((P, ap.shape[1], n))

            rank_b = rank[:, :].unsqueeze(1).broadcast_to((P, TILES, E))
            dve.wait_ge(s["exp_done"], 1)
            dve.wait_ge(s["const_step"], 8)
            link(dve.tensor_scalar(big[0][:, :, :], sig[:, :, :], 1.0, None, ALU.add))
            link(dve.reciprocal(sig[:, :, :], big[0][:, :, :]))
            for c in range(TOPK):
                link(dve.tensor_reduce(top[:, c, :], sig[:, :, :], AX, ALU.max))
                link(dve.tensor_tensor(big[0][:, :, :], sig[:, :, :], over(top[:, c, :], E), ALU.is_equal))
                link(dve.tensor_tensor(big[1][:, :, :], big[0][:, :, :], rank_b, ALU.mult))
                link(dve.tensor_reduce(first[:, :], big[1][:, :, :], AX, ALU.max))
                link(dve.tensor_tensor(hot[:, c, :, :], rank_b, over(first[:, :], E), ALU.is_equal))
                if c == 0:
                    link(dve.scalar_tensor_tensor(out=sig[:, :, :], in0=hot[:, c, :, :], scalar=-4.0, in1=sig[:, :, :],
                                                  op0=ALU.mult, op1=ALU.add))
            link(dve.tensor_tensor(both[:, :, :], hot[:, 0, :, :], hot[:, 1, :, :], ALU.add))
            dve.wait_ge(s["step"], steps[0])
            dve.tensor_scalar(C.top[:, :, :], top[:, :, :], C.gate[:, 2:3], None, ALU.mult).then_inc(s["both_done"], 1)
            dve.wait_ge(s["counted"], 1)
            link(dve.tensor_copy(run_n[0][:, :, :], ps_n[:, 1, :].rearrange("p (t e) -> p e t", e=E)))
            cur, d = 0, 1
            while d < TILES:
                link(dve.tensor_copy(run_n[1 - cur][:, :, 0:d], run_n[cur][:, :, 0:d]))
                link(dve.tensor_tensor(run_n[1 - cur][:, :, d:TILES], run_n[cur][:, :, d:TILES],
                                       run_n[cur][:, :, 0:TILES - d], ALU.add))
                cur, d = 1 - cur, 2 * d
            link(dve.tensor_scalar(tiles_i[:, :], run_n[cur][:, :, TILES - 1], float(SLOT_T - 1), None, ALU.add))
            link(dve.tensor_scalar(tiles_i[:, :], tiles_i[:, :], SLOT_T.bit_length() - 1, None, ALU.arith_shift_right))
            link(dve.tensor_copy(tiles_f[:, :], tiles_i[:, :]))
            link(dve.tensor_copy(ends[0][:, :], tiles_f[:, :]))
            ec, d = 0, 1
            while d < E:
                link(dve.tensor_copy(ends[1 - ec][:, 0:d], ends[ec][:, 0:d]))
                link(dve.tensor_tensor(ends[1 - ec][:, d:E], ends[ec][:, d:E], ends[ec][:, 0:E - d], ALU.add))
                ec, d = 1 - ec, 2 * d
            link(dve.tensor_tensor(starts[:, :], ends[ec][:, :], tiles_f[:, :], ALU.subtract))
            link(dve.tensor_tensor(run_n[1 - cur][:, :, :], run_n[cur][:, :, :],
                                   ps_n[:, 1, :].rearrange("p (t e) -> p e t", e=E), ALU.subtract))
            link(dve.tensor_tensor(big[0][:, :, :], run_n[1 - cur][:, :, :].rearrange("p e t -> p t e"),
                                   ps_n[:, 0, :].rearrange("p (t e) -> p t e", e=E), ALU.add))
            link(dve.scalar_tensor_tensor(out=big[1][:, :, :], in0=starts[:, :].unsqueeze(1).broadcast_to((P, TILES, E)),
                                          scalar=float(SLOT_T), in1=big[0][:, :, :], op0=ALU.mult, op1=ALU.add))
            for c in range(TOPK):
                link(dve.tensor_tensor(big[0][:, :, :], big[1][:, :, :], hot[:, c, :, :], ALU.mult))
                link(dve.tensor_reduce(slot_f[:, c, :], big[0][:, :, :], AX, ALU.add))
            link(dve.tensor_copy(C.slots[:, :, :], slot_f[:, :, :]))
            link(dve.tensor_scalar(part_i[:, 0, :, :], C.slots[:, :, :], P.bit_length() - 1, None, ALU.arith_shift_right))
            link(dve.tensor_scalar(part_i[:, 1, :, :], C.slots[:, :, :], P - 1, None, ALU.bitwise_and))
            link(dve.tensor_copy(part[:, :, :, :], part_i[:, :, :, :]))
            link(dve.tensor_tensor(past[:, :, :], ends[ec][:, :].unsqueeze(1).broadcast_to((P, NST, E)),
                                   over(iota[:, 0:NST], E), ALU.is_le))
            link(dve.tensor_reduce(expert_f[:, :], past[:, :, :], AX, ALU.add))
            link(dve.tensor_scalar(C.expert[:, :], expert_f[:, :], float(E - 1), None, ALU.min))

            def one_hot(T, c):
                if not isinstance(T, int) or T >= 1:
                    dve.wait_ge(s["inv_done"], T * TOPK + c - 1)
                dve.tensor_scalar(low_hot[:, c, :], iota[:, :], part[:, 1, c, bass.ds(T, 1)], None,
                                  ALU.is_equal).then_inc(s["low_done"], 1)
                dve.tensor_scalar(high_tok[:, c, :], iota[:, 0:NSUB], part[:, 0, c, bass.ds(T, 1)],
                                  token[:, bass.ds(T, 1)], ALU.is_equal, ALU.mult).then_inc(s["high_done"], 1)

            for c in range(TOPK):
                one_hot(0, c)
            with dve.Fori(1, TILES) as T:
                for c in range(TOPK):
                    one_hot(T, c)
            dve.wait_ge(s["inv_done"], TILES * TOPK)
            link(dve.tensor_copy(C.token_of[:, :], ps_inv[:, 0:NSUB]))


def experts(nc, C, xn_dram, y_dram, parts_dram, split, b1, b2):
    with ExitStack() as ctx:
        m = Mem(nc, ctx, C.sems, "exp")
        w1h, w1l, w2s = split["w1h"], split["w1l"], split["w2s"]
        bias_f = m.sb("bias_f", [P, 2, P])
        rest_f = m.sb("rest_f", [P, 2, P])
        bias_p = m.sb("bias_p", [P, 2, 3, P], BF16)
        b1s = m.sb("b1s", [3, E * F], BF16)
        b2s = m.sb("b2s", [3, E * D], BF16)
        ones3 = m.sb("ones3", [3, P], BF16)
        at_now = m.sb("at_now", [P, 2], I32)
        xg = m.sb("xg", [P, 2, D])
        xhi = m.sb("xhi", [P, 2, D], BF16)
        xlo = m.sb("xlo", [P, 2, D], BF16)
        h = m.sb("h", [P, F])
        hhi = m.sb("hhi", [P, F], BF16)
        hlo = m.sb("hlo", [P, F], BF16)
        y = m.sb("y", [P, 2, D])
        yb = m.sb("yb", [P, 2, D])
        ps_x = m.ps("ps_x", [P, 2, 512])
        ps_h = m.ps("ps_h", [P, 2, 512])
        ps_t = m.ps("ps_t", [P, 2, 512])
        ps_y = m.ps("ps_y", [P, 2, 512])
        names = ("bias_in", "bias_step", "bias_parts", "bias_rows", "ones_done", "at_done", "turned_x", "xhi_done", "xlo_done", "h_done",
                 "gelu_done", "turned_h", "hhi_done", "hlo_done", "y_done", "y_half", "y_sum")
        s = {n: m.sem(n) for n in names}
        gathered = [m.sem(f"gathered{i}") for i in range(2)]
        stored = [m.sem(f"stored{i}") for i in range(2)]
        C.slots_stored = stored
        B1R, B2R = E * F // P, E * D // P
        block = ctx.enter_context(nc.Block())

        def run(eng, step):
            for j in range(2):
                for u in range(SUB):
                    step(j * SUB + u, u, j)
            with eng.Fori(2, NST - 1) as j:
                for u in range(SUB):
                    step(j * SUB + u, u, j)
            for u in range(SUB):
                step((NST - 1) * SUB + u, u, NST - 1)
            step(NSUB, 0, NST)

        def front(t):
            return not isinstance(t, int) or t < NSUB

        def back(t):
            return not isinstance(t, int) or t >= 1

        def ahead(t):
            return not isinstance(t, int) or t + 1 < NSUB

        @block.sync
        def _(sp):
            sp.dma_start(bias_f[0:B1R, 0, :], b1.rearrange("e (c f) -> (e c) f", f=P)).then_inc(s["bias_in"], 16)
            sp.dma_start(bias_f[0:B2R, 1, :], b2.rearrange("e (c f) -> (e c) f", f=P)).then_inc(s["bias_in"], 16)
            sp.wait_ge(s["bias_step"], 10)
            for n, rows in enumerate((B1R, B2R)):
                for i in range(3):
                    sp.dma_start(parts_dram[n, i, 0:rows * P].rearrange("(r f) -> r f", f=P),
                                 bias_p[0:rows, n, i, :]).then_inc(s["bias_parts"], 16)
            sp.wait_ge(s["bias_parts"], 96)
            for n, (dst, rows) in enumerate(((b1s, B1R), (b2s, B2R))):
                sp.dma_start(dst[:, :], parts_dram[n, :, 0:rows * P]).then_inc(s["bias_rows"], 16)

            def step(t, u, j):
                if back(t):
                    sp.wait_ge(s["y_sum"], t)
                    sp.dma_start(y_dram[bass.ds((t - 1) * P, P), :], y[:, 1 - u, :]).then_inc(stored[1 - u], 16)

            run(sp, step)
            for u in range(2):
                sp.wait_ge(stored[u], 16 * NSUB // 2)

        @block.gpsimd
        def _(pool):
            pool.memset(ones3[:, :], 1.0).then_inc(s["ones_done"], 1)

            def step(t, u, j):
                if not front(t):
                    return
                if not isinstance(t, int) or t >= 2:
                    pool.wait_ge(s["turned_x"], t - 1)
                    pool.wait_ge(gathered[u], 16 * j)
                pool.tensor_copy(at_now[:, u:u + 1], C.token_of[:, bass.ds(t, 1)]).then_inc(s["at_done"], 1)
                copied = counted(pool, t + 1)
                pool.wait_ge(C.rows_stored, 16 * B)
                pool.wait_ge(s["at_done"], copied)
                pool.indirect_dma_start(out=xg[:, u, :], out_offset=None, in_=xn_dram[:, :],
                                        in_offset=bass.IndirectOffsetOnAxis(ap=at_now[:, u:u + 1].bitcast(U32), axis=0)
                                        ).then_inc(gathered[u], 16)

            run(pool, step)

        @block.tensor
        def _(pe):
            pe.wait_ge(s["bias_rows"], 32)
            pe.wait_ge(s["ones_done"], 1)

            def turn_x(t, u, j):
                pe.wait_ge(gathered[u], 16 * (j + 1))
                if not isinstance(t, int) or t >= 2:
                    pe.wait_ge(s["xlo_done"], t - 1)
                for k in range(KD):
                    mm = pe.transpose(ps_x[:, u, k * P:(k + 1) * P], xg[:, u, k * P:(k + 1) * P], C.ident[:, :])
                mm.then_inc(s["turned_x"], 1)

            def turn_h(t):
                for j in range(2):
                    pe.wait_ge(s["gelu_done"], 2 * t + j + 1)
                    wait(pe, s["hlo_done"], 2 * (t - 1) + j + 1 if not isinstance(t, int) or t > 0 else 0)
                    for f in range(4):
                        mm = pe.transpose(ps_t[:, j, f * P:(f + 1) * P], h[:, (4 * j + f) * P:(4 * j + f + 1) * P],
                                          C.ident[:, :])
                    mm.then_inc(s["turned_h"], 1)

            def first(t, u, e):
                pe.wait_ge(s["xhi_done"], t + 1)
                for j in range(2):
                    if not isinstance(t, int) or t >= 1:
                        pe.wait_ge(s["gelu_done"], 2 * (t - 1) + j + 1)
                    cols = slice(j * 512, (j + 1) * 512)
                    out = ps_h[:, j, :]
                    for k in range(KD):
                        hi = xhi[:, u, k * P:(k + 1) * P]
                        pe.matmul(out, hi, w1h[:, bass.ds(e * KD + k, 1), cols].rearrange("p o f -> p (o f)"),
                                  start=(k == 0), stop=False)
                        pe.matmul(out, hi, w1l[:, bass.ds(e * KD + k, 1), cols].rearrange("p o f -> p (o f)"),
                                  start=False, stop=False)
                    pe.matmul(out, ones3[:, :], b1s[:, bass.ds(e * F + j * 512, 512)], start=False, stop=False)
                    if j == 0:
                        pe.wait_ge(s["xlo_done"], t + 1)
                    for k in range(KD):
                        mm = pe.matmul(out, xlo[:, u, k * P:(k + 1) * P],
                                       w1h[:, bass.ds(e * KD + k, 1), cols].rearrange("p o f -> p (o f)"),
                                       start=False, stop=(k == KD - 1))
                    mm.then_inc(s["h_done"], 1)

            def second(t, u, e):
                if not isinstance(t, int) or t >= 2:
                    pe.wait_ge(s["y_sum"], t - 1)
                out = ps_y[:, u, :]
                for f in range(FCH):
                    if f % 4 == 0:
                        pe.wait_ge(s["hhi_done"], 2 * t + f // 4 + 1)
                    pe.matmul(out, hhi[:, f * P:(f + 1) * P],
                              w2s[:, bass.ds(e * FCH + f, 1), 0:2 * D].rearrange("p o f -> p (o f)"),
                              start=(f == 0), stop=False)
                for f in range(FCH):
                    if f % 4 == 0:
                        pe.wait_ge(s["hlo_done"], 2 * t + f // 4 + 1)
                    pe.matmul(out[:, 0:D], hlo[:, f * P:(f + 1) * P],
                              w2s[:, bass.ds(e * FCH + f, 1), 0:D].rearrange("p o f -> p (o f)"),
                              start=False, stop=False)
                pe.matmul(out[:, 0:D], ones3[:, :], b2s[:, bass.ds(e * D, D)], start=False,
                          stop=True).then_inc(s["y_done"], 1)

            state = {}

            def expert(j):
                return pe.value_load(C.expert[0:1, bass.ds(j, 1)], min_val=0, max_val=E - 1)

            def step(t, u, j):
                if isinstance(t, int) and t == 0:
                    turn_x(0, 0, 0)
                if ahead(t):
                    turn_x(t + 1, 1 - u, j + u)
                if back(t):
                    turn_h(t - 1)
                if front(t):
                    if u == 0:
                        state["now"] = expert(j)
                    first(t, u, state["now"])
                if back(t):
                    second(t - 1, 1 - u, expert(j - 1) if u == 0 else state["now"])

            run(pe, step)

        @block.scalar
        def _(act):
            def xhi_of(t, u):
                act.wait_ge(s["turned_x"], t + 1)
                if not isinstance(t, int) or t >= 2:
                    act.wait_ge(s["h_done"], 2 * (t - 2) + 2)
                act.activation(xhi[:, u, :], ps_x[:, u, 0:D], ACT.Copy).then_inc(s["xhi_done"], 1)

            def step(t, u, j):
                if isinstance(t, int) and t == 0:
                    xhi_of(0, 0)
                if ahead(t):
                    xhi_of(t + 1, 1 - u)
                if back(t):
                    for i in range(2):
                        act.wait_ge(s["turned_h"], 2 * (t - 1) + i + 1)
                        if not isinstance(t, int) or t >= 2:
                            act.wait_ge(s["y_done"], t - 1)
                        act.activation(hhi[:, i * 512:(i + 1) * 512], ps_t[:, i, :], ACT.Copy).then_inc(s["hhi_done"], 1)
                if front(t):
                    for i in range(2):
                        act.wait_ge(s["h_done"], 2 * t + i + 1)
                        if not isinstance(t, int) or t >= 1:
                            act.wait_ge(s["turned_h"], 2 * (t - 1) + i + 1)
                        act.activation(h[:, i * 512:(i + 1) * 512], ps_h[:, i, :],
                                       ACT.Gelu_apprx_tanh).then_inc(s["gelu_done"], 1)
                if back(t):
                    act.wait_ge(s["y_done"], t)
                    if not isinstance(t, int) or t >= 3:
                        act.wait_ge(s["y_sum"], t - 2)
                    act.activation(yb[:, 1 - u, :], ps_y[:, 1 - u, D:2 * D], ACT.Copy).then_inc(s["y_half"], 1)

            run(act, step)

        @block.vector
        def _(dve):
            dve.wait_ge(s["bias_in"], 32)
            n = 0
            for i in range(3):
                src = bias_f if i == 0 else rest_f
                for k, rows in enumerate((B1R, B2R)):
                    dve.tensor_copy(bias_p[0:rows, k, i, :], src[0:rows, k, :]).then_inc(s["bias_step"], 1)
                n += 2
                dve.wait_ge(s["bias_step"], n)
                if i < 2:
                    for k, rows in enumerate((B1R, B2R)):
                        dve.tensor_tensor(rest_f[0:rows, k, :], src[0:rows, k, :], bias_p[0:rows, k, i, :],
                                          ALU.subtract).then_inc(s["bias_step"], 1)
                    n += 2
                    dve.wait_ge(s["bias_step"], n)

            def xlo_of(t, u):
                dve.wait_ge(s["xhi_done"], t + 1)
                if not isinstance(t, int) or t >= 2:
                    dve.wait_ge(s["h_done"], 2 * (t - 2) + 2)
                dve.tensor_tensor(xlo[:, u, :], ps_x[:, u, 0:D], xhi[:, u, :], ALU.subtract).then_inc(s["xlo_done"], 1)

            def step(t, u, j):
                if isinstance(t, int) and t == 0:
                    xlo_of(0, 0)
                if ahead(t):
                    xlo_of(t + 1, 1 - u)
                if back(t):
                    for i in range(2):
                        dve.wait_ge(s["hhi_done"], 2 * (t - 1) + i + 1)
                        if not isinstance(t, int) or t >= 2:
                            dve.wait_ge(s["y_done"], t - 1)
                        dve.tensor_tensor(hlo[:, i * 512:(i + 1) * 512], ps_t[:, i, :], hhi[:, i * 512:(i + 1) * 512],
                                          ALU.subtract).then_inc(s["hlo_done"], 1)
                    dve.wait_ge(s["y_half"], t)
                    if not isinstance(t, int) or t >= 3:
                        dve.wait_ge(stored[1 - u], 16 * (j - 1 if u == 0 else j))
                    dve.tensor_tensor(y[:, 1 - u, :], ps_y[:, 1 - u, 0:D], yb[:, 1 - u, :],
                                      ALU.add).then_inc(s["y_sum"], 1)

            run(dve, step)


def combine(nc, C, x1_dram, y_dram, x2_dram):
    with ExitStack() as ctx:
        m = Mem(nc, ctx, C.sems, "comb")
        R = 4
        at_now = m.sb("at_now", [P, R, TOPK], I32)
        yg = m.sb("yg", [P, R, TOPK, D])
        x = m.sb("x", [P, R, D])
        half_sum = m.sb("half_sum", [P, R, D])
        x2 = m.sb("x2", [P, R, D])
        at_done, half_done, x2_done = m.sem("at_done"), m.sem("half_done"), m.sem("x2_done")
        x_in = [m.sem(f"x_in{r}") for r in range(R)]
        gathered = [[m.sem(f"gathered{r}_{c}") for c in range(TOPK)] for r in range(R)]
        stored = [m.sem(f"stored{r}") for r in range(R)]
        block = ctx.enter_context(nc.Block())

        def run(eng, step):
            for r in range(R):
                step(r, r, 0)
            with eng.Fori(1, TILES // R) as i:
                for r in range(R):
                    step(i * R + r, r, i)

        def again(T):
            return not isinstance(T, int)

        @block.sync
        def _(sp):
            def step(T, r, i):
                if again(T):
                    sp.wait_ge(half_done, T - R + 1)
                sp.dma_start(x[:, r, :], x1_dram[bass.ds(T * P, P), :]).then_inc(x_in[r], 16)

            run(sp, step)

        @block.scalar
        def _(act):
            def step(T, r, i):
                act.wait_ge(x2_done, T + 1)
                act.dma_start(x2_dram[bass.ds(T * P, P), :], x2[:, r, :]).then_inc(stored[r], 16)

            run(act, step)
            for r in range(R):
                act.wait_ge(stored[r], 16 * TILES // R)

        @block.gpsimd
        def _(pool):
            def step(T, r, i):
                if again(T):
                    pool.wait_ge(x2_done, T - R + 1)
                    for c in range(TOPK):
                        pool.wait_ge(gathered[r][c], 16 * i)
                pool.tensor_copy(at_now[:, r, :].unsqueeze(2), C.slots[:, :, bass.ds(T, 1)]).then_inc(at_done, 1)
                copied = counted(pool, T + 1)
                for c in range(TOPK):
                    pool.wait_ge(C.slots_stored[c], 16 * NSUB // 2)
                    if c == 0:
                        pool.wait_ge(at_done, copied)
                    pool.indirect_dma_start(out=yg[:, r, c, :], out_offset=None, in_=y_dram[:, :],
                                            in_offset=bass.IndirectOffsetOnAxis(ap=at_now[:, r, c:c + 1].bitcast(U32), axis=0)
                                            ).then_inc(gathered[r][c], 16)

            run(pool, step)

        @block.vector
        def _(dve):
            def step(T, r, i):
                dve.wait_ge(x_in[r], 16 * (i + 1))
                for c in range(TOPK):
                    dve.wait_ge(gathered[r][c], 16 * (i + 1))
                if again(T):
                    dve.wait_ge(stored[r], 16 * i)
                dve.scalar_tensor_tensor(out=half_sum[:, r, :], in0=yg[:, r, 0, :], scalar=C.top[:, 0, bass.ds(T, 1)],
                                         in1=x[:, r, :], op0=ALU.mult, op1=ALU.add).then_inc(half_done, 1)
                dve.wait_ge(half_done, T + 1)
                dve.scalar_tensor_tensor(out=x2[:, r, :], in0=yg[:, r, 1, :], scalar=C.top[:, 1, bass.ds(T, 1)],
                                         in1=half_sum[:, r, :], op0=ALU.mult, op1=ALU.add).then_inc(x2_done, 1)

            run(dve, step)


def quantise_weights(nc, C, w_in, w_out, b_in):
    with ExitStack() as ctx:
        m = Mem(nc, ctx, C.sems, "qw")
        wi = m.sb("wi", [P, KD, F])
        wiT = m.sb("wiT", [P, FCH, D])
        amax = m.sb("amax", [P, 2, FCH])
        inv = m.sb("inv", [P, 2, FCH])
        scale = m.sb("scale", [P, 2, FCH])
        ps = m.ps("ps", [P, 4, 512])
        names = ("w_in_loaded", "w_out_loaded", "bias_loaded", "turned", "wiT_done", "step", "rounded", "back", "back_done")
        s = {n: m.sem(n) for n in names}
        block = ctx.enter_context(nc.Block())

        @block.sync
        def _(sp):
            sp.dma_start(wi[:, :, :], w_in.rearrange("(k p) f -> p k f", p=P)).then_inc(s["w_in_loaded"], 16)
            sp.dma_start(C.wo_q[:, :, :], w_out.rearrange("(f p) d -> p f d", p=P)).then_inc(s["w_out_loaded"], 16)
            with nc.allow_non_contiguous_dma(reason="a short bias, one element to a partition"):
                sp.dma_start(C.b_in[:, :], b_in.rearrange("(f p) -> p f", p=P)).then_inc(s["bias_loaded"], 16)

        @block.tensor
        def _(pe):
            pe.wait_ge(s["w_in_loaded"], 16)
            for f in range(FCH):
                for k in range(KD):
                    mm = pe.transpose(ps[:, f // 2, f % 2 * D + k * P:f % 2 * D + (k + 1) * P],
                                      wi[:, k, f * P:(f + 1) * P], C.ident[:, :])
                if f % 2:
                    mm.then_inc(s["turned"], 1)
            pe.wait_ge(s["rounded"], 1)
            for k in range(KD):
                for f in range(FCH):
                    mm = pe.transpose(ps[:, 2 * k + f // 4, f % 4 * P:(f % 4 + 1) * P],
                                      wiT[:, f, k * P:(k + 1) * P], C.ident[:, :])
                    if f % 4 == 3:
                        mm.then_inc(s["back"], 1)

        @block.scalar
        def _(act):
            for j in range(4):
                act.wait_ge(s["turned"], j + 1)
                act.activation(wiT[:, 2 * j:2 * j + 2, :].rearrange("p f d -> p (f d)"), ps[:, j, :],
                               ACT.Copy).then_inc(s["wiT_done"], 1)
            for j in range(4):
                act.wait_ge(s["back"], j + 1)
                act.activation(C.wi_q[:, j // 2, j % 2 * 512:(j % 2 + 1) * 512], ps[:, j, :],
                               ACT.Copy).then_inc(s["back_done"], 1)
            act.wait_ge(s["back_done"], 4)
            act.wait_ge(s["bias_loaded"], 16)

        @block.vector
        def _(dve):
            steps = [0]

            def link(ins):
                steps[0] += 1
                ins.then_inc(s["step"], 1)
                dve.wait_ge(s["step"], steps[0])

            dve.wait_ge(s["wiT_done"], 4)
            dve.wait_ge(s["w_out_loaded"], 16)
            for i, wt in enumerate((wiT, C.wo_q)):
                link(dve.tensor_reduce(amax[:, i, :], wt[:, :, :], AX, ALU.max, apply_absolute_value=True))
            link(dve.tensor_scalar(amax[:, :, :], amax[:, :, :], 1e-8, None, ALU.max))
            link(dve.reciprocal(inv[:, :, :], amax[:, :, :]))
            link(dve.tensor_scalar(scale[:, :, :], inv[:, :, :], 127.0, None, ALU.mult))
            link(dve.reciprocal(inv[:, :, :], scale[:, :, :]))
            link(dve.tensor_copy(C.wi_step[:, :], inv[:, 0, :]))
            for i, wt in enumerate((wiT, C.wo_q)):
                for f in range(FCH):
                    link(dve.tensor_scalar(wt[:, f, :], wt[:, f, :], scale[:, i, f:f + 1], MAGIC, ALU.mult, ALU.add))
                link(dve.tensor_scalar(wt[:, :, :], wt[:, :, :], MAGIC, 127.0, ALU.subtract, ALU.min))
                if i == 0:
                    link(dve.tensor_scalar(wt[:, :, :], wt[:, :, :], -128.0, None, ALU.max))
                    dve.tensor_copy(amax[:, 0, 0:1], inv[:, 0, 0:1]).then_inc(s["rounded"], 1)
                else:
                    for f in range(FCH):
                        link(dve.tensor_scalar(wt[:, f, :], wt[:, f, :], -128.0, inv[:, 1, f:f + 1], ALU.max, ALU.mult))


def ffn(nc, C, x3_dram, out_dram, b_out):
    G = 4
    NG = TILES // G
    with ExitStack() as octx:
        o = Mem(nc, octx, C.sems, "ffn")
        hid = o.sb("hid", [P, FCH, B * N])
        xhi = o.sb("xhi", [P, KD, B * N], BF16)
        xlo = o.sb("xlo", [P, KD, B * N], BF16)
        in_step = o.sb("in_step", [P, FCH])
        h_scale = o.sb("h_scale", [P, 2])

        def steps_of(dve, sem, count, amax_all, out, tmp):
            for ins in (lambda: dve.tensor_scalar(tmp[:, 0:1], amax_all[:, 0:1], 1e-8, None, ALU.max),
                        lambda: dve.reciprocal(tmp[:, 1:2], tmp[:, 0:1]),
                        lambda: dve.tensor_scalar(out[:, 0:1], tmp[:, 1:2], 32767.0, None, ALU.mult),
                        lambda: dve.reciprocal(out[:, 1:2], out[:, 0:1])):
                ins().then_inc(sem, 1)
                count += 1
                dve.wait_ge(sem, count)
            return count

        with ExitStack() as ctx:
            m = Mem(nc, ctx, C.sems, "f1")
            xn = hid[:, FCH - 2:FCH, :].rearrange("p f (t d) -> p (f t) d", d=D)
            stats = m.sb("stats", [P, TPB, 6])
            mv = m.sb("mv", [P, TILES, 2])
            veps = m.sb("veps", [P, TILES])
            rstd = m.sb("rstd", [P, TILES])
            amax = m.sb("amax", [P, TILES])
            amax1 = m.sb("amax1", [P, 1])
            amax_all = m.sb("amax_all", [P, 1])
            tmp = m.sb("tmp", [P, 2])
            x_scale = m.sb("x_scale", [P, 2])
            ps = m.ps("ps", [P, 4, 512])
            names = ("stats_done", "mean_done", "veps_done", "rstd_done", "xn_done", "amax_done", "all_done", "step",
                     "scaled", "rounded", "turned", "hi_done", "lo_done")
            s = {n: m.sem(n) for n in names}
            x_in = [m.sem(f"x_in{b}") for b in range(B)]
            x3_v = x3_dram.rearrange("(b t p) d -> b p t d", t=TPB, p=P)
            block = ctx.enter_context(nc.Block())

            @block.sync
            def _(sp):
                for b in range(B):
                    sp.dma_start(xn[:, b * TPB:(b + 1) * TPB, :], x3_v[b]).then_inc(x_in[b], 16)

            @block.gpsimd
            def _(pool):
                for b in range(B):
                    pool.wait_ge(s["veps_done"], b + 1)
                    a = b * TPB
                    pool.tensor_tensor(rstd[:, a:a + TPB], veps[:, a:a + TPB], C.half[:, 0:TPB],
                                       ALU.pow).then_inc(s["rstd_done"], 1)
                pool.wait_ge(s["amax_done"], TILES + 1)
                pool.partition_all_reduce(amax_all[:, :], amax1[:, :], P, RMAX).then_inc(s["all_done"], 1)

            @block.vector
            def _(dve):
                for b in range(B):
                    dve.wait_ge(x_in[b], 16)
                    wait(dve, s["mean_done"], b * TPB)
                    for t in range(TPB):
                        dve.bn_stats(stats[:, t, :], xn[:, b * TPB + t, :]).then_inc(s["stats_done"], 1)
                    for t in range(TPB):
                        dve.wait_ge(s["stats_done"], b * TPB + t + 1)
                        dve.bn_aggr(mv[:, b * TPB + t, :], stats[:, t, :]).then_inc(s["mean_done"], 1)
                    dve.wait_ge(s["mean_done"], (b + 1) * TPB)
                    dve.tensor_scalar(veps[:, b * TPB:(b + 1) * TPB], mv[:, b * TPB:(b + 1) * TPB, 1], EPS, None,
                                      ALU.add).then_inc(s["veps_done"], 1)
                    dve.wait_ge(s["rstd_done"], b + 1)
                    for t in range(TPB):
                        T = b * TPB + t
                        dve.tensor_scalar(xn[:, T, :], xn[:, T, :], mv[:, T, 0:1], rstd[:, T:T + 1], ALU.subtract,
                                          ALU.mult).then_inc(s["xn_done"], 1)
                    for t in range(TPB):
                        T = b * TPB + t
                        dve.wait_ge(s["xn_done"], T + 1)
                        dve.tensor_reduce(amax[:, T:T + 1], xn[:, T, :], AX, ALU.max,
                                          apply_absolute_value=True).then_inc(s["amax_done"], 1)
                dve.wait_ge(s["amax_done"], TILES)
                dve.tensor_reduce(amax1[:, :], amax[:, :], AX, ALU.max).then_inc(s["amax_done"], 1)
                dve.wait_ge(s["all_done"], 1)
                n = steps_of(dve, s["step"], 0, amax_all, x_scale, tmp)
                dve.tensor_scalar(in_step[:, :], C.wi_step[:, :], x_scale[:, 1:2], None, ALU.mult).then_inc(s["step"], 1)

                def round_tile(T):
                    dve.tensor_scalar(xn[:, T, :], xn[:, T, :], x_scale[:, 0:1], MAGIC, ALU.mult,
                                      ALU.add).then_inc(s["scaled"], 1)
                    dve.wait_ge(s["scaled"], T + 1)
                    dve.tensor_scalar(xn[:, T, :], xn[:, T, :], MAGIC, None, ALU.subtract).then_inc(s["rounded"], 1)

                def low(T):
                    dve.wait_ge(s["hi_done"], T + 1)
                    c = slice(T * P, (T + 1) * P)
                    dve.tensor_tensor(xlo[:, :, c], ps[:, T % 4, 0:D].rearrange("p (k t) -> p k t", k=KD), xhi[:, :, c],
                                      ALU.subtract).then_inc(s["lo_done"], 1)

                for T in range(TILES):
                    round_tile(T)
                    if T >= 2:
                        low(T - 2)
                low(TILES - 2)
                low(TILES - 1)

            @block.tensor
            def _(pe):
                for T in range(TILES):
                    pe.wait_ge(s["rounded"], T + 1)
                    wait(pe, s["lo_done"], T - 3)
                    for k in range(KD):
                        mm = pe.transpose(ps[:, T % 4, k * P:(k + 1) * P], xn[:, T, k * P:(k + 1) * P], C.ident[:, :])
                    mm.then_inc(s["turned"], 1)

            @block.scalar
            def _(act):
                for T in range(TILES):
                    act.wait_ge(s["turned"], T + 1)
                    act.activation(xhi[:, :, T * P:(T + 1) * P], ps[:, T % 4, 0:D].rearrange("p (k t) -> p k t", k=KD),
                                   ACT.Copy).then_inc(s["hi_done"], 1)

        with ExitStack() as ctx:
            m = Mem(nc, ctx, C.sems, "f2")
            amax = m.sb("amax", [P, NG, FCH])
            amax1 = m.sb("amax1", [P, 1])
            amax_all = m.sb("amax_all", [P, 1])
            tmp = m.sb("tmp", [P, 2])
            R = 8
            ps = m.ps("ps", [P, R, 512])
            h_done, gelu_done, amax_done, all_done, step = (m.sem(n) for n in ("h_done", "gelu_done", "amax_done", "all_done", "step"))
            block = ctx.enter_context(nc.Block())

            @block.tensor
            def _(pe):
                def group(g):
                    for f in range(FCH):
                        if not isinstance(g, int):
                            pe.wait_ge(gelu_done, (g - 1) * FCH + f + 1)
                        part = [(k, xx) for k in range(KD) for xx in (xhi, xlo)]
                        for i, (k, xx) in enumerate(part):
                            mm = pe.matmul(ps[:, f, :], C.wi_q[:, k, f * P:(f + 1) * P], xx[:, k, bass.ds(g * 512, 512)],
                                           start=(i == 0), stop=(i == len(part) - 1))
                        mm.then_inc(h_done, 1)

                group(0)
                with pe.Fori(1, NG) as g:
                    group(g)

            @block.scalar
            def _(act):
                with act.Fori(0, NG) as g:
                    for f in range(FCH):
                        act.wait_ge(h_done, g * FCH + f + 1)
                        act.activation(hid[:, f, bass.ds(g * 512, 512)], ps[:, f, :], ACT.Gelu, bias=C.b_in[:, f:f + 1],
                                       scale=in_step[:, f:f + 1]).then_inc(gelu_done, 1)

            @block.vector
            def _(dve):
                with dve.Fori(0, NG) as g:
                    for f in range(FCH):
                        dve.wait_ge(gelu_done, g * FCH + f + 1)
                        dve.tensor_reduce(amax[:, bass.ds(g, 1), f:f + 1].rearrange("p o f -> p (o f)"),
                                          hid[:, f, bass.ds(g * 512, 512)], AX, ALU.max,
                                          apply_absolute_value=True).then_inc(amax_done, 1)
                dve.wait_ge(amax_done, NG * FCH)
                dve.tensor_reduce(amax1[:, :], amax[:, :, :].rearrange("p g f -> p (g f)"), AX,
                                  ALU.max).then_inc(amax_done, 1)
                dve.wait_ge(all_done, 1)
                steps_of(dve, step, 0, amax_all, h_scale, tmp)

            @block.gpsimd
            def _(pool):
                pool.wait_ge(amax_done, NG * FCH + 1)
                pool.partition_all_reduce(amax_all[:, :], amax1[:, :], P, RMAX).then_inc(all_done, 1)

        with ExitStack() as ctx:
            m = Mem(nc, ctx, C.sems, "f3")
            R = 4
            hq = m.sb("hq", [P, 2, FCH, P])
            x = m.sb("x", [P, R, D])
            gbo = m.sb("gbo", [P, D])
            y = m.sb("y", [P, R, D])
            ps = m.ps("ps", [P, 2, 512])
            names = ("bias_in", "gbo_done", "scaled", "hq_done", "o_done", "xb_done", "y_done")
            s = {n: m.sem(n) for n in names}
            x_in = [m.sem(f"x_in{r}") for r in range(R)]
            stored = [m.sem(f"stored{r}") for r in range(R)]
            block = ctx.enter_context(nc.Block())

            def run(eng, step):
                for r in range(R):
                    step(r, r, 0)
                with eng.Fori(1, TILES // R) as i:
                    for r in range(R):
                        step(i * R + r, r, i)

            def again(T):
                return not isinstance(T, int)

            @block.sync
            def _(sp):
                sp.dma_start(gbo[:, :], b_out.partition_broadcast(P)).then_inc(s["bias_in"], 16)

                def step(T, r, i):
                    if again(T):
                        sp.wait_ge(s["y_done"], T - R + 1)
                    sp.dma_start(x[:, r, :], x3_dram[bass.ds(T * P, P), :]).then_inc(x_in[r], 16)

                run(sp, step)

            @block.scalar
            def _(act):
                def step(T, r, i):
                    act.wait_ge(s["y_done"], T + 1)
                    act.dma_start(out_dram[bass.ds(T * P, P), :], y[:, r, :]).then_inc(stored[r], 16)

                run(act, step)
                for r in range(R):
                    act.wait_ge(stored[r], 16 * TILES // R)

            @block.gpsimd
            def _(pool):
                pool.wait_ge(s["bias_in"], 16)
                pool.tensor_scalar(gbo[:, :], gbo[:, :], C.gate[:, 3:4], None, ALU.mult).then_inc(s["gbo_done"], 1)
                pool.wait_ge(s["gbo_done"], 1)

                def step(T, r, i):
                    pool.wait_ge(x_in[r], 16 * (i + 1))
                    pool.tensor_tensor(x[:, r, :], x[:, r, :], gbo[:, :], ALU.add).then_inc(s["xb_done"], 1)

                run(pool, step)

            @block.vector
            def _(dve):
                def quantise(T, u):
                    if again(T) or T >= 2:
                        dve.wait_ge(s["o_done"], T - 1)
                    dve.tensor_scalar(hq[:, u, :, :], hid[:, :, bass.ds(T * P, P)], h_scale[:, 0:1], MAGIC, ALU.mult,
                                      ALU.add).then_inc(s["scaled"], 1)
                    dve.wait_ge(s["scaled"], T + 1)
                    dve.tensor_scalar(hq[:, u, :, :], hq[:, u, :, :], MAGIC, h_scale[:, 1:2], ALU.subtract,
                                      ALU.mult).then_inc(s["hq_done"], 1)

                def residual(T, r, i):
                    dve.wait_ge(s["o_done"], T + 1)
                    dve.wait_ge(s["xb_done"], T + 1)
                    if again(T):
                        dve.wait_ge(stored[r], 16 * i)
                    dve.scalar_tensor_tensor(out=y[:, r, :], in0=ps[:, r % 2, 0:D], scalar=C.gate[:, 3:4], in1=x[:, r, :],
                                             op0=ALU.mult, op1=ALU.add).then_inc(s["y_done"], 1)

                quantise(0, 0)

                def step(T, r, i):
                    quantise(T + 1, (r + 1) % 2)
                    residual(T, r, i)

                for r in range(R):
                    step(r, r, 0)
                with dve.Fori(1, TILES // R - 1) as i:
                    for r in range(R):
                        step(i * R + r, r, i)
                for r in range(R):
                    T = TILES - R + r
                    if T + 1 < TILES:
                        quantise(T + 1, (r + 1) % 2)
                    dve.wait_ge(stored[r], 16 * (TILES // R - 1))
                    residual(T, r, TILES // R - 1)

            @block.tensor
            def _(pe):
                def step(T, r, i):
                    u = r % 2
                    pe.wait_ge(s["hq_done"], T + 1)
                    if again(T) or T >= 2:
                        pe.wait_ge(s["y_done"], T - 1)
                    for f in range(FCH):
                        mm = pe.matmul(ps[:, u, 0:D], hq[:, u, f, :], C.wo_q[:, f, :], start=(f == 0), stop=(f == FCH - 1))
                    mm.then_inc(s["o_done"], 1)

                run(pe, step)


class Consts:
    pass


def program(nc, io, out):
    x1_dram, x2_dram, x3_dram, xn_dram = (nc.dram_tensor(n, (B * N, D), F32).ap() for n in ("x1", "x2", "x3", "xn2"))
    y_dram = nc.dram_tensor("y_slots", (NSUB * P, D), F32).ap()
    parts_dram = nc.dram_tensor("bias_parts", (2, 3, E * F), BF16).ap()
    x_dram = io["x"].rearrange("b n d -> (b n) d")
    out_dram = out.rearrange("b n d -> (b n) d")
    with ExitStack() as ctx:
        C = Consts()
        C.sems = []
        m = Mem(nc, ctx, C.sems, "all")
        C.ident = m.sb("ident", [P, P])
        C.ones = m.sb("ones", [P, P])
        C.half = m.sb("half", [P, TPB])
        C.gate = m.sb("gate", [P, 4])
        C.ctxT = m.sb("ctxT", [P, 2, B, REPS * KEYS])
        C.ctxT_now = m.sb("ctxT_now", [P, 2, REPS * KEYS])
        C.top = m.sb("top", [P, TOPK, TILES])
        C.slots = m.sb("slots", [P, TOPK, TILES], I32)
        C.expert = m.sb("expert", [P, NST], I32)
        C.token_of = m.sb("token_of", [P, NSUB], I32)
        prologue(nc, io, C)
        with ExitStack() as moe:
            mm = Mem(nc, moe, C.sems, "moe")
            split = {"w1": io["L0_ffn_W1"], "w2": io["L0_ffn_W2"],
                     "w1h": mm.sb("w1h", [P, E * KD, F], BF16), "w1l": mm.sb("w1l", [P, E * KD, F], BF16),
                     "w2s": mm.sb("w2s", [P, E * FCH, 2 * D], BF16)}
            w0 = {"wq": io["L0_xattn_Wq"], "bq": io["L0_xattn_bq"], "wk": io["L0_xattn_Wk"], "bk": io["L0_xattn_bk"],
                  "wv": io["L0_xattn_Wv"], "bv": io["L0_xattn_bv"], "wo": io["L0_xattn_Wo"], "bo": io["L0_xattn_bo"]}
            attention(nc, "a0", C, x_dram, x1_dram, w0, 8, 0, CLAMP, split)
            routing(nc, C, x1_dram, xn_dram, io["L0_ffn_Wg"])
            experts(nc, C, xn_dram, y_dram, parts_dram, split, io["L0_ffn_b1"], io["L0_ffn_b2"])
        combine(nc, C, x1_dram, y_dram, x2_dram)
        clear_semaphores(nc, C)
        inner = HEADS * 64
        w1 = {"wq": io["L1_xattn_w_q"], "wk": io["L1_xattn_w_kv"][:, 0:inner], "wv": io["L1_xattn_w_kv"][:, inner:2 * inner],
              "wo": io["L1_xattn_w_out"], "bo": io["L1_xattn_b_out"]}
        attention(nc, "a1", C, x2_dram, x3_dram, w1, 2, 1, None)
        C.wi_q = m.sb("wi_q", [P, KD, F], BF16)
        C.wo_q = m.sb("wo_q", [P, FCH, D])
        C.b_in = m.sb("b_in", [P, FCH])
        C.wi_step = m.sb("wi_step", [P, FCH])
        quantise_weights(nc, C, io["L1_ffn_W_in"], io["L1_ffn_W_out"], io["L1_ffn_b_in"])
        ffn(nc, C, x3_dram, out_dram, io["L1_ffn_b_out"])


_INS = ["x", "ctx_768", "g_xattn", "g_ffn", "L0_xattn_Wq", "L0_xattn_bq", "L0_xattn_Wk", "L0_xattn_bk", "L0_xattn_Wv",
        "L0_xattn_bv", "L0_xattn_Wo", "L0_xattn_bo", "L0_ffn_Wg", "L0_ffn_W1", "L0_ffn_b1", "L0_ffn_W2", "L0_ffn_b2",
        "L1_xattn_w_q", "L1_xattn_w_kv", "L1_xattn_w_out", "L1_xattn_b_out", "L1_ffn_W_in", "L1_ffn_b_in", "L1_ffn_W_out",
        "L1_ffn_b_out"]


def kernel(**inputs):
    import numpy as _np
    import concourse.bacc as _bacc
    from concourse import mybir as _mybir
    from concourse.bass_utils import run_bass_kernel_spmd as _run

    nc = _bacc.Bacc("TRN2", target_bir_lowering=False, num_devices=1)
    arrays, io = {}, {}
    for name in _INS:
        a = _np.ascontiguousarray(inputs[name])
        arrays[f"in_{name}_dram"] = a
        io[name] = nc.dram_tensor(f"in_{name}_dram", a.shape, _mybir.dt.from_np(a.dtype), kind="ExternalInput").ap()
    out = nc.dram_tensor("out_0_dram", (B, N, D), F32, kind="ExternalOutput").ap()
    program(nc, io, out)
    r = _run(nc, [arrays], core_ids=[0])
    return r.results[0]["out_0_dram"]
```

```python
from contextlib import ExitStack

import concourse.bass as bass
from concourse import mybir

F32 = mybir.dt.float32
BF16 = mybir.dt.bfloat16
I32 = mybir.dt.int32
U32 = mybir.dt.uint32
ALU = mybir.AluOpType
ACT = mybir.ActivationFunctionType
AX = mybir.AxisListType.X
RMAX = bass.bass_isa.ReduceOp.max

P = 128
B, N, D = 4, 1024, 256
KEYS, DC = 77, 192
TILES = B * N // P
TPB = N // P
KD = D // P
HEADS = 16
ROWS = HEADS * KEYS
RCH = -(-ROWS // P)
CTX_K = [(0, P), (P, DC - P)]
REPS = 3
HPB = 6
SB = [(j * HPB, min(HEADS, (j + 1) * HPB)) for j in range(-(-HEADS // HPB))]
E, F, TOPK = 8, 1024, 2
FCH = F // P
SLOT_T = 256
SUB = SLOT_T // P
NST = (B * N * TOPK + E * (SLOT_T - 1)) // SLOT_T
NSUB = NST * SUB
EPS = 1e-5
CLAMP = 10000.0
MAGIC = 1.5 * 2.0 ** 23


def wait(eng, sem, value):
    if isinstance(value, int) and value <= 0:
        return
    eng.wait_ge(sem, value)


def counted(eng, value):
    return value if isinstance(value, int) else eng.snap(eng.to_reg(value))


class Mem:

    def __init__(self, nc, ctx, sems, tag):
        self.nc, self.ctx, self.sems, self.tag = nc, ctx, sems, tag

    def sb(self, name, shape, dt=F32):
        return self.ctx.enter_context(self.nc.sbuf_tensor(f"{self.tag}_{name}", shape, dt))

    def ps(self, name, shape, dt=F32):
        return self.ctx.enter_context(self.nc.psum_tensor(f"{self.tag}_{name}", shape, dt))

    def sem(self, name):
        self.sems.append(self.nc.alloc_semaphore(name=f"{self.tag}_{name}"))
        return self.sems[-1]


def clear_semaphores(nc, C):
    nc.clear_and_free_semaphores(C.sems)
    nc.all_engine_barrier()
    C.sems.clear()


def blocks_of(hpg):
    out = []
    for g in range(HEADS // hpg):
        lo, hi = g * hpg * KEYS, (g + 1) * hpg * KEYS
        out += [(c, g) for c in range(RCH) if c * P < hi and (c + 1) * P > lo]
    return out


def pieces_of(hpg):
    out = []
    for j, (a, z) in enumerate(SB):
        for g in range(HEADS // hpg):
            lo, hi = max(a, g * hpg), min(z, (g + 1) * hpg)
            if lo < hi:
                out.append((j, g, lo, hi))
    return out


def prologue(nc, io, C):
    with ExitStack() as ctx:
        m = Mem(nc, ctx, C.sems, "pro")
        ctx_rows = m.sb("ctx_rows", [KEYS, B, DC])
        g_row = m.sb("g_row", [P, 4])
        ps = m.ps("ps", [P, 2, 512])
        loaded, ones_set, ident_set, turned, copied = (m.sem(x) for x in ("loaded", "ones", "ident", "turned", "copied"))
        tanh_done, ones_row = m.sem("tanh_done"), m.sem("ones_row")
        block = ctx.enter_context(nc.Block())

        @block.sync
        def _(sp):
            sp.dma_start(ctx_rows[:, :, :], io["ctx_768"].rearrange("b k d -> k b d")).then_inc(loaded, 16)
            sp.dma_start(g_row[:, 0:2], io["g_xattn"].partition_broadcast(P)).then_inc(loaded, 16)
            sp.dma_start(g_row[:, 2:4], io["g_ffn"].partition_broadcast(P)).then_inc(loaded, 16)

        @block.gpsimd
        def _(pool):
            pool.memset(C.ident[:, :], 0.0).then_inc(ones_set, 1)
            pool.memset(C.ones[:, :], 1.0).then_inc(ones_set, 1)
            pool.memset(C.half[:, :], -0.5).then_inc(ones_set, 1)
            pool.wait_ge(ones_set, 1)
            pool.affine_select(out=C.ident[:, :], in_=C.ident[:, :], compare_op=ALU.not_equal, fill=1.0, base=0,
                               pattern=[[-1, P]], channel_multiplier=1).then_inc(ident_set, 1)
            pool.wait_ge(ones_set, 3)

        @block.tensor
        def _(pe):
            pe.wait_ge(loaded, 48)
            pe.wait_ge(ident_set, 1)
            for b in range(B):
                if b >= 2:
                    pe.wait_ge(copied, 2 * (b - 1))
                for k, (at, n) in enumerate(CTX_K):
                    pe.transpose(ps[0:n, b % 2, k * KEYS:(k + 1) * KEYS], ctx_rows[:, b, at:at + n],
                                 C.ident[0:KEYS, 0:KEYS]).then_inc(turned, 1)

        @block.vector
        def _(dve):
            dve.memset(C.ctxT[DC - P:DC - P + 1, 1, :, :], 1.0).then_inc(ones_row, 1)
            for b in range(B):
                dve.wait_ge(turned, 2 * (b + 1))
                for k, (at, n) in enumerate(CTX_K):
                    dve.tensor_copy(C.ctxT[0:n, k, b, :], ps[0:n, b % 2, k * KEYS:(k + 1) * KEYS]).then_inc(copied, 1)
            dve.wait_ge(copied, 2 * B)
            dve.wait_ge(ones_row, 1)

        @block.scalar
        def _(act):
            act.wait_ge(loaded, 48)
            act.activation(C.gate[:, :], g_row[:, :], ACT.Tanh).then_inc(tanh_done, 1)
            act.wait_ge(tanh_done, 1)


def attention(nc, C, x_in, x_out, w, gate_col, split):
    hpg = 8
    ng = HEADS // hpg
    dh = P // hpg
    blocks = blocks_of(hpg)
    scale = float(dh) ** -0.5
    NSB = len(SB)
    ctx_rows = (P, DC - P + 1)
    pieces = pieces_of(hpg)
    vgroups = [blocks[i:i + 4] for i in range(0, len(blocks), 4)]
    NVG = len(vgroups)
    RING, SKEW = 8, 3
    with ExitStack() as ctx:
        m = Mem(nc, ctx, C.sems, "a0")
        wq = m.sb("wq", [P, KD, ng * P])
        wk = m.sb("wk", [P, 2, ng * P])
        wv = m.sb("wv", [P, 2, ng * P])
        wo = m.sb("wo", [P, ng, D])
        bq = m.sb("bq", [P, ng])
        gbo = m.sb("gbo", [P, D])
        kmask = m.sb("kmask", [P, hpg])
        vmask = m.sb("vmask", [P, len(blocks), hpg])
        ctx_now = m.sb("ctx_now", [P, 2, REPS * KEYS])
        kblk = m.sb("kblk", [P, ng, hpg * KEYS])
        vblk = m.sb("vblk", [P, len(blocks), P])
        x = m.sb("x", [P, RING, D])
        stats = m.sb("stats", [P, 2, 6])
        mv = m.sb("mv", [P, 2, 2])
        veps = m.sb("veps", [P, 2])
        rstd = m.sb("rstd", [P, 2])
        xn = m.sb("xn", [P, D])
        xnT = m.sb("xnT", [P, KD, P])
        qT = m.sb("qT", [P, ng, P])
        mx = m.sb("mx", [P, HEADS])
        z = m.sb("z", [P, 2, ROWS])
        ssum = m.sb("ssum", [P, HEADS])
        rsum = m.sb("rsum", [P, 2, HEADS])
        pT = m.sb("pT", [P, RCH, P])
        attnT = m.sb("attnT", [P, ng, P])
        xo = m.sb("xo", [P, 2, D])
        stage = m.sb("stage", [P, 2, 2, 512])
        ps_sc = m.ps("ps_sc", [P, NSB, 512])
        ps_xq = m.ps("ps_xq", [P, 512])
        ps_p = m.ps("ps_p", [P, 3, 512])
        ps_vo = m.ps("ps_vo", [P, 512])
        ps_x, ps_q = ps_xq[:, 0:D], ps_xq[:, D:2 * D]
        ps_v, ps_o = ps_vo[:, 0:D], ps_vo[:, D:2 * D]

        weights_in, masks_done, gbo_done = m.sem("weights_in"), m.sem("masks_done"), m.sem("gbo_done")
        x_loaded = [m.sem(f"x_loaded{i}") for i in range(RING)]
        x_stored = [m.sem(f"x_stored{i}") for i in range(2)]
        piece_in = [m.sem(f"piece_in{i}") for i in range(2)]
        names = ("stats_done", "mean_done", "veps_done", "rstd_done", "xn_done", "turned_x", "xnT_done", "q_done",
                 "qT_done", "k_proj", "k_done", "v_proj", "v_done", "scores_done", "max_done", "mx_done", "z_done",
                 "zc_done", "exp_done", "sum_done", "rsum_done", "norm_done", "turned_p", "pT_done", "pv_done",
                 "attn_done", "o_done", "xo_done", "xb_done", "mask_step", "ctx_done", "hi_done", "lo_done")
        s = {n: m.sem(n) for n in names}
        N_WEIGHTS = 10
        MASKS = 4 + 2 * len(blocks)
        block = ctx.enter_context(nc.Block())

        def run(eng, slot):
            for t in range(TPB + SKEW):
                slot(t, t % TPB, t // TPB)
            with eng.Fori(1, B - 1) as b:
                for t in range(SKEW, TPB + SKEW):
                    slot(b * TPB + t, t % TPB, b + t // TPB)
            for t in range(SKEW, TPB + SKEW):
                slot((B - 1) * TPB + t, t % TPB, B - 1 + t // TPB)

        def has(T):
            return not isinstance(T, int) or 0 <= T < TILES

        @block.sync
        def _(sp):
            def load(T, r):
                sp.dma_start(x[:, r, :], x_in[bass.ds(T * P, P), :]).then_inc(x_loaded[r], 16)

            load(0, 0)
            for dst, name, bias in ((wk, "wk", "bk"), (wv, "wv", "bv")):
                for k, (at, n) in enumerate(CTX_K):
                    sp.dma_start(dst[0:n, k, :], w[name][at:at + n, :]).then_inc(weights_in, 16)
                sp.dma_start(dst[DC - P:DC - P + 1, 1, :], w[bias].unsqueeze(0)).then_inc(weights_in, 16)
            sp.dma_start(wq[:, :, :], w["wq"].rearrange("(k p) n -> p k n", p=P)).then_inc(weights_in, 16)
            sp.dma_start(wo[:, :, :], w["wo"].rearrange("(g p) n -> p g n", p=P)).then_inc(weights_in, 16)
            sp.dma_start(gbo[:, :], w["bo"].partition_broadcast(P)).then_inc(weights_in, 16)
            with nc.allow_non_contiguous_dma(reason="a short bias, one element to a partition"):
                sp.dma_start(bq[:, :], w["bq"].rearrange("(g p) -> p g", p=P)).then_inc(weights_in, 16)
            for r in range(1, RING - SKEW):
                load(r, r)

            def slot(T, t, b):
                if has(T):
                    wait(sp, s["hi_done"], 2 * (T - 1))
                    wait(sp, s["lo_done"], 2 * (T - 1))
                    sp.dma_start(stage[:, t % 2, 0, :],
                                 split["w1"].rearrange("e (c p) f -> (e c) p f", p=P)
                                 [bass.ds(b * (TPB // 2) + t // 2, 1), :, t % 2 * 512:(t % 2 + 1) * 512]
                                 .rearrange("o p f -> p (o f)")).then_inc(piece_in[t % 2], 16)
                    sp.dma_start(stage[:, t % 2, 1, :].rearrange("p (g d) -> p g d", d=D),
                                 split["w2"].rearrange("e (g p) d -> p (e g) d", p=P)
                                 [:, bass.ds(T * 2, 2), :]).then_inc(piece_in[t % 2], 16)
                if has(T - SKEW):
                    sp.wait_ge(s["xo_done"], T - SKEW + 1)
                    sp.dma_start(x_out[bass.ds((T - SKEW) * P, P), :],
                                 xo[:, (t - SKEW) % 2, :]).then_inc(x_stored[(t - SKEW) % 2], 16)
                    if has(T + RING - SKEW):
                        load(T + RING - SKEW, (t - SKEW) % RING)
                elif T + RING - SKEW < RING:
                    load(T + RING - SKEW, T + RING - SKEW)

            run(sp, slot)
            for i in range(2):
                sp.wait_ge(x_stored[i], 16 * TILES // 2)

        @block.gpsimd
        def _(pool):
            def power(T, u):
                pool.wait_ge(s["veps_done"], T + 1)
                pool.tensor_tensor(rstd[:, u:u + 1], veps[:, u:u + 1], C.half[:, 0:1], ALU.pow).then_inc(s["rstd_done"], 1)

            pool.memset(kmask[:, :], 1.0).then_inc(s["mask_step"], 1)
            pool.memset(vmask[:, :, :], 1.0).then_inc(s["mask_step"], 1)
            pool.wait_ge(s["mask_step"], 2)
            pool.affine_select(out=kmask[:, :], in_=kmask[:, :], compare_op=ALU.is_ge, fill=0.0, base=0,
                               pattern=[[-dh, hpg]], channel_multiplier=1).then_inc(s["mask_step"], 1)
            pool.wait_ge(s["mask_step"], 3)
            pool.affine_select(out=kmask[:, :], in_=kmask[:, :], compare_op=ALU.is_ge, fill=0.0, base=dh - 1,
                               pattern=[[dh, hpg]], channel_multiplier=-1).then_inc(s["mask_step"], 1)
            power(0, 0)
            power(1, 1)
            for i, (c, g) in enumerate(blocks):
                at = c * P - g * hpg * KEYS
                pool.affine_select(out=vmask[:, i, :], in_=vmask[:, i, :], compare_op=ALU.is_ge, fill=0.0, base=at,
                                   pattern=[[-KEYS, hpg]], channel_multiplier=1).then_inc(s["mask_step"], 1)
            pool.wait_ge(s["mask_step"], 4 + len(blocks))
            for i, (c, g) in enumerate(blocks):
                at = c * P - g * hpg * KEYS
                pool.affine_select(out=vmask[:, i, :], in_=vmask[:, i, :], compare_op=ALU.is_ge, fill=0.0,
                                   base=KEYS - 1 - at, pattern=[[KEYS, hpg]],
                                   channel_multiplier=-1).then_inc(s["mask_step"], 1)
            pool.wait_ge(weights_in, 16 * N_WEIGHTS)
            pool.tensor_scalar(gbo[:, :], gbo[:, :], C.gate[:, gate_col:gate_col + 1], None,
                               ALU.mult).then_inc(gbo_done, 1)
            pool.wait_ge(gbo_done, 1)

            def slot(T, t, b):
                u = t % 2
                if has(T + 2):
                    power(T + 2, u)
                if has(T - 1):
                    v = (t - 1) % 2
                    pool.wait_ge(s["rsum_done"], T)
                    zt = z[:, v, :].rearrange("p (h k) -> p h k", k=KEYS)
                    pool.tensor_tensor(zt, zt, rsum[:, v, :].unsqueeze(2).broadcast_to((P, HEADS, KEYS)),
                                       ALU.mult).then_inc(s["norm_done"], 1)
                if has(T):
                    pool.wait_ge(s["hi_done"], 2 * T + 2)
                    w1, w2 = split["w1s"], split["w2s"]
                    at = bass.ds(b * (TPB // 2) + t // 2, 1)
                    cols = slice(t % 2 * 512, (t % 2 + 1) * 512)
                    pool.tensor_tensor(w1[:, at, 1, cols].rearrange("p o f -> p (o f)"), stage[:, u, 0, :],
                                       w1[:, at, 0, cols].rearrange("p o f -> p (o f)"),
                                       ALU.subtract).then_inc(s["lo_done"], 1)
                    pool.tensor_tensor(w2[:, bass.ds(T * 2, 2), D:2 * D],
                                       stage[:, u, 1, :].rearrange("p (g d) -> p g d", d=D),
                                       w2[:, bass.ds(T * 2, 2), 0:D], ALU.subtract).then_inc(s["lo_done"], 1)
                    pool.wait_ge(s["xn_done"], T + 1)
                    pool.tensor_tensor(x[:, t, :], x[:, t, :], gbo[:, :], ALU.add).then_inc(s["xb_done"], 1)

            run(pool, slot)

        @block.tensor
        def _(pe):
            def turn_x(T):
                pe.wait_ge(s["xn_done"], T + 1)
                wait(pe, s["qT_done"], T)
                for k in range(KD):
                    mm = pe.transpose(ps_x[:, k * P:(k + 1) * P], xn[:, k * P:(k + 1) * P], C.ident[:, :])
                mm.then_inc(s["turned_x"], 1)

            def keys(T, b):
                pe.wait_ge(s["ctx_done"], b + 1)
                pe.wait_ge(s["xnT_done"], T + 1)
                for g in range(ng):
                    for k, n in enumerate(ctx_rows):
                        mm = pe.matmul(ps_q[:, g * KEYS:(g + 1) * KEYS], wk[0:n, k, g * P:(g + 1) * P],
                                       ctx_now[0:n, k, 0:KEYS], start=(k == 0), stop=(k == 1))
                mm.then_inc(s["k_proj"], 1)

            def values():
                for j, group in enumerate(vgroups):
                    for i, (c, g) in enumerate(group):
                        at0 = c * P % KEYS
                        for k, n in enumerate(ctx_rows):
                            mm = pe.matmul(ps_p[:, j, i * P:(i + 1) * P], ctx_now[0:n, k, at0:at0 + P],
                                           wv[0:n, k, g * P:(g + 1) * P], start=(k == 0), stop=(k == 1))
                    mm.then_inc(s["v_proj"], 1)

            turn_x(0)
            pe.wait_ge(weights_in, 16 * N_WEIGHTS)
            keys(0, 0)

            def slot(T, t, b):
                u = t % 2
                if has(T):
                    pe.wait_ge(s["xnT_done"], T + 1)
                    if t == 0:
                        pe.wait_ge(s["k_done"], b + 1)
                    for g in range(ng):
                        for k in range(KD):
                            mm = pe.matmul(ps_q[:, g * P:(g + 1) * P], wq[:, k, g * P:(g + 1) * P], xnT[:, k, :],
                                           start=(k == 0), stop=(k == KD - 1))
                    mm.then_inc(s["q_done"], 1)
                if has(T - 2):
                    pe.wait_ge(s["norm_done"], T - 1)
                    if t == 2:
                        pe.wait_ge(s["v_done"], NVG * (b + 1))
                    for j in range(3):
                        wait(pe, s["pT_done"], 3 * (T - 3) + j + 1)
                        for c in range(4 * j, min(RCH, 4 * j + 4)):
                            n = min(P, ROWS - c * P)
                            mm = pe.transpose(ps_p[0:n, j, c % 4 * P:(c % 4 + 1) * P], z[:, u, c * P:c * P + n],
                                              C.ident[:, :])
                        mm.then_inc(s["turned_p"], 1)
                if has(T - 3):
                    pe.wait_ge(s["attn_done"], T - 2)
                    for g in range(ng):
                        mm = pe.matmul(ps_o, attnT[:, g, :], wo[:, g, :], start=(g == 0), stop=(g == ng - 1))
                    mm.then_inc(s["o_done"], 1)
                if has(T):
                    pe.wait_ge(s["qT_done"], T + 1)
                    for j, (a, _) in enumerate(SB):
                        wait(pe, s["z_done"], NSB * (T - 1) + j + 1)
                        for jj, g, h0, h1 in pieces:
                            if jj == j:
                                mm = pe.matmul(ps_sc[:, j, (h0 - a) * KEYS:(h1 - a) * KEYS], qT[:, g, :],
                                               kblk[:, g, (h0 - g * hpg) * KEYS:(h1 - g * hpg) * KEYS],
                                               start=True, stop=True)
                        mm.then_inc(s["scores_done"], 1)
                if has(T + 1):
                    turn_x(T + 1)
                if has(T - 2):
                    wait(pe, s["xo_done"], T - 2)
                    for g in range(ng):
                        mine = [i for i, (c, gg) in enumerate(blocks) if gg == g]
                        for i in mine:
                            c = blocks[i][0]
                            if g == 0 and (i == mine[0] or c % 4 == 0):
                                pe.wait_ge(s["pT_done"], 3 * (T - 2) + c // 4 + 1)
                            if g == 1 and c == 8:
                                pe.wait_ge(s["pT_done"], 3 * (T - 2) + 3)
                            n = min(P, ROWS - c * P)
                            mm = pe.matmul(ps_v[:, g * P:(g + 1) * P], vblk[0:n, i, :], pT[0:n, c, :],
                                           start=(i == mine[0]), stop=(i == mine[-1]))
                    mm.then_inc(s["pv_done"], 1)
                if has(T) and t == 1:
                    wait(pe, s["pT_done"], 3 * (T - 1))
                    values()
                if has(T + 1) and t == TPB - 1:
                    keys(T + 1, b + 1)

            run(pe, slot)

        @block.scalar
        def _(act):
            def context(b):
                wait(act, s["v_proj"], NVG * b)
                wait(act, s["k_proj"], b)
                for k, n in enumerate(ctx_rows):
                    ins = act.activation(ctx_now[0:n, k, :].rearrange("p (r k) -> p r k", r=REPS),
                                         C.ctxT[0:n, k, bass.ds(b, 1), :].broadcast_to((n, REPS, KEYS)), ACT.Copy)
                ins.then_inc(s["ctx_done"], 1)

            def turned(T):
                act.wait_ge(s["turned_x"], T + 1)
                wait(act, s["q_done"], T)
                act.activation(xnT[:, :, :].rearrange("p k t -> p (k t)"), ps_x, ACT.Copy).then_inc(s["xnT_done"], 1)

            context(0)
            act.wait_ge(weights_in, 16 * N_WEIGHTS)
            turned(0)

            def slot(T, t, b):
                u = t % 2
                if has(T - 3):
                    act.wait_ge(s["pv_done"], T - 2)
                    wait(act, s["o_done"], T - 3)
                    act.activation(attnT[:, :, :].rearrange("p g t -> p (g t)"), ps_v, ACT.Copy).then_inc(s["attn_done"], 1)
                if has(T - 1):
                    v = (t - 1) % 2
                    act.wait_ge(s["zc_done"], T)
                    act.activation(z[:, v, :], z[:, v, :], ACT.Exp, scale=scale).then_inc(s["exp_done"], 1)
                if has(T):
                    act.wait_ge(s["q_done"], T + 1)
                    wait(act, s["scores_done"], NSB * T)
                    for g in range(ng):
                        ins = act.activation(qT[:, g, :], ps_q[:, g * P:(g + 1) * P], ACT.Identity, bias=bq[:, g:g + 1])
                    ins.then_inc(s["qT_done"], 1)
                if has(T - 2):
                    wait(act, s["pv_done"], T - 2)
                    for j in range(3):
                        act.wait_ge(s["turned_p"], 3 * (T - 2) + j + 1)
                        if j < 2:
                            ins = act.activation(pT[:, 4 * j:4 * j + 4, :].rearrange("p c t -> p (c t)"), ps_p[:, j, :],
                                                 ACT.Copy)
                        else:
                            last = ROWS - (RCH - 1) * P
                            act.activation(pT[:, RCH - 2, :], ps_p[:, 2, 0:P], ACT.Copy)
                            ins = act.activation(pT[0:last, RCH - 1, :], ps_p[0:last, 2, P:2 * P], ACT.Copy)
                        ins.then_inc(s["pT_done"], 1)
                if has(T):
                    act.wait_ge(piece_in[u], 32 * (b * (TPB // 2) + t // 2 + 1))
                    act.activation(split["w1s"][:, bass.ds(b * (TPB // 2) + t // 2, 1), 0,
                                                u * 512:(u + 1) * 512].rearrange("p o f -> p (o f)"),
                                   stage[:, u, 0, :], ACT.Copy).then_inc(s["hi_done"], 1)
                    act.activation(split["w2s"][:, bass.ds(T * 2, 2), 0:D],
                                   stage[:, u, 1, :].rearrange("p (g d) -> p g d", d=D),
                                   ACT.Copy).then_inc(s["hi_done"], 1)
                if has(T + 1):
                    turned(T + 1)
                if t == 4 and has(T + TPB):
                    context(b + 1)

            run(act, slot)

        @block.vector
        def _(dve):
            def ln_stats(T, u, r, turn):
                dve.wait_ge(x_loaded[r], 16 * (turn + 1))
                dve.bn_stats(stats[:, u, :], x[:, r, :]).then_inc(s["stats_done"], 1)
                dve.wait_ge(s["stats_done"], T + 1)

            def ln_mean(T, u):
                dve.bn_aggr(mv[:, u, :], stats[:, u, :]).then_inc(s["mean_done"], 1)
                dve.wait_ge(s["mean_done"], T + 1)
                dve.tensor_scalar(veps[:, u:u + 1], mv[:, u, 1:2], EPS, None, ALU.add).then_inc(s["veps_done"], 1)

            def ln(T, u, r):
                dve.wait_ge(s["rstd_done"], T + 1)
                wait(dve, s["turned_x"], T)
                dve.tensor_scalar(xn[:, :], x[:, r, :], mv[:, u, 0:1], rstd[:, u:u + 1], ALU.subtract,
                                  ALU.mult).then_inc(s["xn_done"], 1)

            def block_keys(T, b):
                dve.wait_ge(s["k_proj"], b + 1)
                wait(dve, s["scores_done"], T * NSB)
                for h in range(hpg):
                    ins = dve.tensor_scalar(kblk[:, :, h * KEYS:(h + 1) * KEYS],
                                            ps_q[:, 0:ng * KEYS].rearrange("p (g k) -> p g k", k=KEYS),
                                            kmask[:, h:h + 1], None, ALU.mult)
                ins.then_inc(s["k_done"], 1)

            def block_values(T, b):
                for j, group in enumerate(vgroups):
                    dve.wait_ge(s["v_proj"], b * NVG + j + 1)
                    if j == 0:
                        wait(dve, s["pv_done"], T)
                    n = len(group)
                    dve.tensor_tensor(
                        vblk[:, 4 * j:4 * j + n, :].rearrange("p i (h d) -> p (i h) d", d=dh),
                        ps_p[:, j, 0:n * P].rearrange("p (i d) -> p i d", d=dh),
                        vmask[:, 4 * j:4 * j + n, :].rearrange("p i h -> p (i h)").unsqueeze(2)
                        .broadcast_to((P, n * hpg, dh)), ALU.mult).then_inc(s["v_done"], 1)

            def sums(T, v):
                dve.wait_ge(s["exp_done"], T + 1)
                dve.tensor_reduce(ssum[:, :], z[:, v, :].rearrange("p (h k) -> p h k", k=KEYS), AX,
                                  ALU.add).then_inc(s["sum_done"], 1)
                dve.wait_ge(s["sum_done"], T + 1)
                wait(dve, s["norm_done"], T - 1)
                dve.reciprocal(rsum[:, v, :], ssum[:, :]).then_inc(s["rsum_done"], 1)

            ln_stats(0, 0, 0, 0)
            ln_mean(0, 0)
            ln_stats(1, 1, 1, 0)
            ln_mean(1, 1)
            ln(0, 0, 0)
            dve.wait_ge(s["mask_step"], 4)
            block_keys(0, 0)

            def slot(T, t, b):
                u = t % 2
                if has(T + 2):
                    ln_stats(T + 2, u, (t + 2) % RING, b + (t + 2) // RING)
                if has(T + 1):
                    ln(T + 1, (t + 1) % 2, (t + 1) % RING)
                if has(T + 2):
                    ln_mean(T + 2, u)
                if has(T - 2) and t == 2:
                    if isinstance(T, int) and T == 2:
                        dve.wait_ge(s["mask_step"], MASKS)
                    block_values(T - 2, b)
                if has(T - 1):
                    sums(T - 1, (t - 1) % 2)
                if has(T - SKEW):
                    v = (t - SKEW) % 2
                    turn = b if t >= SKEW else b - 1
                    dve.wait_ge(s["o_done"], T - SKEW + 1)
                    dve.wait_ge(s["xb_done"], T - SKEW + 1)
                    if has(T - SKEW - 2):
                        dve.wait_ge(x_stored[v], 16 * (turn * (TPB // 2) + (t - SKEW) % TPB // 2))
                    dve.scalar_tensor_tensor(out=xo[:, v, :], in0=ps_o, scalar=C.gate[:, gate_col:gate_col + 1],
                                             in1=x[:, (t - SKEW) % RING, :], op0=ALU.mult,
                                             op1=ALU.add).then_inc(s["xo_done"], 1)
                if has(T):
                    for j, (h0, h1) in enumerate(SB):
                        dve.wait_ge(s["scores_done"], T * NSB + j + 1)
                        dve.tensor_reduce(mx[:, h0:h1],
                                          ps_sc[:, j, 0:(h1 - h0) * KEYS].rearrange("p (h k) -> p h k", k=KEYS), AX,
                                          ALU.max).then_inc(s["max_done"], 1)
                    dve.wait_ge(s["max_done"], NSB * (T + 1))
                    dve.tensor_scalar(mx[:, :], mx[:, :], -CLAMP / scale, CLAMP / scale, ALU.max,
                                      ALU.min).then_inc(s["mx_done"], 1)
                    dve.wait_ge(s["mx_done"], T + 1)
                    if has(T - 2):
                        dve.wait_ge(s["turned_p"], 3 * (T - 1))
                    for j, (h0, h1) in enumerate(SB):
                        dve.scalar_tensor_tensor(
                            out=z[:, u, h0 * KEYS:h1 * KEYS].rearrange("p (h k) -> p h k", k=KEYS),
                            in0=ps_sc[:, j, 0:(h1 - h0) * KEYS].rearrange("p (h k) -> p h k", k=KEYS),
                            scalar=-CLAMP / scale, in1=mx[:, h0:h1].unsqueeze(2).broadcast_to((P, h1 - h0, KEYS)),
                            op0=ALU.max, op1=ALU.subtract).then_inc(s["z_done"], 1)
                    dve.wait_ge(s["z_done"], NSB * (T + 1))
                    dve.tensor_scalar(z[:, u, :], z[:, u, :], 0.0, None, ALU.min).then_inc(s["zc_done"], 1)
                if has(T + 1) and t == TPB - 1:
                    block_keys(T + 1, b + 1)

            run(dve, slot)


def routing(nc, C, x1_dram, xn_dram, wg):
    with ExitStack() as ctx:
        m = Mem(nc, ctx, C.sems, "route")
        x = m.sb("x", [P, TILES, D])
        wg_sb = m.sb("wg", [P, KD, E])
        stats = m.sb("stats", [P, TPB, 6])
        mv = m.sb("mv", [P, TILES, 2])
        veps = m.sb("veps", [P, TILES])
        rstd = m.sb("rstd", [P, TILES])
        xT = m.sb("xT", [P, 2, KD * P])
        lower = m.sb("lower", [P, P])
        iota_i = m.sb("iota_i", [P, P], I32)
        iota = m.sb("iota", [P, P])
        token_i = m.sb("token_i", [P, TILES], I32)
        token = m.sb("token", [P, TILES])
        rank_i = m.sb("rank_i", [P, E], I32)
        rank = m.sb("rank", [P, E])
        sig = m.sb("sig", [P, TILES, E])
        big = [m.sb(f"big{i}", [P, TILES, E]) for i in range(2)]
        hot = m.sb("hot", [P, TOPK, TILES, E])
        top = m.sb("top", [P, TOPK, TILES])
        first = m.sb("first", [P, TILES])
        both = m.sb("both", [P, TILES, E])
        run_n = [m.sb(f"run_n{i}", [P, E, TILES]) for i in range(2)]
        tiles_f = m.sb("tiles_f", [P, E])
        tiles_i = m.sb("tiles_i", [P, E], I32)
        ends = [m.sb(f"ends{i}", [P, E]) for i in range(2)]
        starts = m.sb("starts", [P, E])
        slot_f = m.sb("slot_f", [P, TOPK, TILES])
        part_i = m.sb("part_i", [P, 2, TOPK, TILES], I32)
        part = m.sb("part", [P, 2, TOPK, TILES])
        expert_f = m.sb("expert_f", [P, NST])
        past = m.sb("past", [P, NST, E])
        low_hot = m.sb("low_hot", [P, TOPK, P])
        high_tok = m.sb("high_tok", [P, TOPK, NSUB])
        ps_x = m.ps("ps_x", [P, 2, 512])
        ps_l = m.ps("ps_l", [P, 512])
        ps_n = m.ps("ps_n", [P, 2, TILES * E])
        ps_inv = m.ps("ps_inv", [P, 512])
        names = ("const_step", "wg_in", "stats_done", "mean_done", "veps_done", "rstd_done", "xn_done", "turned", "xT_done",
                 "logits_done", "exp_done", "step", "both_done", "counted", "low_done", "high_done", "inv_done", "xn_stored")
        s = {n: m.sem(n) for n in names}
        C.rows_stored = s["xn_stored"]
        x_in = [m.sem(f"x_in{b}") for b in range(B)]
        block = ctx.enter_context(nc.Block())
        x1_v = x1_dram.rearrange("(b t p) d -> b p t d", t=TPB, p=P)
        xn_v = xn_dram.rearrange("(b t p) d -> b p t d", t=TPB, p=P)

        @block.sync
        def _(sp):
            for b in range(B):
                sp.dma_start(x[:, b * TPB:(b + 1) * TPB, :], x1_v[b]).then_inc(x_in[b], 16)
            sp.dma_start(wg_sb[:, :, :], wg.rearrange("(k p) e -> p k e", p=P)).then_inc(s["wg_in"], 16)
            for b in range(B):
                sp.wait_ge(s["xn_done"], (b + 1) * TPB)
                sp.dma_start(xn_v[b], x[:, b * TPB:(b + 1) * TPB, :]).then_inc(s["xn_stored"], 16)
            sp.wait_ge(s["xn_stored"], 16 * B)

        @block.gpsimd
        def _(pool):
            pool.memset(lower[:, :], 1.0).then_inc(s["const_step"], 1)
            pool.iota(iota_i[:, :], pattern=[[1, P]], base=0, channel_multiplier=0).then_inc(s["const_step"], 1)
            pool.iota(token_i[:, :], pattern=[[P, TILES]], base=0, channel_multiplier=1).then_inc(s["const_step"], 1)
            pool.iota(rank_i[:, :], pattern=[[-1, E]], base=E, channel_multiplier=0).then_inc(s["const_step"], 1)
            pool.wait_ge(s["const_step"], 4)
            pool.affine_select(out=lower[:, :], in_=lower[:, :], compare_op=ALU.is_ge, fill=0.0, base=-1,
                               pattern=[[1, P]], channel_multiplier=-1).then_inc(s["const_step"], 1)
            pool.tensor_copy(iota[:, :], iota_i[:, :]).then_inc(s["const_step"], 1)
            pool.tensor_copy(token[:, :], token_i[:, :]).then_inc(s["const_step"], 1)
            pool.tensor_copy(rank[:, :], rank_i[:, :]).then_inc(s["const_step"], 1)
            for b in range(B):
                pool.wait_ge(s["veps_done"], b + 1)
                a = b * TPB
                pool.tensor_tensor(rstd[:, a:a + TPB], veps[:, a:a + TPB], C.half[:, 0:TPB],
                                   ALU.pow).then_inc(s["rstd_done"], 1)

        @block.tensor
        def _(pe):
            def turn(T, u):
                pe.wait_ge(s["xn_done"], T + 1)
                wait(pe, s["xT_done"], T - 1)
                for k in range(KD):
                    mm = pe.transpose(ps_x[:, u, k * P:(k + 1) * P], x[:, T, k * P:(k + 1) * P], C.ident[:, :])
                mm.then_inc(s["turned"], 1)

            def logits(T, u):
                pe.wait_ge(s["xT_done"], T + 1)
                for k in range(KD):
                    mm = pe.matmul(ps_l[:, T * E:(T + 1) * E], xT[:, u, k * P:(k + 1) * P], wg_sb[:, k, :],
                                   start=(k == 0), stop=(k == KD - 1))
                mm.then_inc(s["logits_done"], 1)

            pe.wait_ge(s["wg_in"], 16)
            for T in range(TILES):
                turn(T, T % 2)
                if T >= 1:
                    logits(T - 1, (T - 1) % 2)
            logits(TILES - 1, (TILES - 1) % 2)
            pe.wait_ge(s["both_done"], 1)
            pe.wait_ge(s["const_step"], 8)
            flat = both[:, :, :].rearrange("p t e -> p (t e)")
            pe.matmul(ps_n[:, 0, :], lower[:, :], flat, start=True, stop=True)
            pe.matmul(ps_n[:, 1, :], C.ones[:, :], flat, start=True, stop=True).then_inc(s["counted"], 1)

            def invert(T, c, start, stop):
                pe.wait_ge(s["low_done"], T * TOPK + c + 1)
                pe.wait_ge(s["high_done"], T * TOPK + c + 1)
                pe.matmul(ps_inv[:, 0:NSUB], low_hot[:, c, :], high_tok[:, c, :], start=start, stop=stop,
                          skip_group_check=True).then_inc(s["inv_done"], 1)

            invert(0, 0, True, False)
            invert(0, 1, False, False)
            with pe.Fori(1, TILES - 1) as T:
                for c in range(TOPK):
                    invert(T, c, False, False)
            invert(TILES - 1, 0, False, False)
            invert(TILES - 1, 1, False, True)

        @block.scalar
        def _(act):
            for T in range(TILES):
                act.wait_ge(s["turned"], T + 1)
                wait(act, s["logits_done"], T - 1)
                act.activation(xT[:, T % 2, :], ps_x[:, T % 2, 0:KD * P], ACT.Copy).then_inc(s["xT_done"], 1)
            act.wait_ge(s["logits_done"], TILES)
            act.activation(sig[:, :, :].rearrange("p t e -> p (t e)"), ps_l[:, 0:TILES * E], ACT.Exp,
                           scale=-1.0).then_inc(s["exp_done"], 1)

        @block.vector
        def _(dve):
            for b in range(B):
                dve.wait_ge(x_in[b], 16)
                if b:
                    dve.wait_ge(s["mean_done"], b * TPB)
                for t in range(TPB):
                    dve.bn_stats(stats[:, t, :], x[:, b * TPB + t, :]).then_inc(s["stats_done"], 1)
                for t in range(TPB):
                    dve.wait_ge(s["stats_done"], b * TPB + t + 1)
                    dve.bn_aggr(mv[:, b * TPB + t, :], stats[:, t, :]).then_inc(s["mean_done"], 1)
                dve.wait_ge(s["mean_done"], (b + 1) * TPB)
                dve.tensor_scalar(veps[:, b * TPB:(b + 1) * TPB], mv[:, b * TPB:(b + 1) * TPB, 1], EPS, None,
                                  ALU.add).then_inc(s["veps_done"], 1)
                dve.wait_ge(s["rstd_done"], b + 1)
                for t in range(TPB):
                    T = b * TPB + t
                    dve.tensor_scalar(x[:, T, :], x[:, T, :], mv[:, T, 0:1], rstd[:, T:T + 1], ALU.subtract,
                                      ALU.mult).then_inc(s["xn_done"], 1)

            steps = [0]

            def link(ins):
                steps[0] += 1
                ins.then_inc(s["step"], 1)
                dve.wait_ge(s["step"], steps[0])

            def over(ap, n):
                return ap.unsqueeze(2).broadcast_to((P, ap.shape[1], n))

            rank_b = rank[:, :].unsqueeze(1).broadcast_to((P, TILES, E))
            dve.wait_ge(s["exp_done"], 1)
            dve.wait_ge(s["const_step"], 8)
            link(dve.tensor_scalar(big[0][:, :, :], sig[:, :, :], 1.0, None, ALU.add))
            link(dve.reciprocal(sig[:, :, :], big[0][:, :, :]))
            for c in range(TOPK):
                link(dve.tensor_reduce(top[:, c, :], sig[:, :, :], AX, ALU.max))
                link(dve.tensor_tensor(big[0][:, :, :], sig[:, :, :], over(top[:, c, :], E), ALU.is_equal))
                link(dve.tensor_tensor(big[1][:, :, :], big[0][:, :, :], rank_b, ALU.mult))
                link(dve.tensor_reduce(first[:, :], big[1][:, :, :], AX, ALU.max))
                link(dve.tensor_tensor(hot[:, c, :, :], rank_b, over(first[:, :], E), ALU.is_equal))
                if c == 0:
                    link(dve.scalar_tensor_tensor(out=sig[:, :, :], in0=hot[:, c, :, :], scalar=-4.0, in1=sig[:, :, :],
                                                  op0=ALU.mult, op1=ALU.add))
            link(dve.tensor_tensor(both[:, :, :], hot[:, 0, :, :], hot[:, 1, :, :], ALU.add))
            dve.wait_ge(s["step"], steps[0])
            dve.tensor_scalar(C.top[:, :, :], top[:, :, :], C.gate[:, 2:3], None, ALU.mult).then_inc(s["both_done"], 1)
            dve.wait_ge(s["counted"], 1)
            link(dve.tensor_copy(run_n[0][:, :, :], ps_n[:, 1, :].rearrange("p (t e) -> p e t", e=E)))
            cur, d = 0, 1
            while d < TILES:
                link(dve.tensor_copy(run_n[1 - cur][:, :, 0:d], run_n[cur][:, :, 0:d]))
                link(dve.tensor_tensor(run_n[1 - cur][:, :, d:TILES], run_n[cur][:, :, d:TILES],
                                       run_n[cur][:, :, 0:TILES - d], ALU.add))
                cur, d = 1 - cur, 2 * d
            link(dve.tensor_scalar(tiles_i[:, :], run_n[cur][:, :, TILES - 1], float(SLOT_T - 1), None, ALU.add))
            link(dve.tensor_scalar(tiles_i[:, :], tiles_i[:, :], SLOT_T.bit_length() - 1, None, ALU.arith_shift_right))
            link(dve.tensor_copy(tiles_f[:, :], tiles_i[:, :]))
            link(dve.tensor_copy(ends[0][:, :], tiles_f[:, :]))
            ec, d = 0, 1
            while d < E:
                link(dve.tensor_copy(ends[1 - ec][:, 0:d], ends[ec][:, 0:d]))
                link(dve.tensor_tensor(ends[1 - ec][:, d:E], ends[ec][:, d:E], ends[ec][:, 0:E - d], ALU.add))
                ec, d = 1 - ec, 2 * d
            link(dve.tensor_tensor(starts[:, :], ends[ec][:, :], tiles_f[:, :], ALU.subtract))
            link(dve.tensor_tensor(run_n[1 - cur][:, :, :], run_n[cur][:, :, :],
                                   ps_n[:, 1, :].rearrange("p (t e) -> p e t", e=E), ALU.subtract))
            link(dve.tensor_tensor(big[0][:, :, :], run_n[1 - cur][:, :, :].rearrange("p e t -> p t e"),
                                   ps_n[:, 0, :].rearrange("p (t e) -> p t e", e=E), ALU.add))
            link(dve.scalar_tensor_tensor(out=big[1][:, :, :], in0=starts[:, :].unsqueeze(1).broadcast_to((P, TILES, E)),
                                          scalar=float(SLOT_T), in1=big[0][:, :, :], op0=ALU.mult, op1=ALU.add))
            for c in range(TOPK):
                link(dve.tensor_tensor(big[0][:, :, :], big[1][:, :, :], hot[:, c, :, :], ALU.mult))
                link(dve.tensor_reduce(slot_f[:, c, :], big[0][:, :, :], AX, ALU.add))
            link(dve.tensor_copy(C.slots[:, :, :], slot_f[:, :, :]))
            link(dve.tensor_scalar(part_i[:, 0, :, :], C.slots[:, :, :], P.bit_length() - 1, None, ALU.arith_shift_right))
            link(dve.tensor_scalar(part_i[:, 1, :, :], C.slots[:, :, :], P - 1, None, ALU.bitwise_and))
            link(dve.tensor_copy(part[:, :, :, :], part_i[:, :, :, :]))
            link(dve.tensor_tensor(past[:, :, :], ends[ec][:, :].unsqueeze(1).broadcast_to((P, NST, E)),
                                   over(iota[:, 0:NST], E), ALU.is_le))
            link(dve.tensor_reduce(expert_f[:, :], past[:, :, :], AX, ALU.add))
            link(dve.tensor_scalar(C.expert[:, :], expert_f[:, :], float(E - 1), None, ALU.min))

            def one_hot(T, c):
                if not isinstance(T, int) or T >= 1:
                    dve.wait_ge(s["inv_done"], T * TOPK + c - 1)
                dve.tensor_scalar(low_hot[:, c, :], iota[:, :], part[:, 1, c, bass.ds(T, 1)], None,
                                  ALU.is_equal).then_inc(s["low_done"], 1)
                dve.tensor_scalar(high_tok[:, c, :], iota[:, 0:NSUB], part[:, 0, c, bass.ds(T, 1)],
                                  token[:, bass.ds(T, 1)], ALU.is_equal, ALU.mult).then_inc(s["high_done"], 1)

            for c in range(TOPK):
                one_hot(0, c)
            with dve.Fori(1, TILES) as T:
                for c in range(TOPK):
                    one_hot(T, c)
            dve.wait_ge(s["inv_done"], TILES * TOPK)
            link(dve.tensor_copy(C.token_of[:, :], ps_inv[:, 0:NSUB]))


def experts(nc, C, xn_dram, y_dram, split, b1, b2):
    HB = FCH // 2
    PER = SUB * HB
    with ExitStack() as ctx:
        m = Mem(nc, ctx, C.sems, "exp")
        w1s, w2s = split["w1s"], split["w2s"]
        b1_rows = m.sb("b1_rows", [E * FCH, P])
        b1T = m.sb("b1T", [P, E, FCH])
        b2_all = m.sb("b2_all", [P, E, D])
        w1_now = m.sb("w1_now", [P, 2, KD, 2, F], BF16)
        b1_now = m.sb("b1_now", [P, 2, FCH])
        at_now = m.sb("at_now", [P, 2, SUB], I32)
        xg = m.sb("xg", [P, 2, SUB, D])
        xhi = m.sb("xhi", [P, KD, SLOT_T], BF16)
        xlo = m.sb("xlo", [P, KD, SLOT_T], BF16)
        h = m.sb("h", [P, FCH, SLOT_T])
        hhi = m.sb("hhi", [P, 2, FCH, SLOT_T], BF16)
        hlo = m.sb("hlo", [P, 2, FCH, SLOT_T], BF16)
        y = m.sb("y", [P, SUB, D])
        yb = m.sb("yb", [P, SUB, D])
        ps_x = m.ps("ps_x", [P, 2, 512])
        ps_h = m.ps("ps_h", [P, HB, 512])
        ps_y = m.ps("ps_y", [P, SUB, 512])
        names = ("bias_in", "b1_turned", "b1_done", "b1_now_done", "w1_now_done", "at_done", "turned_x", "xhi_done",
                 "xlo_done", "h_done", "gelu_done", "hhi_done", "hlo_done", "y_done", "y_low", "y_sum")
        s = {n: m.sem(n) for n in names}
        gathered = [[m.sem(f"gathered{v}_{u}") for u in range(SUB)] for v in range(2)]
        stored = [m.sem(f"stored{u}") for u in range(SUB)]
        C.slots_stored = stored
        for sem in stored:
            C.sems.remove(sem)
        block = ctx.enter_context(nc.Block())
        PEEL = 3

        def run(eng, step):
            for j in range(PEEL):
                step(j, j % 2, j // 2)
            with eng.Fori(0, (NST - PEEL) // 2 - 1) as i:
                for d in range(2):
                    j = PEEL + d
                    step(i * 2 + j, j % 2, i + j // 2)
            for j in range(NST - 2, NST + 1):
                step(j, j % 2, j // 2)

        def has(j):
            return not isinstance(j, int) or 0 <= j < NST

        @block.sync
        def _(sp):
            sp.dma_start(b1_rows[:, :], b1.rearrange("e (c f) -> (e c) f", f=P)).then_inc(s["bias_in"], 16)
            sp.dma_start(b2_all[:, :, :].rearrange("p e d -> p (e d)"),
                         b2.rearrange("e d -> (e d)").partition_broadcast(P)).then_inc(s["bias_in"], 16)

            def step(j, v, n):
                if has(j - 1):
                    for u in range(SUB):
                        sp.wait_ge(s["y_sum"], (j - 1) * SUB + u + 1)
                        sp.dma_start(y_dram[bass.ds((j - 1) * SLOT_T + u * P, P), :], y[:, u, :]).then_inc(stored[u], 16)

            run(sp, step)
            for u in range(SUB):
                sp.wait_ge(stored[u], 16 * NST)

        @block.gpsimd
        def _(pool):
            def step(j, v, n):
                if not has(j):
                    return
                if has(j - 2):
                    pool.wait_ge(s["turned_x"], j - 1)
                    for u in range(SUB):
                        pool.wait_ge(gathered[v][u], 16 * n)
                pool.tensor_copy(at_now[:, v, :], C.token_of[:, bass.ds(j * SUB, SUB)]).then_inc(s["at_done"], 1)
                copied = counted(pool, j + 1)
                for u in range(SUB):
                    pool.wait_ge(C.rows_stored, 16 * B)
                    if u == 0:
                        pool.wait_ge(s["at_done"], copied)
                    pool.indirect_dma_start(out=xg[:, v, u, :], out_offset=None, in_=xn_dram[:, :],
                                            in_offset=bass.IndirectOffsetOnAxis(ap=at_now[:, v, u:u + 1].bitcast(U32), axis=0)
                                            ).then_inc(gathered[v][u], 16)

            run(pool, step)

        @block.tensor
        def _(pe):
            def turn_x(j, v, n):
                wait(pe, s["xlo_done"], j - 1)
                for u in range(SUB):
                    pe.wait_ge(gathered[v][u], 16 * (n + 1))
                    for k in range(KD):
                        mm = pe.transpose(ps_x[:, v, k * SLOT_T + u * P:k * SLOT_T + (u + 1) * P],
                                          xg[:, v, u, k * P:(k + 1) * P], C.ident[:, :])
                mm.then_inc(s["turned_x"], 1)

            def first(j, v):
                pe.wait_ge(s["w1_now_done"], j + 1)
                pe.wait_ge(s["xhi_done"], j + 1)
                pe.wait_ge(s["xlo_done"], j + 1)
                for i in range(HB):
                    wait(pe, s["gelu_done"], HB * (j - 1) + i + 1)
                    for f in (2 * i, 2 * i + 1):
                        parts = [(k, hl, xx) for k in range(KD) for hl, xx in ((0, xhi), (0, xlo), (1, xhi))]
                        for q, (k, hl, xx) in enumerate(parts):
                            mm = pe.matmul(ps_h[:, i, f % 2 * SLOT_T:(f % 2 + 1) * SLOT_T],
                                           w1_now[:, v, k, hl, f * P:(f + 1) * P], xx[:, k, :],
                                           start=(q == 0), stop=(q == len(parts) - 1))
                    mm.then_inc(s["h_done"], 1)

            def second(j, v, e):
                for u in range(SUB):
                    wait(pe, s["y_sum"], SUB * (j - 1) + u + 1)
                    slots = slice(u * P, (u + 1) * P)
                    for f in range(FCH):
                        if u == 0 and f % 2 == 0:
                            pe.wait_ge(s["hhi_done"], HB * j + f // 2 + 1)
                        pe.matmul(ps_y[:, u, :], hhi[:, v, f, slots],
                                  w2s[:, bass.ds(e * FCH + f, 1), 0:2 * D].rearrange("p o f -> p (o f)"),
                                  start=(f == 0), stop=False)
                    for f in range(FCH):
                        if u == 0 and f % 2 == 0:
                            pe.wait_ge(s["hlo_done"], HB * j + f // 2 + 1)
                        mm = pe.matmul(ps_y[:, u, 0:D], hlo[:, v, f, slots],
                                       w2s[:, bass.ds(e * FCH + f, 1), 0:D].rearrange("p o f -> p (o f)"),
                                       start=False, stop=(f == FCH - 1))
                    mm.then_inc(s["y_done"], 1)

            pe.wait_ge(s["bias_in"], 32)
            pe.transpose(ps_y[:, 0, 0:E * FCH], b1_rows[:, :], C.ident[0:E * FCH, 0:E * FCH]).then_inc(s["b1_turned"], 1)
            pe.wait_ge(s["b1_done"], 1)

            def step(j, v, n):
                if isinstance(j, int) and j == 0:
                    turn_x(0, 0, 0)
                if has(j):
                    first(j, v)
                if has(j + 1):
                    turn_x(j + 1, 1 - v, n + v)
                if has(j - 1):
                    second(j - 1, 1 - v, pe.value_load(C.expert[0:1, bass.ds(j - 1, 1)], min_val=0, max_val=E - 1))

            run(pe, step)

        @block.scalar
        def _(act):
            act.wait_ge(s["b1_turned"], 1)
            act.activation(b1T[:, :, :].rearrange("p e c -> p (e c)"), ps_y[:, 0, 0:E * FCH], ACT.Copy).then_inc(s["b1_done"], 1)

            def high_x(j, v):
                act.wait_ge(s["turned_x"], j + 1)
                wait(act, s["h_done"], HB * j)
                act.activation(xhi[:, :, :].rearrange("p k t -> p (k t)"), ps_x[:, v, :], ACT.Copy).then_inc(s["xhi_done"], 1)

            def step(j, v, n):
                if isinstance(j, int) and j == 0:
                    high_x(0, 0)
                if has(j):
                    act.wait_ge(s["b1_now_done"], j + 1)
                    wait(act, s["y_done"], SUB * (j - 1))
                    for i in range(HB):
                        act.wait_ge(s["h_done"], HB * j + i + 1)
                        wait(act, s["hlo_done"], HB * (j - 1) + i + 1)
                        for f in (2 * i, 2 * i + 1):
                            ins = act.activation(h[:, f, :], ps_h[:, i, f % 2 * SLOT_T:(f % 2 + 1) * SLOT_T],
                                                 ACT.Gelu_apprx_tanh, bias=b1_now[:, v, f:f + 1])
                        ins.then_inc(s["gelu_done"], 1)
                        act.wait_ge(s["gelu_done"], HB * j + i + 1)
                        act.activation(hhi[:, v, 2 * i:2 * i + 2, :].rearrange("p f t -> p (f t)"),
                                       h[:, 2 * i:2 * i + 2, :].rearrange("p f t -> p (f t)"),
                                       ACT.Copy).then_inc(s["hhi_done"], 1)
                if has(j + 1):
                    high_x(j + 1, 1 - v)

            run(act, step)

        @block.vector
        def _(dve):
            def weights(j, v, e):
                wait(dve, s["h_done"], HB * (j - 1))
                dve.tensor_copy(w1_now[:, v, :, :, :].rearrange("p k c f -> p (k c f)"),
                                w1s[:, bass.ds(e * KD, KD), :, :].rearrange("p k c f -> p (k c f)")).then_inc(s["w1_now_done"], 1)
                wait(dve, s["gelu_done"], HB * (j - 1))
                dve.tensor_copy(b1_now[:, v, :], b1T[:, bass.ds(e, 1), :].rearrange("p o f -> p (o f)")
                                ).then_inc(s["b1_now_done"], 1)

            def low_x(j, v):
                dve.wait_ge(s["xhi_done"], j + 1)
                wait(dve, s["h_done"], HB * j)
                dve.tensor_tensor(xlo[:, :, :].rearrange("p k t -> p (k t)"), ps_x[:, v, :],
                                  xhi[:, :, :].rearrange("p k t -> p (k t)"), ALU.subtract).then_inc(s["xlo_done"], 1)

            def expert(j):
                return dve.value_load(C.expert[0:1, bass.ds(j, 1)], min_val=0, max_val=E - 1)

            def step(j, v, n):
                if isinstance(j, int) and j == 0:
                    dve.wait_ge(s["b1_done"], 1)
                    weights(0, 0, expert(0))
                    low_x(0, 0)
                if has(j + 1):
                    weights(j + 1, 1 - v, expert(j + 1))
                if has(j):
                    for i in range(HB):
                        dve.wait_ge(s["hhi_done"], HB * j + i + 1)
                        if i == 0:
                            wait(dve, s["y_done"], SUB * (j - 1))
                        dve.tensor_tensor(hlo[:, v, 2 * i:2 * i + 2, :].rearrange("p f t -> p (f t)"),
                                          h[:, 2 * i:2 * i + 2, :].rearrange("p f t -> p (f t)"),
                                          hhi[:, v, 2 * i:2 * i + 2, :].rearrange("p f t -> p (f t)"),
                                          ALU.subtract).then_inc(s["hlo_done"], 1)
                if has(j + 1):
                    low_x(j + 1, 1 - v)
                if has(j - 1):
                    e = expert(j - 1)
                    for u in range(SUB):
                        dve.wait_ge(s["y_done"], SUB * (j - 1) + u + 1)
                        dve.tensor_tensor(yb[:, u, :], ps_y[:, u, D:2 * D],
                                          b2_all[:, bass.ds(e, 1), :].rearrange("p o d -> p (o d)"),
                                          ALU.add).then_inc(s["y_low"], 1)
                        dve.wait_ge(s["y_low"], SUB * (j - 1) + u + 1)
                        if has(j - 2):
                            dve.wait_ge(stored[u], 16 * (j - 1))
                        dve.tensor_tensor(y[:, u, :], ps_y[:, u, 0:D], yb[:, u, :], ALU.add).then_inc(s["y_sum"], 1)

            run(dve, step)


def fold(nc, C, w, w_in, w_out, b_in):
    hpg = 2
    ng = HEADS // hpg
    dh = P // hpg
    with ExitStack() as ctx:
        m = Mem(nc, ctx, C.sems, "fold")
        wq, wi = (C.xn4[:, 8 * i:8 * i + 8, :].rearrange("p (k n) d -> p k (n d)", k=KD) for i in range(2))
        wiT, w_of = (C.xn4[:, 8 * i:8 * i + 8, :] for i in range(2, 4))
        wqT = m.sb("wqT", [P, ng, D])
        wk = m.sb("wk", [P, 2, ng * P])
        wv = m.sb("wv", [P, 2, ng * P])
        wo = m.sb("wo", [P, ng, D])
        head_mask = m.sb("head_mask", [P, hpg])
        kblk = m.sb("kblk", [P, B, ng, hpg * KEYS])
        values = m.sb("values", [P, ng, B * KEYS])
        vblk = m.sb("vblk", [P, 2, RCH * P])
        amax = m.sb("amax", [P, 2, FCH])
        inv = m.sb("inv", [P, 2, FCH])
        scale = m.sb("scale", [P, 2, FCH])
        NB = 8
        ps = m.ps("ps", [P, NB, 512])
        wq_in, wkv_in, wo_in, wi_in, w_of_in, b_in_in = (
            m.sem(n) for n in ("wq_in", "wkv_in", "wo_in", "wi_in", "w_of_in", "b_in_in"))
        names = ("mask_step", "zeroed", "filled", "emptied", "high_done", "low_done", "vblk_done", "step", "wi_done", "wo_done")
        s = {n: m.sem(n) for n in names}
        filled, emptied, high_done, low_done = s["filled"], s["emptied"], s["high_done"], s["low_done"]
        block = ctx.enter_context(nc.Block())

        TURN0 = 0
        K0 = TURN0 + ng // 2
        V0 = K0 + ng
        WI0 = V0 + ng
        B0 = WI0 + FCH // 2
        KF, VF = KD * len(SB), RCH // 2
        END0 = B0 + B * (KF + VF)

        @block.sync
        def _(sp):
            sp.dma_start(wq[:, :, :], w["wq"].rearrange("(k p) n -> p k n", p=P)).then_inc(wq_in, 16)
            for dst, name in ((wk, "wk"), (wv, "wv")):
                for k, (at, n) in enumerate(CTX_K):
                    sp.dma_start(dst[0:n, k, :], w[name][at:at + n, :]).then_inc(wkv_in, 16)
            sp.dma_start(w_of[:, :, :], w_out.rearrange("(f p) d -> p f d", p=P)).then_inc(w_of_in, 16)
            sp.dma_start(wi[:, :, :], w_in.rearrange("(k p) f -> p k f", p=P)).then_inc(wi_in, 16)
            sp.dma_start(wo[:, :, :], w["wo"].rearrange("(g p) n -> p g n", p=P)).then_inc(wo_in, 16)
            with nc.allow_non_contiguous_dma(reason="a short bias, one element to a partition"):
                sp.dma_start(C.b_in[:, :], b_in.rearrange("(f p) -> p f", p=P)).then_inc(b_in_in, 16)
            sp.wait_ge(b_in_in, 16)

        @block.gpsimd
        def _(pool):
            pool.memset(head_mask[:, :], 1.0).then_inc(s["mask_step"], 1)
            pool.wait_ge(s["mask_step"], 1)
            pool.affine_select(out=head_mask[:, :], in_=head_mask[:, :], compare_op=ALU.is_ge, fill=0.0, base=0,
                               pattern=[[-dh, hpg]], channel_multiplier=1).then_inc(s["mask_step"], 1)
            pool.wait_ge(s["mask_step"], 2)
            pool.affine_select(out=head_mask[:, :], in_=head_mask[:, :], compare_op=ALU.is_ge, fill=0.0, base=dh - 1,
                               pattern=[[dh, hpg]], channel_multiplier=-1).then_inc(s["mask_step"], 1)

        @block.tensor
        def _(pe):
            def bank(fill):
                if NB <= fill < B0 + NB:
                    pe.wait_ge(emptied, fill - NB + 1)
                elif fill >= B0 + NB:
                    pe.wait_ge(low_done, fill - NB - B0 + 1)
                return fill % NB

            def turn(first, source):
                for i in range(ng // 2):
                    at = bank(first + i)
                    for j in range(2 * KD):
                        g, k = 2 * i + j // KD, j % KD
                        mm = pe.transpose(ps[:, at, j * P:(j + 1) * P], source[:, k, g * P:(g + 1) * P], C.ident[:, :])
                    mm.then_inc(filled, 1)

            pe.wait_ge(wq_in, 16)
            turn(TURN0, wq)
            pe.wait_ge(wkv_in, 16 * 4)
            for first, weights in ((K0, wk), (V0, wv)):
                for g in range(ng):
                    at = bank(first + g)
                    for k, (_, n) in enumerate(CTX_K):
                        mm = pe.matmul(ps[:, at, 0:B * KEYS], weights[0:n, k, g * P:(g + 1) * P],
                                       C.ctxT[0:n, k, :, :], start=(k == 0), stop=(k == 1))
                    mm.then_inc(filled, 1)
            pe.wait_ge(wi_in, 16)
            turn(WI0, wi)
            pe.wait_ge(wo_in, 16)
            for b in range(B):
                fill = B0 + b * (KF + VF)
                pe.wait_ge(emptied, K0 + ng)
                for k in range(KD):
                    for h0, h1 in SB:
                        at = bank(fill)
                        for g in range(h0 // hpg, h1 // hpg):
                            mm = pe.matmul(ps[:, at, (g * hpg - h0) * KEYS:(g * hpg + hpg - h0) * KEYS],
                                           wqT[:, g, k * P:(k + 1) * P], kblk[:, b, g, :], start=True, stop=True)
                        mm.then_inc(filled, 1)
                        fill += 1
                pe.wait_ge(s["vblk_done"], b + 1)
                for i in range(VF):
                    at = bank(fill)
                    for c in (2 * i, 2 * i + 1):
                        mine = [g for cc, g in blocks_of(hpg) if cc == c]
                        for g in mine:
                            mm = pe.matmul(ps[:, at, c % 2 * D:(c % 2 + 1) * D], vblk[:, g % 2, c * P:(c + 1) * P],
                                           wo[:, g, :], start=(g == mine[0]), stop=(g == mine[-1]))
                    mm.then_inc(filled, 1)
                    fill += 1
            pe.wait_ge(s["wi_done"], 1)
            for k in range(KD):
                for j in range(FCH // 4):
                    at = bank(END0 + k * FCH // 4 + j)
                    for f in range(4 * j, 4 * j + 4):
                        mm = pe.transpose(ps[:, at, f % 4 * P:(f % 4 + 1) * P], wiT[:, f, k * P:(k + 1) * P], C.ident[:, :])
                    mm.then_inc(filled, 1)

        @block.scalar
        def _(act):
            def block_values(b):
                for odd in range(2):
                    for h in range(hpg):
                        ins = act.activation(
                            vblk[:, odd, 0:ROWS].rearrange("p (g o h k) -> p g o h k", o=2, h=hpg,
                                                           k=KEYS)[:, :, odd, h, :],
                            values.rearrange("p (g o) (b k) -> p g o b k", o=2, b=B)[:, :, odd, b, :],
                            ACT.Identity, scale=head_mask[:, h:h + 1])
                ins.then_inc(s["vblk_done"], 1)

            def copy_turned(first, dst):
                for i in range(ng // 2):
                    act.wait_ge(filled, first + i + 1)
                    act.activation(dst[:, 2 * i:2 * i + 2, :].rearrange("p g d -> p (g d)"), ps[:, (first + i) % NB, :],
                                   ACT.Copy).then_inc(emptied, 1)

            copy_turned(TURN0, wqT)
            act.wait_ge(s["mask_step"], 3)
            for g in range(ng):
                act.wait_ge(filled, K0 + g + 1)
                for h in range(hpg):
                    ins = act.activation(kblk[:, :, g, h * KEYS:(h + 1) * KEYS],
                                         ps[:, (K0 + g) % NB, 0:B * KEYS].rearrange("p (b k) -> p b k", b=B),
                                         ACT.Identity, scale=head_mask[:, h:h + 1])
                ins.then_inc(emptied, 1)
            for g in range(ng):
                act.wait_ge(filled, V0 + g + 1)
                act.activation(values[:, g, :], ps[:, (V0 + g) % NB, 0:B * KEYS], ACT.Copy).then_inc(emptied, 1)
            copy_turned(WI0, wiT)
            act.wait_ge(s["zeroed"], 1)
            act.wait_ge(emptied, WI0)
            block_values(0)
            for b in range(B):
                fill = B0 + b * (KF + VF)
                for k in range(KD):
                    for h0, h1 in SB:
                        act.wait_ge(filled, fill + 1)
                        act.activation(C.k_fold[:, b, k, 0, h0 * KEYS:h1 * KEYS], ps[:, fill % NB, 0:(h1 - h0) * KEYS],
                                       ACT.Copy).then_inc(high_done, 1)
                        fill += 1
                for i in range(VF):
                    act.wait_ge(filled, fill + 1)
                    act.activation(C.v_fold[:, b, 0, 2 * i:2 * i + 2, :].rearrange("p c d -> p (c d)"), ps[:, fill % NB, :],
                                   ACT.Copy).then_inc(high_done, 1)
                    fill += 1
                if b + 1 < B:
                    block_values(b + 1)
            for k in range(KD):
                for j in range(FCH // 4):
                    fill = END0 + k * FCH // 4 + j
                    act.wait_ge(filled, fill + 1)
                    act.activation(C.wi_q[:, k, j * 512:(j + 1) * 512], ps[:, fill % NB, :], ACT.Copy)

        @block.vector
        def _(dve):
            steps = [0]

            def link(ins):
                steps[0] += 1
                ins.then_inc(s["step"], 1)
                dve.wait_ge(s["step"], steps[0])

            def quantise(wt, i, f0, f1, out):
                c = slice(f0, f1)
                link(dve.tensor_reduce(amax[:, i, c], wt[:, c, :], AX, ALU.max, apply_absolute_value=True))
                link(dve.tensor_scalar(amax[:, i, c], amax[:, i, c], 1e-8, None, ALU.max))
                link(dve.reciprocal(inv[:, i, c], amax[:, i, c]))
                link(dve.tensor_scalar(scale[:, i, c], inv[:, i, c], 127.0, None, ALU.mult))
                for f in range(f0, f1):
                    ins = dve.tensor_scalar(wt[:, f, :], wt[:, f, :], scale[:, i, f:f + 1], MAGIC, ALU.mult, ALU.add)
                link(ins)
                link(dve.tensor_scalar(wt[:, c, :], wt[:, c, :], MAGIC, 127.0, ALU.subtract, ALU.min))
                return dve.tensor_scalar(out[:, c, :], wt[:, c, :], -128.0, None, ALU.max)

            dve.memset(vblk[:, :, :], 0.0).then_inc(s["zeroed"], 1)
            dve.wait_ge(w_of_in, 16)
            quantise(w_of, 1, 0, FCH, C.wo_q).then_inc(s["wo_done"], 1)
            dve.reciprocal(C.wo_step[:, :], scale[:, 1, :]).then_inc(s["wo_done"], 1)
            fill = B0
            for b in range(B):
                def low(out, ps_in):
                    dve.wait_ge(high_done, fill - B0 + 1)
                    dve.tensor_tensor(out[1], ps_in, out[0], ALU.subtract).then_inc(low_done, 1)

                for k in range(KD):
                    for h0, h1 in SB:
                        c = slice(h0 * KEYS, h1 * KEYS)
                        low([C.k_fold[:, b, k, hl, c] for hl in range(2)], ps[:, fill % NB, 0:(h1 - h0) * KEYS])
                        fill += 1
                for i in range(VF):
                    low([C.v_fold[:, b, hl, 2 * i:2 * i + 2, :].rearrange("p c d -> p (c d)") for hl in range(2)],
                        ps[:, fill % NB, :])
                    fill += 1
                if 3 * b < FCH:
                    if b == 0:
                        dve.wait_ge(emptied, B0)
                    ins = quantise(wiT, 0, 3 * b, min(FCH, 3 * b + 3), wiT)
                    if 3 * b + 3 >= FCH:
                        ins.then_inc(s["wi_done"], 1)
                        dve.reciprocal(C.wi_step[:, :], scale[:, 0, :])


def folded_attention(nc, C, x1_dram, y_dram, x_out, bo, gate_col, scale):
    RING, GR, LAST, AHEAD = 8, 4, 4, 4
    NSB = len(SB)
    with ExitStack() as ctx:
        m = Mem(nc, ctx, C.sems, "a1")
        k_now = m.sb("k_now", [P, KD, 2, ROWS], BF16)
        v_now = m.sb("v_now", [P, 2, RCH, D], BF16)
        gbo = m.sb("gbo", [P, D])
        x = m.sb("x", [P, RING, D])
        at_now = m.sb("at_now", [P, GR, TOPK], I32)
        yg = m.sb("yg", [P, GR, TOPK, D])
        stats = m.sb("stats", [P, 2, 6])
        mv = m.sb("mv", [P, 2, 2])
        veps = m.sb("veps", [P, 2])
        rstd = m.sb("rstd", [P, 2])
        stats_o = m.sb("stats_o", [P, 2, 6])
        mv_o = m.sb("mv_o", [P, 2, 2])
        veps_o = m.sb("veps_o", [P, 2])
        rstd_o = m.sb("rstd_o", [P, 2])
        xn = m.sb("xn", [P, 2, D])
        xhi = m.sb("xhi", [P, 2, KD, P], BF16)
        xlo = m.sb("xlo", [P, 2, KD, P], BF16)
        mx = m.sb("mx", [P, HEADS])
        nmx = m.sb("nmx", [P, HEADS])
        z = m.sb("z", [P, 2, ROWS])
        ssum = m.sb("ssum", [P, 2, HEADS])
        rsum = m.sb("rsum", [P, 2, HEADS])
        phi = m.sb("phi", [P, RCH, P], BF16)
        plo = m.sb("plo", [P, RCH, P], BF16)
        xo = m.sb("xo", [P, 2, D])
        ps_sc = m.ps("ps_sc", [P, NSB, 512])
        ps_x = m.ps("ps_x", [P, 512])
        ps_p = m.ps("ps_p", [P, 3, 512])
        ps_o = m.ps("ps_o", [P, 512])
        bias_in, gbo_done = m.sem("bias_in"), m.sem("gbo_done")
        x_loaded = [m.sem(f"x_loaded{i}") for i in range(RING)]
        gathered = [[m.sem(f"gathered{r}_{c}") for c in range(TOPK)] for r in range(GR)]
        x_stored = [m.sem(f"x_stored{i}") for i in range(2)]
        names = ("at_done", "half_done", "x2_done", "stats_done", "mean_done", "veps_done", "rstd_done", "xn_done", "turned_x",
                 "xhi_done", "xlo_done", "k_now_done", "v_now_done", "scores_done", "max_done", "nmx_done", "exp_done",
                 "rsum_done", "norm_done", "turned_p", "phi_done", "plo_done", "o_done", "xo_done", "xb_done",
                 "ostats_done", "omean_done", "oveps_done", "orstd_done", "xn_out", "amax_done")
        s = {n: m.sem(n) for n in names}
        full = [(0, 0, 4, P), (1, 4, 8, P), (2, 8, RCH - 1, P), (2, RCH - 1, RCH, ROWS - (RCH - 1) * P)]
        block = ctx.enter_context(nc.Block())

        def run(eng, slot):
            for t in range(TPB + LAST):
                slot(t, t % TPB, t // TPB)
            with eng.Fori(1, B - 1) as b:
                for t in range(LAST, TPB + LAST):
                    slot(b * TPB + t, t % TPB, b + t // TPB)
            for t in range(LAST, TPB + LAST):
                slot((B - 1) * TPB + t, t % TPB, B - 1 + t // TPB)

        def has(T):
            return not isinstance(T, int) or 0 <= T < TILES

        @block.sync
        def _(sp):
            def load(T, r):
                sp.dma_start(x[:, r, :], x1_dram[bass.ds(T * P, P), :]).then_inc(x_loaded[r], 16)

            for r in range(2):
                load(r, r)
            sp.dma_start(gbo[:, :], bo.partition_broadcast(P)).then_inc(bias_in, 16)
            for r in range(2, AHEAD):
                load(r, r)

            def slot(T, t, b):
                if has(T - 3):
                    sp.wait_ge(s["xo_done"], T - 2)
                    sp.dma_start(x_out[bass.ds((T - 3) * P, P), :], xo[:, (t - 3) % 2, :]).then_inc(x_stored[(t - 3) % 2], 16)
                if has(T + AHEAD):
                    load(T + AHEAD, (t + AHEAD) % RING)

            run(sp, slot)
            for i in range(2):
                sp.wait_ge(x_stored[i], 16 * TILES // 2)

        @block.gpsimd
        def _(pool):
            def power(T, u):
                pool.wait_ge(s["veps_done"], T + 1)
                pool.tensor_tensor(rstd[:, u:u + 1], veps[:, u:u + 1], C.half[:, 0:1], ALU.pow).then_inc(s["rstd_done"], 1)

            def gather(T, r, turn):
                if has(T - GR):
                    pool.wait_ge(s["x2_done"], T - GR + 1)
                    for c in range(TOPK):
                        pool.wait_ge(gathered[r][c], 16 * turn)
                pool.tensor_copy(at_now[:, r, :].unsqueeze(2), C.slots[:, :, bass.ds(T, 1)]).then_inc(s["at_done"], 1)
                copied = counted(pool, T + 1)
                for c in range(TOPK):
                    pool.wait_ge(C.slots_stored[c], 16 * NST)
                    if c == 0:
                        pool.wait_ge(s["at_done"], copied)
                    pool.indirect_dma_start(out=yg[:, r, c, :], out_offset=None, in_=y_dram[:, :],
                                            in_offset=bass.IndirectOffsetOnAxis(ap=at_now[:, r, c:c + 1].bitcast(U32), axis=0)
                                            ).then_inc(gathered[r][c], 16)

            pool.wait_ge(bias_in, 16)
            pool.tensor_scalar(gbo[:, :], gbo[:, :], C.gate[:, gate_col:gate_col + 1], None, ALU.mult).then_inc(gbo_done, 1)
            for T in range(3):
                gather(T, T, 0)
            power(0, 0)
            power(1, 1)

            def slot(T, t, b):
                if has(T - 1):
                    w = (t - 1) % 2
                    pool.wait_ge(s["rsum_done"], T)
                    zt = z[:, w, :].rearrange("p (h k) -> p h k", k=KEYS)
                    pool.tensor_tensor(zt, zt, rsum[:, w, :].unsqueeze(2).broadcast_to((P, HEADS, KEYS)),
                                       ALU.mult).then_inc(s["norm_done"], 1)
                if has(T):
                    pool.wait_ge(s["xn_done"], T + 1)
                    pool.tensor_tensor(x[:, t, :], x[:, t, :], gbo[:, :], ALU.add).then_inc(s["xb_done"], 1)
                if has(T + 3):
                    gather(T + 3, (t + 3) % GR, b * (TPB // GR) + (t + 3) // GR)
                if has(T - 3):
                    pool.wait_ge(s["oveps_done"], T - 2)
                    v = (t - 3) % 2
                    pool.tensor_tensor(rstd_o[:, v:v + 1], veps_o[:, v:v + 1], C.half[:, 0:1],
                                       ALU.pow).then_inc(s["orstd_done"], 1)
                if has(T + 2):
                    power(T + 2, t % 2)

            run(pool, slot)

        @block.tensor
        def _(pe):
            def turn_x(T, u):
                pe.wait_ge(s["xn_done"], T + 1)
                wait(pe, s["xlo_done"], T)
                for k in range(KD):
                    mm = pe.transpose(ps_x[:, k * P:(k + 1) * P], xn[:, u, k * P:(k + 1) * P], C.ident[:, :])
                mm.then_inc(s["turned_x"], 1)

            turn_x(0, 0)

            def slot(T, t, b):
                u = t % 2
                if has(T - 2):
                    pe.wait_ge(s["norm_done"], T - 1)
                    for j, c0, c1, n in full:
                        if c0 < RCH - 1:
                            wait(pe, s["plo_done"], 3 * (T - 3) + j + 1)
                        for c in range(c0, c1):
                            mm = pe.transpose(ps_p[0:n, j, c % 4 * P:(c % 4 + 1) * P], z[:, u, c * P:c * P + n],
                                              C.ident[:, :])
                        if c1 != RCH - 1:
                            mm.then_inc(s["turned_p"], 1)
                if has(T):
                    if t == 0:
                        pe.wait_ge(s["k_now_done"], b + 1)
                    pe.wait_ge(s["xlo_done"], T + 1)
                    for j, (h0, h1) in enumerate(SB):
                        wait(pe, s["exp_done"], NSB * (T - 1) + j + 1)
                        n = (h1 - h0) * KEYS
                        parts = [(xx, k, hl) for k in range(KD) for xx, hl in ((xhi, 0), (xhi, 1), (xlo, 0))]
                        for i, (xx, k, hl) in enumerate(parts):
                            mm = pe.matmul(ps_sc[:, j, 0:n], xx[:, u, k, :], k_now[:, k, hl, h0 * KEYS:h1 * KEYS],
                                           start=(i == 0), stop=(i == len(parts) - 1))
                        mm.then_inc(s["scores_done"], 1)
                if has(T + 1):
                    turn_x(T + 1, (t + 1) % 2)
                if has(T - 2):
                    if t == 2:
                        pe.wait_ge(s["v_now_done"], b + 1)
                    wait(pe, s["xo_done"], T - 2)
                    for j, c0, c1, n in full:
                        if c0 < RCH - 1:
                            pe.wait_ge(s["plo_done"], 3 * (T - 2) + j + 1)
                        for c in range(c0, c1):
                            for pp, hl in ((phi, 0), (phi, 1), (plo, 0)):
                                last = c == RCH - 1 and pp is plo
                                mm = pe.matmul(ps_o[:, 0:D], pp[0:n, c, :], v_now[0:n, hl, c, :],
                                               start=(c == 0 and pp is phi and hl == 0), stop=last)
                    mm.then_inc(s["o_done"], 1)

            run(pe, slot)

        @block.scalar
        def _(act):
            def high_x(T, u):
                act.wait_ge(s["turned_x"], T + 1)
                wait(act, s["scores_done"], NSB * (T - 1))
                act.activation(xhi[:, u, :, :].rearrange("p k t -> p (k t)"), ps_x[:, 0:D],
                               ACT.Copy).then_inc(s["xhi_done"], 1)

            high_x(0, 0)

            def slot(T, t, b):
                u = t % 2
                if has(T - 2):
                    wait(act, s["o_done"], T - 2)
                    for j, c0, c1, n in full:
                        if c0 < RCH - 1:
                            act.wait_ge(s["turned_p"], 3 * (T - 2) + j + 1)
                        ins = act.activation(phi[0:n, c0:c1, :].rearrange("p c t -> p (c t)"),
                                             ps_p[0:n, j, c0 % 4 * P:(c0 % 4 + c1 - c0) * P], ACT.Copy)
                        if c1 != RCH - 1:
                            ins.then_inc(s["phi_done"], 1)
                def exponentials(j):
                    act.wait_ge(s["nmx_done"], NSB * T + j + 1)
                    if j == 0:
                        wait(act, s["rsum_done"], T - 1)
                    for h in range(*SB[j]):
                        ins = act.activation(z[:, u, h * KEYS:(h + 1) * KEYS],
                                             ps_sc[:, j, (h - SB[j][0]) * KEYS:(h - SB[j][0] + 1) * KEYS], ACT.Exp,
                                             bias=nmx[:, h:h + 1], scale=scale, accum_out=ssum[:, u, h:h + 1])
                    ins.then_inc(s["exp_done"], 1)

                if has(T):
                    exponentials(0)
                if has(T + 1):
                    high_x(T + 1, (t + 1) % 2)
                if has(T):
                    exponentials(1)
                    exponentials(2)

            run(act, slot)

        @block.vector
        def _(dve):
            def x2_first(T, r, turn):
                dve.wait_ge(x_loaded[r], 16 * (turn + 1))
                g = r % GR
                for c in range(TOPK):
                    dve.wait_ge(gathered[g][c], 16 * (turn * (RING // GR) + r // GR + 1))
                dve.scalar_tensor_tensor(out=x[:, r, :], in0=yg[:, g, 0, :], scalar=C.top[:, 0, bass.ds(T, 1)],
                                         in1=x[:, r, :], op0=ALU.mult, op1=ALU.add).then_inc(s["half_done"], 1)

            def x2_second(T, r):
                dve.wait_ge(s["half_done"], T + 1)
                dve.scalar_tensor_tensor(out=x[:, r, :], in0=yg[:, r % GR, 1, :], scalar=C.top[:, 1, bass.ds(T, 1)],
                                         in1=x[:, r, :], op0=ALU.mult, op1=ALU.add).then_inc(s["x2_done"], 1)

            def ln_stats(T, u, r):
                dve.wait_ge(s["x2_done"], T + 1)
                dve.bn_stats(stats[:, u, :], x[:, r, :]).then_inc(s["stats_done"], 1)
                dve.wait_ge(s["stats_done"], T + 1)

            def ln_mean(T, u):
                dve.bn_aggr(mv[:, u, :], stats[:, u, :]).then_inc(s["mean_done"], 1)
                dve.wait_ge(s["mean_done"], T + 1)
                dve.tensor_scalar(veps[:, u:u + 1], mv[:, u, 1:2], EPS, None, ALU.add).then_inc(s["veps_done"], 1)

            def ln(T, u, r):
                dve.wait_ge(s["rstd_done"], T + 1)
                wait(dve, s["turned_x"], T - 1)
                dve.tensor_scalar(xn[:, u, :], x[:, r, :], mv[:, u, 0:1], rstd[:, u:u + 1], ALU.subtract,
                                  ALU.mult).then_inc(s["xn_done"], 1)

            def low_x(T, u):
                dve.wait_ge(s["xhi_done"], T + 1)
                dve.tensor_tensor(xlo[:, u, :, :].rearrange("p k t -> p (k t)"), ps_x[:, 0:D],
                                  xhi[:, u, :, :].rearrange("p k t -> p (k t)"), ALU.subtract).then_inc(s["xlo_done"], 1)

            def keys(T, b):
                wait(dve, s["scores_done"], NSB * T)
                dve.tensor_copy(k_now[:, :, :, :].rearrange("p k c n -> p (k c n)"),
                                C.k_fold[:, bass.ds(b, 1), :, :, :].rearrange("p o k c n -> p (o k c n)")
                                ).then_inc(s["k_now_done"], 1)

            def values(T, b):
                wait(dve, s["o_done"], T)
                dve.tensor_copy(v_now[:, :, :, :].rearrange("p h c d -> p (h c d)"),
                                C.v_fold[:, bass.ds(b, 1), :, :, :].rearrange("p o h c d -> p (o h c d)")
                                ).then_inc(s["v_now_done"], 1)

            for T in range(2):
                x2_first(T, T, 0)
                x2_second(T, T)
                ln_stats(T, T, T)
                ln_mean(T, T)
            ln(0, 0, 0)
            keys(0, 0)
            low_x(0, 0)

            def slot(T, t, b):
                u = t % 2
                v = (t - 3) % 2
                r2 = (t + 2) % RING
                if has(T - 3):
                    turn = b if t >= 3 else b - 1
                    dve.wait_ge(s["o_done"], T - 2)
                    dve.wait_ge(s["xb_done"], T - 2)
                    if has(T - 5):
                        dve.wait_ge(x_stored[v], 16 * (turn * (TPB // 2) + (t - 3) % TPB // 2))
                    dve.scalar_tensor_tensor(out=xo[:, v, :], in0=ps_o[:, 0:D], scalar=C.gate[:, gate_col:gate_col + 1],
                                             in1=x[:, (t - 3) % RING, :], op0=ALU.mult,
                                             op1=ALU.add).then_inc(s["xo_done"], 1)
                if has(T - 1):
                    w = (t - 1) % 2
                    dve.wait_ge(s["exp_done"], NSB * T)
                    if has(T - 3):
                        dve.wait_ge(s["norm_done"], T - 2)
                    dve.reciprocal(rsum[:, w, :], ssum[:, w, :]).then_inc(s["rsum_done"], 1)
                if t == 2 and has(T):
                    values(T - 2, b)
                if has(T - 3):
                    dve.wait_ge(s["xo_done"], T - 2)
                    dve.bn_stats(stats_o[:, v, :], xo[:, v, :]).then_inc(s["ostats_done"], 1)
                if has(T + 1):
                    ln(T + 1, (t + 1) % 2, (t + 1) % RING)
                if has(T - 2):
                    wait(dve, s["o_done"], T - 2)
                for bank, (h0, h1) in enumerate(SB):
                    if has(T - 2):
                        for j, c0, c1, n in full:
                            if j == bank:
                                if c0 < RCH - 1:
                                    dve.wait_ge(s["phi_done"], 3 * (T - 2) + j + 1)
                                ins = dve.tensor_tensor(plo[0:n, c0:c1, :].rearrange("p c t -> p (c t)"),
                                                        ps_p[0:n, j, c0 % 4 * P:(c0 % 4 + c1 - c0) * P],
                                                        phi[0:n, c0:c1, :].rearrange("p c t -> p (c t)"), ALU.subtract)
                        ins.then_inc(s["plo_done"], 1)
                    if has(T):
                        dve.wait_ge(s["scores_done"], T * NSB + bank + 1)
                        dve.tensor_reduce(mx[:, h0:h1],
                                          ps_sc[:, bank, 0:(h1 - h0) * KEYS].rearrange("p (h k) -> p h k", k=KEYS), AX,
                                          ALU.max).then_inc(s["max_done"], 1)
                        dve.wait_ge(s["max_done"], T * NSB + bank + 1)
                        if bank == 0:
                            wait(dve, s["exp_done"], NSB * T)
                            if has(T - 3):
                                dve.wait_ge(s["ostats_done"], T - 2)
                        dve.tensor_scalar(nmx[:, h0:h1], mx[:, h0:h1], -scale, None, ALU.mult).then_inc(s["nmx_done"], 1)
                if t == TPB - 1 and has(T + 1):
                    keys(T + 1, b + 1)
                if has(T - 3):
                    if not has(T):
                        dve.wait_ge(s["ostats_done"], T - 2)
                    dve.bn_aggr(mv_o[:, v, :], stats_o[:, v, :]).then_inc(s["omean_done"], 1)
                if has(T + 2):
                    x2_first(T + 2, r2, b + (t + 2) // RING)
                if has(T - 3):
                    dve.wait_ge(s["omean_done"], T - 2)
                    dve.tensor_scalar(veps_o[:, v:v + 1], mv_o[:, v, 1:2], EPS, None, ALU.add).then_inc(s["oveps_done"], 1)
                if has(T + 1):
                    low_x(T + 1, (t + 1) % 2)
                if has(T + 2):
                    x2_second(T + 2, r2)
                    ln_stats(T + 2, u, r2)
                if has(T - 4):
                    w = (t - 4) % 2
                    dve.wait_ge(s["orstd_done"], T - 3)
                    dve.tensor_scalar(C.xn4[:, bass.ds(T - 4, 1), :].rearrange("p o d -> p (o d)"), xo[:, w, :],
                                      mv_o[:, w, 0:1], rstd_o[:, w:w + 1], ALU.subtract, ALU.mult).then_inc(s["xn_out"], 1)
                if has(T + 2):
                    ln_mean(T + 2, u)
                if has(T - 4):
                    dve.wait_ge(s["xn_out"], T - 3)
                    dve.tensor_reduce(C.xn4_max[:, bass.ds(T - 4, 1)],
                                      C.xn4[:, bass.ds(T - 4, 1), :].rearrange("p o d -> p (o d)"), AX, ALU.max,
                                      apply_absolute_value=True).then_inc(s["amax_done"], 1)

            run(dve, slot)




def ffn(nc, C, x3_dram, out_dram, b_out):
    G = 4
    NG = TILES // G
    GT = G * P
    with ExitStack() as octx:
        o = Mem(nc, octx, C.sems, "ffn")
        hid = o.sb("hid", [P, FCH, B * N])
        xhi = o.sb("xhi", [P, KD, B * N], BF16)
        xlo = o.sb("xlo", [P, KD, B * N], BF16)
        in_step = o.sb("in_step", [P, FCH])
        out_step = o.sb("out_step", [P, FCH])
        h_scale = o.sb("h_scale", [P, 2])

        def steps_of(dve, sem, count, amax_all, out, tmp):
            for ins in (lambda: dve.tensor_scalar(tmp[:, 0:1], amax_all[:, 0:1], 1e-8, None, ALU.max),
                        lambda: dve.reciprocal(tmp[:, 1:2], tmp[:, 0:1]),
                        lambda: dve.tensor_scalar(out[:, 0:1], tmp[:, 1:2], 32767.0, None, ALU.mult),
                        lambda: dve.reciprocal(out[:, 1:2], out[:, 0:1])):
                ins().then_inc(sem, 1)
                count += 1
                dve.wait_ge(sem, count)
            return count

        with ExitStack() as ctx:
            m = Mem(nc, ctx, C.sems, "f1")
            xn = C.xn4
            amax1 = m.sb("amax1", [P, 1])
            amax_all = m.sb("amax_all", [P, 1])
            tmp = m.sb("tmp", [P, 2])
            x_scale = m.sb("x_scale", [P, 2])
            ps = m.ps("ps", [P, 4, 512])
            names = ("amax_done", "all_done", "step", "scaled", "rounded", "turned", "hi_done", "lo_done")
            s = {n: m.sem(n) for n in names}
            PAIRS = TILES // 2
            block = ctx.enter_context(nc.Block())

            @block.gpsimd
            def _(pool):
                pool.wait_ge(s["amax_done"], 1)
                pool.partition_all_reduce(amax_all[:, :], amax1[:, :], P, RMAX).then_inc(s["all_done"], 1)

            @block.vector
            def _(dve):
                dve.tensor_reduce(amax1[:, :], C.xn4_max[:, :], AX, ALU.max).then_inc(s["amax_done"], 1)
                dve.wait_ge(s["all_done"], 1)
                steps_of(dve, s["step"], 0, amax_all, x_scale, tmp)
                dve.tensor_scalar(in_step[:, :], C.wi_step[:, :], x_scale[:, 1:2], None, ALU.mult)

                def scale(i):
                    dve.tensor_scalar(xn[:, 2 * i:2 * i + 2, :], xn[:, 2 * i:2 * i + 2, :], x_scale[:, 0:1], MAGIC, ALU.mult,
                                      ALU.add).then_inc(s["scaled"], 1)

                def round_off(i):
                    dve.wait_ge(s["scaled"], i + 1)
                    dve.tensor_scalar(xn[:, 2 * i:2 * i + 2, :], xn[:, 2 * i:2 * i + 2, :], MAGIC, None,
                                      ALU.subtract).then_inc(s["rounded"], 1)

                def low(i):
                    dve.wait_ge(s["hi_done"], i + 1)
                    c = slice(2 * i * P, (2 * i + 2) * P)
                    dve.tensor_tensor(xlo[:, :, c], ps[:, i % 4, :].rearrange("p (k t) -> p k t", k=KD), xhi[:, :, c],
                                      ALU.subtract).then_inc(s["lo_done"], 1)

                scale(0)
                for i in range(PAIRS):
                    if i + 1 < PAIRS:
                        scale(i + 1)
                    round_off(i)
                    if i >= 2:
                        low(i - 2)
                low(PAIRS - 2)
                low(PAIRS - 1)

            @block.tensor
            def _(pe):
                for i in range(PAIRS):
                    pe.wait_ge(s["rounded"], i + 1)
                    wait(pe, s["lo_done"], i - 3)
                    for k in range(KD):
                        for v in range(2):
                            mm = pe.transpose(ps[:, i % 4, (2 * k + v) * P:(2 * k + v + 1) * P],
                                              xn[:, 2 * i + v, k * P:(k + 1) * P], C.ident[:, :])
                    mm.then_inc(s["turned"], 1)

            @block.scalar
            def _(act):
                for i in range(PAIRS):
                    act.wait_ge(s["turned"], i + 1)
                    act.activation(xhi[:, :, 2 * i * P:(2 * i + 2) * P], ps[:, i % 4, :].rearrange("p (k t) -> p k t", k=KD),
                                   ACT.Copy).then_inc(s["hi_done"], 1)

        with ExitStack() as ctx:
            m = Mem(nc, ctx, C.sems, "f2")
            amax = m.sb("amax", [P, NG, FCH])
            amax1 = m.sb("amax1", [P, 1])
            amax_all = m.sb("amax_all", [P, 1])
            tmp = m.sb("tmp", [P, 2])
            R = 8
            ps = m.ps("ps", [P, R, 512])
            h_done, gelu_done, amax_done, all_done, step = (m.sem(n) for n in ("h_done", "gelu_done", "amax_done", "all_done", "step"))
            block = ctx.enter_context(nc.Block())

            @block.tensor
            def _(pe):
                def group(g):
                    for f in range(FCH):
                        if not isinstance(g, int):
                            pe.wait_ge(gelu_done, (g - 1) * FCH + f + 1)
                        part = [(k, xx) for k in range(KD) for xx in (xhi, xlo)]
                        for i, (k, xx) in enumerate(part):
                            mm = pe.matmul(ps[:, f, :], C.wi_q[:, k, f * P:(f + 1) * P], xx[:, k, bass.ds(g * 512, 512)],
                                           start=(i == 0), stop=(i == len(part) - 1))
                        mm.then_inc(h_done, 1)

                group(0)
                with pe.Fori(1, NG) as g:
                    group(g)

            @block.scalar
            def _(act):
                with act.Fori(0, NG) as g:
                    for f in range(FCH):
                        act.wait_ge(h_done, g * FCH + f + 1)
                        act.activation(hid[:, f, bass.ds(g * 512, 512)], ps[:, f, :], ACT.Gelu, bias=C.b_in[:, f:f + 1],
                                       scale=in_step[:, f:f + 1]).then_inc(gelu_done, 1)

            @block.vector
            def _(dve):
                with dve.Fori(0, NG) as g:
                    for f in range(FCH):
                        dve.wait_ge(gelu_done, g * FCH + f + 1)
                        dve.tensor_reduce(amax[:, bass.ds(g, 1), f:f + 1].rearrange("p o f -> p (o f)"),
                                          hid[:, f, bass.ds(g * 512, 512)], AX, ALU.max,
                                          apply_absolute_value=True).then_inc(amax_done, 1)
                dve.wait_ge(amax_done, NG * FCH)
                dve.tensor_reduce(amax1[:, :], amax[:, :, :].rearrange("p g f -> p (g f)"), AX,
                                  ALU.max).then_inc(amax_done, 1)
                dve.wait_ge(all_done, 1)
                steps_of(dve, step, 0, amax_all, h_scale, tmp)
                dve.tensor_scalar(out_step[:, :], C.wo_step[:, :], h_scale[:, 1:2], None, ALU.mult)

            @block.gpsimd
            def _(pool):
                pool.wait_ge(amax_done, NG * FCH + 1)
                pool.partition_all_reduce(amax_all[:, :], amax1[:, :], P, RMAX).then_inc(all_done, 1)

        with ExitStack() as ctx:
            m = Mem(nc, ctx, C.sems, "f3")
            x = C.xn4[:, 0:G, :]
            y = C.xn4[:, G:2 * G, :]
            gbo = C.xn4[:, 2 * G, :]
            hhi = xhi[:, :, :].rearrange("p v (f t) -> p v f t", t=GT)
            hlo = xlo[:, :, :].rearrange("p v (f t) -> p v f t", t=GT)
            ON_POOL = 3
            ps = m.ps("ps", [P, 2, 512])
            names = ("bias_in", "gbo_done", "scaled", "unit_done", "hi_done", "lo_dve", "lo_pool", "o_done", "xb_done", "y_done")
            s = {n: m.sem(n) for n in names}
            x_in = [m.sem(f"x_in{r}") for r in range(G)]
            stored = [m.sem(f"stored{r}") for r in range(G)]
            block = ctx.enter_context(nc.Block())

            def run(eng, step):
                step(0, 0)
                step(1, 1)
                with eng.Fori(0, (NG - 4) // 2) as i:
                    for d in range(2):
                        step(i * 2 + 2 + d, d)
                for g in range(NG - 2, NG + 1):
                    step(g, g % 2)

            def has(g):
                return not isinstance(g, int) or 0 <= g < NG

            @block.sync
            def _(sp):
                sp.dma_start(gbo, b_out.partition_broadcast(P)).then_inc(s["bias_in"], 16)

                def step(g, v):
                    if has(g):
                        for r in range(G):
                            if has(g - 1):
                                sp.wait_ge(s["y_done"], (g - 1) * G + r + 1)
                            sp.dma_start(x[:, r, :], x3_dram[bass.ds(g * GT + r * P, P), :]).then_inc(x_in[r], 16)
                    if has(g - 1):
                        for r in range(G):
                            sp.wait_ge(s["y_done"], (g - 1) * G + r + 1)
                            sp.dma_start(out_dram[bass.ds((g - 1) * GT + r * P, P), :], y[:, r, :]).then_inc(stored[r], 16)

                run(sp, step)
                for r in range(G):
                    sp.wait_ge(stored[r], 16 * NG)

            @block.gpsimd
            def _(pool):
                pool.wait_ge(s["bias_in"], 16)
                pool.tensor_scalar(gbo, gbo, C.gate[:, 3:4], None, ALU.mult).then_inc(s["gbo_done"], 1)
                pool.wait_ge(s["gbo_done"], 1)

                def step(g, v):
                    if has(g):
                        for f in range(ON_POOL):
                            if f == 0 and has(g - 2):
                                pool.wait_ge(s["o_done"], (g - 1) * G)
                            pool.wait_ge(s["hi_done"], g * FCH + f + 1)
                            pool.tensor_tensor(hlo[:, v, f, :], hid[:, f, bass.ds(g * GT, GT)], hhi[:, v, f, :],
                                               ALU.subtract).then_inc(s["lo_pool"], 1)
                        for r in range(G):
                            pool.wait_ge(x_in[r], (g + 1) * 16)
                            pool.tensor_tensor(x[:, r, :], x[:, r, :], gbo, ALU.add).then_inc(s["xb_done"], 1)

                run(pool, step)

            @block.scalar
            def _(act):
                def step(g, v):
                    if has(g):
                        for f in range(FCH):
                            if f == 0 and has(g - 2):
                                act.wait_ge(s["o_done"], (g - 1) * G)
                            act.wait_ge(s["unit_done"], g * FCH + f + 1)
                            act.activation(hhi[:, v, f, :], hid[:, f, bass.ds(g * GT, GT)], ACT.Copy).then_inc(s["hi_done"], 1)

                run(act, step)

            @block.vector
            def _(dve):
                def scale(g, f):
                    h = hid[:, f, bass.ds(g * GT, GT)]
                    dve.tensor_scalar(h, h, h_scale[:, 0:1], MAGIC, ALU.mult, ALU.add).then_inc(s["scaled"], 1)

                def unit(g, f):
                    h = hid[:, f, bass.ds(g * GT, GT)]
                    dve.wait_ge(s["scaled"], g * FCH + f + 1)
                    dve.tensor_scalar(h, h, MAGIC, out_step[:, f:f + 1], ALU.subtract, ALU.mult).then_inc(s["unit_done"], 1)

                def low(g, v, f):
                    dve.wait_ge(s["hi_done"], g * FCH + f + 1)
                    dve.tensor_tensor(hlo[:, v, f, :], hid[:, f, bass.ds(g * GT, GT)], hhi[:, v, f, :],
                                      ALU.subtract).then_inc(s["lo_dve"], 1)

                def residual(g, r):
                    dve.wait_ge(s["o_done"], g * G + r + 1)
                    dve.wait_ge(s["xb_done"], g * G + r + 1)
                    if has(g - 1):
                        dve.wait_ge(stored[r], g * 16)
                    dve.scalar_tensor_tensor(out=y[:, r, :], in0=ps[:, r % 2, 0:D], scalar=C.gate[:, 3:4], in1=x[:, r, :],
                                             op0=ALU.mult, op1=ALU.add).then_inc(s["y_done"], 1)

                def step(g, v):
                    if has(g):
                        scale(g, 0)
                        for f in range(FCH):
                            if f + 1 < FCH:
                                scale(g, f + 1)
                            unit(g, f)
                            if f - 1 >= ON_POOL:
                                low(g, v, f - 1)
                            if has(g - 1) and f % 2:
                                residual(g - 1, f // 2)
                        low(g, v, FCH - 1)
                    else:
                        for r in range(G):
                            residual(g - 1, r)

                run(dve, step)

            @block.tensor
            def _(pe):
                def step(g, v):
                    if not has(g - 1):
                        return
                    w = 1 - v
                    pe.wait_ge(s["lo_dve"], g * (FCH - ON_POOL))
                    pe.wait_ge(s["lo_pool"], g * ON_POOL)
                    for r in range(G):
                        if r >= 2 or has(g - 2):
                            pe.wait_ge(s["y_done"], (g - 1) * G + r - 1)
                        for f in range(FCH):
                            for i, part in enumerate((hhi, hlo)):
                                mm = pe.matmul(ps[:, r % 2, 0:D], part[:, w, f, r * P:(r + 1) * P], C.wo_q[:, f, :],
                                               start=(f == 0 and i == 0), stop=(f == FCH - 1 and i == 1))
                        mm.then_inc(s["o_done"], 1)

                run(pe, step)


class Consts:
    pass


def program(nc, io, out):
    x1_dram, x3_dram, xn_dram = (nc.dram_tensor(n, (B * N, D), F32).ap() for n in ("x1", "x3", "xn2"))
    y_dram = nc.dram_tensor("y_slots", (NSUB * P, D), F32).ap()
    x_dram = io["x"].rearrange("b n d -> (b n) d")
    out_dram = out.rearrange("b n d -> (b n) d")
    with ExitStack() as ctx:
        C = Consts()
        C.sems = []
        m = Mem(nc, ctx, C.sems, "all")
        C.ident = m.sb("ident", [P, P])
        C.ones = m.sb("ones", [P, P])
        C.half = m.sb("half", [P, TPB])
        C.gate = m.sb("gate", [P, 4])
        C.ctxT = m.sb("ctxT", [P, 2, B, KEYS])
        C.top = m.sb("top", [P, TOPK, TILES])
        C.slots = m.sb("slots", [P, TOPK, TILES], I32)
        C.expert = m.sb("expert", [P, NST], I32)
        C.token_of = m.sb("token_of", [P, NSUB], I32)
        prologue(nc, io, C)
        with ExitStack() as moe:
            mm = Mem(nc, moe, C.sems, "moe")
            split = {"w1": io["L0_ffn_W1"], "w2": io["L0_ffn_W2"],
                     "w1s": mm.sb("w1s", [P, E * KD, 2, F], BF16), "w2s": mm.sb("w2s", [P, E * FCH, 2 * D], BF16)}
            w0 = {"wq": io["L0_xattn_Wq"], "bq": io["L0_xattn_bq"], "wk": io["L0_xattn_Wk"], "bk": io["L0_xattn_bk"],
                  "wv": io["L0_xattn_Wv"], "bv": io["L0_xattn_bv"], "wo": io["L0_xattn_Wo"], "bo": io["L0_xattn_bo"]}
            attention(nc, C, x_dram, x1_dram, w0, 0, split)
            routing(nc, C, x1_dram, xn_dram, io["L0_ffn_Wg"])
            experts(nc, C, xn_dram, y_dram, split, io["L0_ffn_b1"], io["L0_ffn_b2"])
        C.wi_q = m.sb("wi_q", [P, KD, F], BF16)
        C.wo_q = m.sb("wo_q", [P, FCH, D], BF16)
        C.b_in = m.sb("b_in", [P, FCH])
        C.wi_step = m.sb("wi_step", [P, FCH])
        C.wo_step = m.sb("wo_step", [P, FCH])
        C.xn4 = m.sb("xn4", [P, TILES, D])
        C.xn4_max = m.sb("xn4_max", [P, TILES])
        inner = HEADS * 64
        w1 = {"wq": io["L1_xattn_w_q"], "wk": io["L1_xattn_w_kv"][:, 0:inner], "wv": io["L1_xattn_w_kv"][:, inner:2 * inner],
              "wo": io["L1_xattn_w_out"]}
        with ExitStack() as folded:
            mm = Mem(nc, folded, C.sems, "folded")
            C.k_fold = mm.sb("k_fold", [P, B, KD, 2, ROWS], BF16)
            C.v_fold = mm.sb("v_fold", [P, B, 2, RCH, D], BF16)
            fold(nc, C, w1, io["L1_ffn_W_in"], io["L1_ffn_W_out"], io["L1_ffn_b_in"])
            clear_semaphores(nc, C)
            folded_attention(nc, C, x1_dram, y_dram, x3_dram, io["L1_xattn_b_out"], 1, 64 ** -0.5)
        ffn(nc, C, x3_dram, out_dram, io["L1_ffn_b_out"])


_INS = ["x", "ctx_768", "g_xattn", "g_ffn", "L0_xattn_Wq", "L0_xattn_bq", "L0_xattn_Wk", "L0_xattn_bk", "L0_xattn_Wv",
        "L0_xattn_bv", "L0_xattn_Wo", "L0_xattn_bo", "L0_ffn_Wg", "L0_ffn_W1", "L0_ffn_b1", "L0_ffn_W2", "L0_ffn_b2",
        "L1_xattn_w_q", "L1_xattn_w_kv", "L1_xattn_w_out", "L1_xattn_b_out", "L1_ffn_W_in", "L1_ffn_b_in", "L1_ffn_W_out",
        "L1_ffn_b_out"]


def kernel(**inputs):
    import numpy as _np
    import concourse.bacc as _bacc
    from concourse import mybir as _mybir
    from concourse.bass_utils import run_bass_kernel_spmd as _run

    nc = _bacc.Bacc("TRN2", target_bir_lowering=False, num_devices=1)
    arrays, io = {}, {}
    for name in _INS:
        a = _np.ascontiguousarray(inputs[name])
        arrays[f"in_{name}_dram"] = a
        io[name] = nc.dram_tensor(f"in_{name}_dram", a.shape, _mybir.dt.from_np(a.dtype), kind="ExternalInput").ap()
    out = nc.dram_tensor("out_0_dram", (B, N, D), F32, kind="ExternalOutput").ap()
    program(nc, io, out)
    r = _run(nc, [arrays], core_ids=[0])
    return r.results[0]["out_0_dram"]
```

```python
from contextlib import ExitStack

import concourse.bass as bass
from concourse import mybir

F32 = mybir.dt.float32
BF16 = mybir.dt.bfloat16
I32 = mybir.dt.int32
U32 = mybir.dt.uint32
ALU = mybir.AluOpType
ACT = mybir.ActivationFunctionType
AX = mybir.AxisListType.X
RMAX = bass.bass_isa.ReduceOp.max

P = 128
B, N, D = 4, 1024, 256
KEYS, DC = 77, 192
TILES = B * N // P
TPB = N // P
KD = D // P
HEADS = 16
ROWS = HEADS * KEYS
RCH = -(-ROWS // P)
CTX_K = [(0, P), (P, DC - P)]
REPS = 3
HPB = 6
SB = [(j * HPB, min(HEADS, (j + 1) * HPB)) for j in range(-(-HEADS // HPB))]
E, F, TOPK = 8, 1024, 2
FCH = F // P
SLOT_T = 256
SUB = SLOT_T // P
NST = (B * N * TOPK + E * (SLOT_T - 1)) // SLOT_T
NSUB = NST * SUB
EPS = 1e-5
CLAMP = 10000.0
MAGIC = 1.5 * 2.0 ** 23


def wait(eng, sem, value):
    if isinstance(value, int) and value <= 0:
        return
    eng.wait_ge(sem, value)


def counted(eng, value):
    return value if isinstance(value, int) else eng.snap(eng.to_reg(value))


class Mem:

    def __init__(self, nc, ctx, sems, tag):
        self.nc, self.ctx, self.sems, self.tag = nc, ctx, sems, tag

    def sb(self, name, shape, dt=F32):
        return self.ctx.enter_context(self.nc.sbuf_tensor(f"{self.tag}_{name}", shape, dt))

    def ps(self, name, shape, dt=F32):
        return self.ctx.enter_context(self.nc.psum_tensor(f"{self.tag}_{name}", shape, dt))

    def sem(self, name):
        self.sems.append(self.nc.alloc_semaphore(name=f"{self.tag}_{name}"))
        return self.sems[-1]


def clear_semaphores(nc, C):
    nc.clear_and_free_semaphores(C.sems)
    nc.all_engine_barrier()
    C.sems.clear()


def blocks_of(hpg):
    out = []
    for g in range(HEADS // hpg):
        lo, hi = g * hpg * KEYS, (g + 1) * hpg * KEYS
        out += [(c, g) for c in range(RCH) if c * P < hi and (c + 1) * P > lo]
    return out


def pieces_of(hpg):
    out = []
    for j, (a, z) in enumerate(SB):
        for g in range(HEADS // hpg):
            lo, hi = max(a, g * hpg), min(z, (g + 1) * hpg)
            if lo < hi:
                out.append((j, g, lo, hi))
    return out


def prologue(nc, io, C):
    with ExitStack() as ctx:
        m = Mem(nc, ctx, C.sems, "pro")
        ctx_rows = m.sb("ctx_rows", [KEYS, B, DC])
        g_row = m.sb("g_row", [P, 4])
        ps = m.ps("ps", [P, 2, 512])
        loaded, ones_set, ident_set, turned, copied = (m.sem(x) for x in ("loaded", "ones", "ident", "turned", "copied"))
        tanh_done, ones_row = m.sem("tanh_done"), m.sem("ones_row")
        block = ctx.enter_context(nc.Block())

        @block.sync
        def _(sp):
            sp.dma_start(ctx_rows[:, :, :], io["ctx_768"].rearrange("b k d -> k b d")).then_inc(loaded, 16)
            sp.dma_start(g_row[:, 0:2], io["g_xattn"].partition_broadcast(P)).then_inc(loaded, 16)
            sp.dma_start(g_row[:, 2:4], io["g_ffn"].partition_broadcast(P)).then_inc(loaded, 16)

        @block.gpsimd
        def _(pool):
            pool.memset(C.ident[:, :], 0.0).then_inc(ones_set, 1)
            pool.memset(C.ones[:, :], 1.0).then_inc(ones_set, 1)
            pool.memset(C.half[:, :], -0.5).then_inc(ones_set, 1)
            pool.wait_ge(ones_set, 1)
            pool.affine_select(out=C.ident[:, :], in_=C.ident[:, :], compare_op=ALU.not_equal, fill=1.0, base=0,
                               pattern=[[-1, P]], channel_multiplier=1).then_inc(ident_set, 1)
            pool.wait_ge(ones_set, 3)

        @block.tensor
        def _(pe):
            pe.wait_ge(loaded, 48)
            pe.wait_ge(ident_set, 1)
            for b in range(B):
                if b >= 2:
                    pe.wait_ge(copied, 2 * (b - 1))
                for k, (at, n) in enumerate(CTX_K):
                    pe.transpose(ps[0:n, b % 2, k * KEYS:(k + 1) * KEYS], ctx_rows[:, b, at:at + n],
                                 C.ident[0:KEYS, 0:KEYS]).then_inc(turned, 1)

        @block.vector
        def _(dve):
            dve.memset(C.ctxT[DC - P:DC - P + 1, 1, :, :], 1.0).then_inc(ones_row, 1)
            for b in range(B):
                dve.wait_ge(turned, 2 * (b + 1))
                for k, (at, n) in enumerate(CTX_K):
                    dve.tensor_copy(C.ctxT[0:n, k, b, :], ps[0:n, b % 2, k * KEYS:(k + 1) * KEYS]).then_inc(copied, 1)
            dve.wait_ge(copied, 2 * B)
            dve.wait_ge(ones_row, 1)

        @block.scalar
        def _(act):
            act.wait_ge(loaded, 48)
            act.activation(C.gate[:, :], g_row[:, :], ACT.Tanh).then_inc(tanh_done, 1)
            act.wait_ge(tanh_done, 1)


def attention(nc, C, x_in, x_out, w, gate_col, split):
    hpg = 8
    ng = HEADS // hpg
    dh = P // hpg
    blocks = blocks_of(hpg)
    scale = float(dh) ** -0.5
    NSB = len(SB)
    ctx_rows = (P, DC - P + 1)
    pieces = pieces_of(hpg)
    vgroups = [blocks[i:i + 4] for i in range(0, len(blocks), 4)]
    NVG = len(vgroups)
    RING, SKEW = 8, 3
    with ExitStack() as ctx:
        m = Mem(nc, ctx, C.sems, "a0")
        wq = m.sb("wq", [P, KD, ng * P])
        wk = m.sb("wk", [P, 2, ng * P])
        wv = m.sb("wv", [P, 2, ng * P])
        wo = m.sb("wo", [P, ng, D])
        bq = m.sb("bq", [P, ng])
        gbo = m.sb("gbo", [P, D])
        kmask = m.sb("kmask", [P, hpg])
        vmask = m.sb("vmask", [P, len(blocks), hpg])
        ctx_now = m.sb("ctx_now", [P, 2, REPS * KEYS])
        kblk = m.sb("kblk", [P, ng, hpg * KEYS])
        vblk = m.sb("vblk", [P, len(blocks), P])
        x = m.sb("x", [P, RING, D])
        stats = m.sb("stats", [P, 2, 6])
        mv = m.sb("mv", [P, 2, 2])
        veps = m.sb("veps", [P, 2])
        rstd = m.sb("rstd", [P, 2])
        xn = m.sb("xn", [P, D])
        xnT = m.sb("xnT", [P, KD, P])
        qT = m.sb("qT", [P, ng, P])
        mx = m.sb("mx", [P, HEADS])
        z = m.sb("z", [P, 2, ROWS])
        ssum = m.sb("ssum", [P, HEADS])
        rsum = m.sb("rsum", [P, 2, HEADS])
        pT = m.sb("pT", [P, RCH, P])
        attnT = m.sb("attnT", [P, ng, P])
        xo = m.sb("xo", [P, 2, D])
        stage = m.sb("stage", [P, 2, 2, 512])
        ps_sc = m.ps("ps_sc", [P, NSB, 512])
        ps_xq = m.ps("ps_xq", [P, 512])
        ps_p = m.ps("ps_p", [P, 3, 512])
        ps_vo = m.ps("ps_vo", [P, 512])
        ps_x, ps_q = ps_xq[:, 0:D], ps_xq[:, D:2 * D]
        ps_v, ps_o = ps_vo[:, 0:D], ps_vo[:, D:2 * D]

        keys_in, weights_in, gbo_done = m.sem("keys_in"), m.sem("weights_in"), m.sem("gbo_done")
        x_loaded = [m.sem(f"x_loaded{i}") for i in range(RING)]
        x_stored = [m.sem(f"x_stored{i}") for i in range(2)]
        piece_in = [m.sem(f"piece_in{i}") for i in range(2)]
        names = ("stats_done", "mean_done", "veps_done", "rstd_done", "xn_done", "turned_x", "xnT_done", "q_done",
                 "qT_done", "k_proj", "k_done", "v_proj", "v_done", "scores_done", "max_done", "mx_done", "z_done",
                 "zc_done", "exp_done", "sum_done", "rsum_done", "norm_done", "turned_p", "pT_done", "pv_done",
                 "attn_done", "o_done", "xo_done", "xb_done", "mask_step", "ctx_done", "hi_done", "lo_done")
        s = {n: m.sem(n) for n in names}
        N_WEIGHTS = 7
        MASKS = 4 + 2 * len(blocks)
        block = ctx.enter_context(nc.Block())

        def run(eng, slot):
            for t in range(TPB + SKEW):
                slot(t, t % TPB, t // TPB)
            with eng.Fori(1, B - 1) as b:
                for t in range(SKEW, TPB + SKEW):
                    slot(b * TPB + t, t % TPB, b + t // TPB)
            for t in range(SKEW, TPB + SKEW):
                slot((B - 1) * TPB + t, t % TPB, B - 1 + t // TPB)

        def has(T):
            return not isinstance(T, int) or 0 <= T < TILES

        def load_projection(eng, dst, name, bias, sem):
            for k, (at, n) in enumerate(CTX_K):
                eng.dma_start(dst[0:n, k, :], w[name][at:at + n, :]).then_inc(sem, 16)
            eng.dma_start(dst[DC - P:DC - P + 1, 1, :], w[bias].unsqueeze(0)).then_inc(sem, 16)

        @block.sync
        def _(sp):
            def load(T, r):
                sp.dma_start(x[:, r, :], x_in[bass.ds(T * P, P), :]).then_inc(x_loaded[r], 16)

            load(0, 0)
            load_projection(sp, wk, "wk", "bk", keys_in)
            load(1, 1)
            sp.dma_start(wq[:, :, :], w["wq"].rearrange("(k p) n -> p k n", p=P)).then_inc(weights_in, 16)
            sp.dma_start(wo[:, :, :], w["wo"].rearrange("(g p) n -> p g n", p=P)).then_inc(weights_in, 16)
            for r in range(2, RING - SKEW):
                load(r, r)

            def slot(T, t, b):
                if has(T):
                    wait(sp, s["hi_done"], 2 * (T - 1))
                    wait(sp, s["lo_done"], 2 * (T - 1))
                    sp.dma_start(stage[:, t % 2, 0, :],
                                 split["w1"].rearrange("e (c p) f -> (e c) p f", p=P)
                                 [bass.ds(b * (TPB // 2) + t // 2, 1), :, t % 2 * 512:(t % 2 + 1) * 512]
                                 .rearrange("o p f -> p (o f)")).then_inc(piece_in[t % 2], 16)
                    sp.dma_start(stage[:, t % 2, 1, :].rearrange("p (g d) -> p g d", d=D),
                                 split["w2"].rearrange("e (g p) d -> p (e g) d", p=P)
                                 [:, bass.ds(T * 2, 2), :]).then_inc(piece_in[t % 2], 16)
                if has(T - SKEW):
                    sp.wait_ge(s["xo_done"], T - SKEW + 1)
                    sp.dma_start(x_out[bass.ds((T - SKEW) * P, P), :],
                                 xo[:, (t - SKEW) % 2, :]).then_inc(x_stored[(t - SKEW) % 2], 16)
                    if has(T + RING - SKEW):
                        load(T + RING - SKEW, (t - SKEW) % RING)
                elif T + RING - SKEW < RING:
                    load(T + RING - SKEW, T + RING - SKEW)

            run(sp, slot)
            for i in range(2):
                sp.wait_ge(x_stored[i], 16 * TILES // 2)

        @block.gpsimd
        def _(pool):
            def power(T, u):
                pool.wait_ge(s["veps_done"], T + 1)
                pool.tensor_tensor(rstd[:, u:u + 1], veps[:, u:u + 1], C.half[:, 0:1], ALU.pow).then_inc(s["rstd_done"], 1)

            pool.memset(kmask[:, :], 1.0).then_inc(s["mask_step"], 1)
            pool.memset(vmask[:, :, :], 1.0).then_inc(s["mask_step"], 1)
            pool.wait_ge(s["mask_step"], 2)
            pool.affine_select(out=kmask[:, :], in_=kmask[:, :], compare_op=ALU.is_ge, fill=0.0, base=0,
                               pattern=[[-dh, hpg]], channel_multiplier=1).then_inc(s["mask_step"], 1)
            pool.wait_ge(s["mask_step"], 3)
            pool.affine_select(out=kmask[:, :], in_=kmask[:, :], compare_op=ALU.is_ge, fill=0.0, base=dh - 1,
                               pattern=[[dh, hpg]], channel_multiplier=-1).then_inc(s["mask_step"], 1)
            power(0, 0)
            power(1, 1)
            for i, (c, g) in enumerate(blocks):
                at = c * P - g * hpg * KEYS
                pool.affine_select(out=vmask[:, i, :], in_=vmask[:, i, :], compare_op=ALU.is_ge, fill=0.0, base=at,
                                   pattern=[[-KEYS, hpg]], channel_multiplier=1).then_inc(s["mask_step"], 1)
            pool.wait_ge(s["mask_step"], 4 + len(blocks))
            for i, (c, g) in enumerate(blocks):
                at = c * P - g * hpg * KEYS
                pool.affine_select(out=vmask[:, i, :], in_=vmask[:, i, :], compare_op=ALU.is_ge, fill=0.0,
                                   base=KEYS - 1 - at, pattern=[[KEYS, hpg]],
                                   channel_multiplier=-1).then_inc(s["mask_step"], 1)
            pool.wait_ge(weights_in, 16 * N_WEIGHTS)
            pool.tensor_scalar(gbo[:, :], gbo[:, :], C.gate[:, gate_col:gate_col + 1], None,
                               ALU.mult).then_inc(gbo_done, 1)
            pool.wait_ge(gbo_done, 1)

            def slot(T, t, b):
                u = t % 2
                if has(T + 2):
                    power(T + 2, u)
                if has(T - 1):
                    v = (t - 1) % 2
                    pool.wait_ge(s["rsum_done"], T)
                    zt = z[:, v, :].rearrange("p (h k) -> p h k", k=KEYS)
                    pool.tensor_tensor(zt, zt, rsum[:, v, :].unsqueeze(2).broadcast_to((P, HEADS, KEYS)),
                                       ALU.mult).then_inc(s["norm_done"], 1)
                if has(T):
                    pool.wait_ge(s["hi_done"], 2 * T + 2)
                    w1, w2 = split["w1s"], split["w2s"]
                    at = bass.ds(b * (TPB // 2) + t // 2, 1)
                    cols = slice(t % 2 * 512, (t % 2 + 1) * 512)
                    pool.tensor_tensor(w1[:, at, 1, cols].rearrange("p o f -> p (o f)"), stage[:, u, 0, :],
                                       w1[:, at, 0, cols].rearrange("p o f -> p (o f)"),
                                       ALU.subtract).then_inc(s["lo_done"], 1)
                    pool.tensor_tensor(w2[:, bass.ds(T * 2, 2), D:2 * D],
                                       stage[:, u, 1, :].rearrange("p (g d) -> p g d", d=D),
                                       w2[:, bass.ds(T * 2, 2), 0:D], ALU.subtract).then_inc(s["lo_done"], 1)
                    pool.wait_ge(s["xn_done"], T + 1)
                    pool.tensor_tensor(x[:, t, :], x[:, t, :], gbo[:, :], ALU.add).then_inc(s["xb_done"], 1)

            run(pool, slot)

        @block.tensor
        def _(pe):
            def turn_x(T):
                pe.wait_ge(s["xn_done"], T + 1)
                wait(pe, s["qT_done"], T)
                for k in range(KD):
                    mm = pe.transpose(ps_x[:, k * P:(k + 1) * P], xn[:, k * P:(k + 1) * P], C.ident[:, :])
                mm.then_inc(s["turned_x"], 1)

            def keys(T, b):
                pe.wait_ge(s["ctx_done"], b + 1)
                pe.wait_ge(s["xnT_done"], T + 1)
                for g in range(ng):
                    for k, n in enumerate(ctx_rows):
                        mm = pe.matmul(ps_q[:, g * KEYS:(g + 1) * KEYS], wk[0:n, k, g * P:(g + 1) * P],
                                       ctx_now[0:n, k, 0:KEYS], start=(k == 0), stop=(k == 1))
                mm.then_inc(s["k_proj"], 1)

            def values():
                for j, group in enumerate(vgroups):
                    for i, (c, g) in enumerate(group):
                        at0 = c * P % KEYS
                        for k, n in enumerate(ctx_rows):
                            mm = pe.matmul(ps_p[:, j, i * P:(i + 1) * P], ctx_now[0:n, k, at0:at0 + P],
                                           wv[0:n, k, g * P:(g + 1) * P], start=(k == 0), stop=(k == 1))
                    mm.then_inc(s["v_proj"], 1)

            turn_x(0)
            pe.wait_ge(keys_in, 16 * 3)
            keys(0, 0)
            pe.wait_ge(weights_in, 16 * N_WEIGHTS)

            def slot(T, t, b):
                u = t % 2
                if has(T):
                    pe.wait_ge(s["xnT_done"], T + 1)
                    if t == 0:
                        pe.wait_ge(s["k_done"], b + 1)
                    for g in range(ng):
                        for k in range(KD):
                            mm = pe.matmul(ps_q[:, g * P:(g + 1) * P], wq[:, k, g * P:(g + 1) * P], xnT[:, k, :],
                                           start=(k == 0), stop=(k == KD - 1))
                    mm.then_inc(s["q_done"], 1)
                if has(T - 2):
                    pe.wait_ge(s["norm_done"], T - 1)
                    if t == 2:
                        pe.wait_ge(s["v_done"], NVG * (b + 1))
                    for j in range(3):
                        wait(pe, s["pT_done"], 3 * (T - 3) + j + 1)
                        for c in range(4 * j, min(RCH, 4 * j + 4)):
                            n = min(P, ROWS - c * P)
                            mm = pe.transpose(ps_p[0:n, j, c % 4 * P:(c % 4 + 1) * P], z[:, u, c * P:c * P + n],
                                              C.ident[:, :])
                        mm.then_inc(s["turned_p"], 1)
                if has(T - 3):
                    pe.wait_ge(s["attn_done"], T - 2)
                    for g in range(ng):
                        mm = pe.matmul(ps_o, attnT[:, g, :], wo[:, g, :], start=(g == 0), stop=(g == ng - 1))
                    mm.then_inc(s["o_done"], 1)
                if has(T):
                    pe.wait_ge(s["qT_done"], T + 1)
                    for j, (a, _) in enumerate(SB):
                        wait(pe, s["z_done"], NSB * (T - 1) + j + 1)
                        for jj, g, h0, h1 in pieces:
                            if jj == j:
                                mm = pe.matmul(ps_sc[:, j, (h0 - a) * KEYS:(h1 - a) * KEYS], qT[:, g, :],
                                               kblk[:, g, (h0 - g * hpg) * KEYS:(h1 - g * hpg) * KEYS],
                                               start=True, stop=True)
                        mm.then_inc(s["scores_done"], 1)
                if has(T + 1):
                    turn_x(T + 1)
                if has(T - 2):
                    wait(pe, s["xo_done"], T - 2)
                    for g in range(ng):
                        mine = [i for i, (c, gg) in enumerate(blocks) if gg == g]
                        for i in mine:
                            c = blocks[i][0]
                            if g == 0 and (i == mine[0] or c % 4 == 0):
                                pe.wait_ge(s["pT_done"], 3 * (T - 2) + c // 4 + 1)
                            if g == 1 and c == 8:
                                pe.wait_ge(s["pT_done"], 3 * (T - 2) + 3)
                            n = min(P, ROWS - c * P)
                            mm = pe.matmul(ps_v[:, g * P:(g + 1) * P], vblk[0:n, i, :], pT[0:n, c, :],
                                           start=(i == mine[0]), stop=(i == mine[-1]))
                    mm.then_inc(s["pv_done"], 1)
                if has(T) and t == 1:
                    wait(pe, s["pT_done"], 3 * (T - 1))
                    values()
                if has(T + 1) and t == TPB - 1:
                    keys(T + 1, b + 1)

            run(pe, slot)

        @block.scalar
        def _(act):
            def context(b):
                wait(act, s["v_proj"], NVG * b)
                wait(act, s["k_proj"], b)
                for k, n in enumerate(ctx_rows):
                    ins = act.activation(ctx_now[0:n, k, :].rearrange("p (r k) -> p r k", r=REPS),
                                         C.ctxT[0:n, k, bass.ds(b, 1), :].broadcast_to((n, REPS, KEYS)), ACT.Copy)
                ins.then_inc(s["ctx_done"], 1)

            def turned(T):
                act.wait_ge(s["turned_x"], T + 1)
                wait(act, s["q_done"], T)
                act.activation(xnT[:, :, :].rearrange("p k t -> p (k t)"), ps_x, ACT.Copy).then_inc(s["xnT_done"], 1)

            load_projection(act, wv, "wv", "bv", weights_in)
            act.dma_start(gbo[:, :], w["bo"].partition_broadcast(P)).then_inc(weights_in, 16)
            with nc.allow_non_contiguous_dma(reason="a short bias, one element to a partition"):
                act.dma_start(bq[:, :], w["bq"].rearrange("(g p) -> p g", p=P)).then_inc(weights_in, 16)
            context(0)
            turned(0)
            act.wait_ge(weights_in, 16 * N_WEIGHTS)

            def slot(T, t, b):
                u = t % 2
                if has(T - 3):
                    act.wait_ge(s["pv_done"], T - 2)
                    wait(act, s["o_done"], T - 3)
                    act.activation(attnT[:, :, :].rearrange("p g t -> p (g t)"), ps_v, ACT.Copy).then_inc(s["attn_done"], 1)
                if has(T - 1):
                    v = (t - 1) % 2
                    act.wait_ge(s["zc_done"], T)
                    act.activation(z[:, v, :], z[:, v, :], ACT.Exp, scale=scale).then_inc(s["exp_done"], 1)
                if has(T):
                    act.wait_ge(s["q_done"], T + 1)
                    wait(act, s["scores_done"], NSB * T)
                    for g in range(ng):
                        ins = act.activation(qT[:, g, :], ps_q[:, g * P:(g + 1) * P], ACT.Identity, bias=bq[:, g:g + 1])
                    ins.then_inc(s["qT_done"], 1)
                if has(T - 2):
                    wait(act, s["pv_done"], T - 2)
                    for j in range(3):
                        act.wait_ge(s["turned_p"], 3 * (T - 2) + j + 1)
                        if j < 2:
                            ins = act.activation(pT[:, 4 * j:4 * j + 4, :].rearrange("p c t -> p (c t)"), ps_p[:, j, :],
                                                 ACT.Copy)
                        else:
                            last = ROWS - (RCH - 1) * P
                            act.activation(pT[:, RCH - 2, :], ps_p[:, 2, 0:P], ACT.Copy)
                            ins = act.activation(pT[0:last, RCH - 1, :], ps_p[0:last, 2, P:2 * P], ACT.Copy)
                        ins.then_inc(s["pT_done"], 1)
                if has(T):
                    act.wait_ge(piece_in[u], 32 * (b * (TPB // 2) + t // 2 + 1))
                    act.activation(split["w1s"][:, bass.ds(b * (TPB // 2) + t // 2, 1), 0,
                                                u * 512:(u + 1) * 512].rearrange("p o f -> p (o f)"),
                                   stage[:, u, 0, :], ACT.Copy).then_inc(s["hi_done"], 1)
                    act.activation(split["w2s"][:, bass.ds(T * 2, 2), 0:D],
                                   stage[:, u, 1, :].rearrange("p (g d) -> p g d", d=D),
                                   ACT.Copy).then_inc(s["hi_done"], 1)
                if has(T + 1):
                    turned(T + 1)
                if t == 4 and has(T + TPB):
                    context(b + 1)

            run(act, slot)

        @block.vector
        def _(dve):
            def ln_stats(T, u, r, turn):
                dve.wait_ge(x_loaded[r], 16 * (turn + 1))
                dve.bn_stats(stats[:, u, :], x[:, r, :]).then_inc(s["stats_done"], 1)
                dve.wait_ge(s["stats_done"], T + 1)

            def ln_mean(T, u):
                dve.bn_aggr(mv[:, u, :], stats[:, u, :]).then_inc(s["mean_done"], 1)
                dve.wait_ge(s["mean_done"], T + 1)
                dve.tensor_scalar(veps[:, u:u + 1], mv[:, u, 1:2], EPS, None, ALU.add).then_inc(s["veps_done"], 1)

            def ln(T, u, r):
                dve.wait_ge(s["rstd_done"], T + 1)
                wait(dve, s["turned_x"], T)
                dve.tensor_scalar(xn[:, :], x[:, r, :], mv[:, u, 0:1], rstd[:, u:u + 1], ALU.subtract,
                                  ALU.mult).then_inc(s["xn_done"], 1)

            def block_keys(T, b):
                dve.wait_ge(s["k_proj"], b + 1)
                wait(dve, s["scores_done"], T * NSB)
                for h in range(hpg):
                    ins = dve.tensor_scalar(kblk[:, :, h * KEYS:(h + 1) * KEYS],
                                            ps_q[:, 0:ng * KEYS].rearrange("p (g k) -> p g k", k=KEYS),
                                            kmask[:, h:h + 1], None, ALU.mult)
                ins.then_inc(s["k_done"], 1)

            def block_values(T, b):
                for j, group in enumerate(vgroups):
                    dve.wait_ge(s["v_proj"], b * NVG + j + 1)
                    if j == 0:
                        wait(dve, s["pv_done"], T)
                    n = len(group)
                    dve.tensor_tensor(
                        vblk[:, 4 * j:4 * j + n, :].rearrange("p i (h d) -> p (i h) d", d=dh),
                        ps_p[:, j, 0:n * P].rearrange("p (i d) -> p i d", d=dh),
                        vmask[:, 4 * j:4 * j + n, :].rearrange("p i h -> p (i h)").unsqueeze(2)
                        .broadcast_to((P, n * hpg, dh)), ALU.mult).then_inc(s["v_done"], 1)

            def sums(T, v):
                dve.wait_ge(s["exp_done"], T + 1)
                dve.tensor_reduce(ssum[:, :], z[:, v, :].rearrange("p (h k) -> p h k", k=KEYS), AX,
                                  ALU.add).then_inc(s["sum_done"], 1)
                dve.wait_ge(s["sum_done"], T + 1)
                wait(dve, s["norm_done"], T - 1)
                dve.reciprocal(rsum[:, v, :], ssum[:, :]).then_inc(s["rsum_done"], 1)

            ln_stats(0, 0, 0, 0)
            ln_mean(0, 0)
            ln(0, 0, 0)
            ln_stats(1, 1, 1, 0)
            ln_mean(1, 1)
            dve.wait_ge(s["mask_step"], 4)
            block_keys(0, 0)

            def slot(T, t, b):
                u = t % 2
                if has(T + 2):
                    ln_stats(T + 2, u, (t + 2) % RING, b + (t + 2) // RING)
                if has(T + 1):
                    ln(T + 1, (t + 1) % 2, (t + 1) % RING)
                if has(T + 2):
                    ln_mean(T + 2, u)
                if has(T - 2) and t == 2:
                    if isinstance(T, int) and T == 2:
                        dve.wait_ge(s["mask_step"], MASKS)
                    block_values(T - 2, b)
                if has(T - 1):
                    sums(T - 1, (t - 1) % 2)
                if has(T - SKEW):
                    v = (t - SKEW) % 2
                    turn = b if t >= SKEW else b - 1
                    dve.wait_ge(s["o_done"], T - SKEW + 1)
                    dve.wait_ge(s["xb_done"], T - SKEW + 1)
                    if has(T - SKEW - 2):
                        dve.wait_ge(x_stored[v], 16 * (turn * (TPB // 2) + (t - SKEW) % TPB // 2))
                    dve.scalar_tensor_tensor(out=xo[:, v, :], in0=ps_o, scalar=C.gate[:, gate_col:gate_col + 1],
                                             in1=x[:, (t - SKEW) % RING, :], op0=ALU.mult,
                                             op1=ALU.add).then_inc(s["xo_done"], 1)
                if has(T):
                    for j, (h0, h1) in enumerate(SB):
                        dve.wait_ge(s["scores_done"], T * NSB + j + 1)
                        dve.tensor_reduce(mx[:, h0:h1],
                                          ps_sc[:, j, 0:(h1 - h0) * KEYS].rearrange("p (h k) -> p h k", k=KEYS), AX,
                                          ALU.max).then_inc(s["max_done"], 1)
                    dve.wait_ge(s["max_done"], NSB * (T + 1))
                    dve.tensor_scalar(mx[:, :], mx[:, :], -CLAMP / scale, CLAMP / scale, ALU.max,
                                      ALU.min).then_inc(s["mx_done"], 1)
                    dve.wait_ge(s["mx_done"], T + 1)
                    if has(T - 2):
                        dve.wait_ge(s["turned_p"], 3 * (T - 1))
                    for j, (h0, h1) in enumerate(SB):
                        dve.scalar_tensor_tensor(
                            out=z[:, u, h0 * KEYS:h1 * KEYS].rearrange("p (h k) -> p h k", k=KEYS),
                            in0=ps_sc[:, j, 0:(h1 - h0) * KEYS].rearrange("p (h k) -> p h k", k=KEYS),
                            scalar=-CLAMP / scale, in1=mx[:, h0:h1].unsqueeze(2).broadcast_to((P, h1 - h0, KEYS)),
                            op0=ALU.max, op1=ALU.subtract).then_inc(s["z_done"], 1)
                    dve.wait_ge(s["z_done"], NSB * (T + 1))
                    dve.tensor_scalar(z[:, u, :], z[:, u, :], 0.0, None, ALU.min).then_inc(s["zc_done"], 1)
                if has(T + 1) and t == TPB - 1:
                    block_keys(T + 1, b + 1)

            run(dve, slot)


def routing(nc, C, x1_dram, xn_dram, wg):
    CH = 4
    NCH = TILES // CH
    PAIRS = TILES // 2
    RI = 4
    with ExitStack() as ctx:
        m = Mem(nc, ctx, C.sems, "route")
        x = m.sb("x", [P, TILES, D])
        wg_sb = m.sb("wg", [P, KD, E])
        stats = m.sb("stats", [P, CH, 6])
        mv = m.sb("mv", [P, TILES, 2])
        veps = m.sb("veps", [P, TILES])
        rstd = m.sb("rstd", [P, TILES])
        xT = m.sb("xT", [P, 2, 2 * KD * P])
        lower = m.sb("lower", [P, P])
        iota_i = m.sb("iota_i", [P, P], I32)
        iota = m.sb("iota", [P, P])
        token_i = m.sb("token_i", [P, TILES], I32)
        token = m.sb("token", [P, TILES])
        rank_i = m.sb("rank_i", [P, E], I32)
        rank = m.sb("rank", [P, E])
        sig = m.sb("sig", [P, TILES, E])
        big = [m.sb(f"big{i}", [P, TILES, E]) for i in range(2)]
        hot = m.sb("hot", [P, TOPK, TILES, E])
        top = m.sb("top", [P, TOPK, TILES])
        first = m.sb("first", [P, TILES])
        both = m.sb("both", [P, TILES, E])
        run_n = [m.sb(f"run_n{i}", [P, E, TILES]) for i in range(2)]
        tiles_f = m.sb("tiles_f", [P, E])
        tiles_i = m.sb("tiles_i", [P, E], I32)
        ends = [m.sb(f"ends{i}", [P, E]) for i in range(2)]
        starts = m.sb("starts", [P, E])
        slot_f = m.sb("slot_f", [P, TOPK, TILES])
        part_i = m.sb("part_i", [P, 2, TOPK, TILES], I32)
        part = m.sb("part", [P, 2, TOPK, TILES])
        expert_f = m.sb("expert_f", [P, NST])
        past = m.sb("past", [P, NST, E])
        low_hot = m.sb("low_hot", [P, RI, TOPK, P])
        high_tok = m.sb("high_tok", [P, RI, TOPK, NSUB])
        ps_x = m.ps("ps_x", [P, 4, 512])
        ps_l = m.ps("ps_l", [P, 512])
        ps_n = m.ps("ps_n", [P, 2, TILES * E])
        ps_inv = m.ps("ps_inv", [P, 512])
        names = ("const_step", "wg_in", "stats_done", "mean_done", "veps_done", "rstd_done", "xn_done", "turned", "xT_done",
                 "logits_done", "exp_done", "step", "both_done", "counted", "high_done", "inv_done", "xn_stored")
        s = {n: m.sem(n) for n in names}
        C.rows_stored, C.row_chunks = s["xn_stored"], NCH
        x_in = [m.sem(f"x_in{b}") for b in range(NCH)]
        block = ctx.enter_context(nc.Block())
        x1_v = x1_dram.rearrange("(b t p) d -> b p t d", t=CH, p=P)
        xn_v = xn_dram.rearrange("(b t p) d -> b p t d", t=CH, p=P)

        @block.sync
        def _(sp):
            for b in range(NCH):
                sp.dma_start(x[:, b * CH:(b + 1) * CH, :], x1_v[b]).then_inc(x_in[b], 16)
                if b == 0:
                    sp.dma_start(wg_sb[:, :, :], wg.rearrange("(k p) e -> p k e", p=P)).then_inc(s["wg_in"], 16)
            for b in range(NCH):
                sp.wait_ge(s["xn_done"], (b + 1) * CH)
                sp.dma_start(xn_v[b], x[:, b * CH:(b + 1) * CH, :]).then_inc(s["xn_stored"], 16)
            sp.wait_ge(s["xn_stored"], 16 * NCH)

        @block.gpsimd
        def _(pool):
            pool.memset(lower[:, :], 1.0).then_inc(s["const_step"], 1)
            pool.iota(iota_i[:, :], pattern=[[1, P]], base=0, channel_multiplier=0).then_inc(s["const_step"], 1)
            pool.iota(token_i[:, :], pattern=[[P, TILES]], base=0, channel_multiplier=1).then_inc(s["const_step"], 1)
            pool.iota(rank_i[:, :], pattern=[[-1, E]], base=E, channel_multiplier=0).then_inc(s["const_step"], 1)
            pool.wait_ge(s["const_step"], 4)
            pool.affine_select(out=lower[:, :], in_=lower[:, :], compare_op=ALU.is_ge, fill=0.0, base=-1,
                               pattern=[[1, P]], channel_multiplier=-1).then_inc(s["const_step"], 1)
            pool.tensor_copy(iota[:, :], iota_i[:, :]).then_inc(s["const_step"], 1)
            pool.tensor_copy(token[:, :], token_i[:, :]).then_inc(s["const_step"], 1)
            pool.tensor_copy(rank[:, :], rank_i[:, :]).then_inc(s["const_step"], 1)
            for b in range(NCH):
                pool.wait_ge(s["veps_done"], b + 1)
                a = b * CH
                pool.tensor_tensor(rstd[:, a:a + CH], veps[:, a:a + CH], C.half[:, 0:CH],
                                   ALU.pow).then_inc(s["rstd_done"], 1)

        @block.tensor
        def _(pe):
            def turn(i):
                pe.wait_ge(s["xn_done"], 2 * i + 2)
                wait(pe, s["xT_done"], i - 3)
                for j in range(2 * KD):
                    T, k = 2 * i + j // KD, j % KD
                    mm = pe.transpose(ps_x[:, i % 4, j * P:(j + 1) * P], x[:, T, k * P:(k + 1) * P], C.ident[:, :])
                mm.then_inc(s["turned"], 1)

            def logits(i):
                pe.wait_ge(s["xT_done"], i + 1)
                for j in range(2 * KD):
                    T, k = 2 * i + j // KD, j % KD
                    mm = pe.matmul(ps_l[:, T * E:(T + 1) * E], xT[:, i % 2, j * P:(j + 1) * P], wg_sb[:, k, :],
                                   start=(k == 0), stop=(k == KD - 1))
                mm.then_inc(s["logits_done"], 1)

            pe.wait_ge(s["wg_in"], 16)
            for i in range(PAIRS):
                turn(i)
                if i >= 2:
                    logits(i - 2)
            logits(PAIRS - 2)
            logits(PAIRS - 1)
            pe.wait_ge(s["both_done"], 1)
            pe.wait_ge(s["const_step"], 8)
            flat = both[:, :, :].rearrange("p t e -> p (t e)")
            pe.matmul(ps_n[:, 0, :], lower[:, :], flat, start=True, stop=True)
            pe.matmul(ps_n[:, 1, :], C.ones[:, :], flat, start=True, stop=True).then_inc(s["counted"], 1)

            def invert(T, r, start, stop):
                for c in range(TOPK):
                    pe.wait_ge(s["high_done"], T * TOPK + c + 1)
                    mm = pe.matmul(ps_inv[:, 0:NSUB], low_hot[:, r, c, :], high_tok[:, r, c, :], start=start and c == 0,
                                   stop=stop and c == TOPK - 1, skip_group_check=True)
                mm.then_inc(s["inv_done"], 1)

            for r in range(RI):
                invert(r, r, r == 0, False)
            with pe.Fori(1, TILES // RI - 1) as i:
                for r in range(RI):
                    invert(i * RI + r, r, False, False)
            for r in range(RI):
                invert(TILES - RI + r, r, False, r == RI - 1)

        @block.scalar
        def _(act):
            for i in range(PAIRS):
                act.wait_ge(s["turned"], i + 1)
                wait(act, s["logits_done"], i - 1)
                act.activation(xT[:, i % 2, :], ps_x[:, i % 4, :], ACT.Copy).then_inc(s["xT_done"], 1)
            act.wait_ge(s["logits_done"], PAIRS)
            act.activation(sig[:, :, :].rearrange("p t e -> p (t e)"), ps_l[:, 0:TILES * E], ACT.Exp,
                           scale=-1.0).then_inc(s["exp_done"], 1)

        @block.vector
        def _(dve):
            for b in range(NCH):
                dve.wait_ge(x_in[b], 16)
                if b:
                    dve.wait_ge(s["mean_done"], b * CH)
                for t in range(CH):
                    dve.bn_stats(stats[:, t, :], x[:, b * CH + t, :]).then_inc(s["stats_done"], 1)
                for t in range(CH):
                    dve.wait_ge(s["stats_done"], b * CH + t + 1)
                    dve.bn_aggr(mv[:, b * CH + t, :], stats[:, t, :]).then_inc(s["mean_done"], 1)
                dve.wait_ge(s["mean_done"], (b + 1) * CH)
                dve.tensor_scalar(veps[:, b * CH:(b + 1) * CH], mv[:, b * CH:(b + 1) * CH, 1], EPS, None,
                                  ALU.add).then_inc(s["veps_done"], 1)
                dve.wait_ge(s["rstd_done"], b + 1)
                for t in range(CH):
                    T = b * CH + t
                    dve.tensor_scalar(x[:, T, :], x[:, T, :], mv[:, T, 0:1], rstd[:, T:T + 1], ALU.subtract,
                                      ALU.mult).then_inc(s["xn_done"], 1)

            steps = [0]

            def link(ins):
                steps[0] += 1
                ins.then_inc(s["step"], 1)
                dve.wait_ge(s["step"], steps[0])

            def over(ap, n):
                return ap.unsqueeze(2).broadcast_to((P, ap.shape[1], n))

            rank_b = rank[:, :].unsqueeze(1).broadcast_to((P, TILES, E))
            dve.wait_ge(s["exp_done"], 1)
            dve.wait_ge(s["const_step"], 8)
            link(dve.tensor_scalar(big[0][:, :, :], sig[:, :, :], 1.0, None, ALU.add))
            link(dve.reciprocal(sig[:, :, :], big[0][:, :, :]))
            for c in range(TOPK):
                link(dve.tensor_reduce(top[:, c, :], sig[:, :, :], AX, ALU.max))
                link(dve.tensor_tensor(big[0][:, :, :], sig[:, :, :], over(top[:, c, :], E), ALU.is_equal))
                link(dve.tensor_tensor(big[1][:, :, :], big[0][:, :, :], rank_b, ALU.mult))
                link(dve.tensor_reduce(first[:, :], big[1][:, :, :], AX, ALU.max))
                link(dve.tensor_tensor(hot[:, c, :, :], rank_b, over(first[:, :], E), ALU.is_equal))
                if c == 0:
                    link(dve.scalar_tensor_tensor(out=sig[:, :, :], in0=hot[:, c, :, :], scalar=-4.0, in1=sig[:, :, :],
                                                  op0=ALU.mult, op1=ALU.add))
            link(dve.tensor_tensor(both[:, :, :], hot[:, 0, :, :], hot[:, 1, :, :], ALU.add))
            dve.wait_ge(s["step"], steps[0])
            dve.tensor_scalar(C.top[:, :, :], top[:, :, :], C.gate[:, 2:3], None, ALU.mult).then_inc(s["both_done"], 1)
            dve.wait_ge(s["counted"], 1)
            link(dve.tensor_copy(run_n[0][:, :, :], ps_n[:, 1, :].rearrange("p (t e) -> p e t", e=E)))
            cur, d = 0, 1
            while d < TILES:
                link(dve.tensor_copy(run_n[1 - cur][:, :, 0:d], run_n[cur][:, :, 0:d]))
                link(dve.tensor_tensor(run_n[1 - cur][:, :, d:TILES], run_n[cur][:, :, d:TILES],
                                       run_n[cur][:, :, 0:TILES - d], ALU.add))
                cur, d = 1 - cur, 2 * d
            link(dve.tensor_scalar(tiles_i[:, :], run_n[cur][:, :, TILES - 1], float(SLOT_T - 1), None, ALU.add))
            link(dve.tensor_scalar(tiles_i[:, :], tiles_i[:, :], SLOT_T.bit_length() - 1, None, ALU.arith_shift_right))
            link(dve.tensor_copy(tiles_f[:, :], tiles_i[:, :]))
            link(dve.tensor_copy(ends[0][:, :], tiles_f[:, :]))
            ec, d = 0, 1
            while d < E:
                link(dve.tensor_copy(ends[1 - ec][:, 0:d], ends[ec][:, 0:d]))
                link(dve.tensor_tensor(ends[1 - ec][:, d:E], ends[ec][:, d:E], ends[ec][:, 0:E - d], ALU.add))
                ec, d = 1 - ec, 2 * d
            link(dve.tensor_tensor(starts[:, :], ends[ec][:, :], tiles_f[:, :], ALU.subtract))
            link(dve.tensor_tensor(run_n[1 - cur][:, :, :], run_n[cur][:, :, :],
                                   ps_n[:, 1, :].rearrange("p (t e) -> p e t", e=E), ALU.subtract))
            link(dve.tensor_tensor(big[0][:, :, :], run_n[1 - cur][:, :, :].rearrange("p e t -> p t e"),
                                   ps_n[:, 0, :].rearrange("p (t e) -> p t e", e=E), ALU.add))
            link(dve.scalar_tensor_tensor(out=big[1][:, :, :], in0=starts[:, :].unsqueeze(1).broadcast_to((P, TILES, E)),
                                          scalar=float(SLOT_T), in1=big[0][:, :, :], op0=ALU.mult, op1=ALU.add))
            for c in range(TOPK):
                link(dve.tensor_tensor(big[0][:, :, :], big[1][:, :, :], hot[:, c, :, :], ALU.mult))
                link(dve.tensor_reduce(slot_f[:, c, :], big[0][:, :, :], AX, ALU.add))
            link(dve.tensor_copy(C.slots[:, :, :], slot_f[:, :, :]))
            link(dve.tensor_scalar(part_i[:, 0, :, :], C.slots[:, :, :], P.bit_length() - 1, None, ALU.arith_shift_right))
            link(dve.tensor_scalar(part_i[:, 1, :, :], C.slots[:, :, :], P - 1, None, ALU.bitwise_and))
            link(dve.tensor_copy(part[:, :, :, :], part_i[:, :, :, :]))
            link(dve.tensor_tensor(past[:, :, :], ends[ec][:, :].unsqueeze(1).broadcast_to((P, NST, E)),
                                   over(iota[:, 0:NST], E), ALU.is_le))
            link(dve.tensor_reduce(expert_f[:, :], past[:, :, :], AX, ALU.add))
            link(dve.tensor_scalar(C.expert[:, :], expert_f[:, :], float(E - 1), None, ALU.min))

            def one_hot(T, r):
                if not isinstance(T, int):
                    dve.wait_ge(s["inv_done"], T - RI + 1)
                for c in range(TOPK):
                    dve.tensor_scalar(low_hot[:, r, c, :], iota[:, :], part[:, 1, c, bass.ds(T, 1)], None, ALU.is_equal)
                    dve.tensor_scalar(high_tok[:, r, c, :], iota[:, 0:NSUB], part[:, 0, c, bass.ds(T, 1)],
                                      token[:, bass.ds(T, 1)], ALU.is_equal, ALU.mult).then_inc(s["high_done"], 1)

            for r in range(RI):
                one_hot(r, r)
            with dve.Fori(1, TILES // RI) as i:
                for r in range(RI):
                    one_hot(i * RI + r, r)
            dve.wait_ge(s["inv_done"], TILES)
            link(dve.tensor_copy(C.token_of[:, :], ps_inv[:, 0:NSUB]))


def experts(nc, C, xn_dram, y_dram, split, b1, b2):
    HB = FCH // 2
    PER = SUB * HB
    with ExitStack() as ctx:
        m = Mem(nc, ctx, C.sems, "exp")
        w1s, w2s = split["w1s"], split["w2s"]
        b1_rows = m.sb("b1_rows", [E * FCH, P])
        b1T = m.sb("b1T", [P, E, FCH])
        b2_all = m.sb("b2_all", [P, E, D])
        w1_now = m.sb("w1_now", [P, 2, KD, 2, F], BF16)
        b1_now = m.sb("b1_now", [P, 2, FCH])
        at_now = m.sb("at_now", [P, 2, SUB], I32)
        xg = m.sb("xg", [P, 2, SUB, D])
        xhi = m.sb("xhi", [P, KD, SLOT_T], BF16)
        xlo = m.sb("xlo", [P, KD, SLOT_T], BF16)
        h = m.sb("h", [P, FCH, SLOT_T])
        hhi = m.sb("hhi", [P, 2, FCH, SLOT_T], BF16)
        hlo = m.sb("hlo", [P, 2, FCH, SLOT_T], BF16)
        y = m.sb("y", [P, SUB, D])
        yb = m.sb("yb", [P, SUB, D])
        ps_x = m.ps("ps_x", [P, 2, 512])
        ps_h = m.ps("ps_h", [P, HB, 512])
        ps_y = m.ps("ps_y", [P, SUB, 512])
        names = ("bias_in", "b1_turned", "b1_done", "b1_now_done", "w1_now_done", "at_done", "turned_x", "xhi_done",
                 "xlo_done", "h_done", "gelu_done", "hhi_done", "hlo_done", "y_done", "y_low", "y_sum")
        s = {n: m.sem(n) for n in names}
        gathered = [[m.sem(f"gathered{v}_{u}") for u in range(SUB)] for v in range(2)]
        stored = [m.sem(f"stored{u}") for u in range(SUB)]
        C.slots_stored = stored
        for sem in stored:
            C.sems.remove(sem)
        block = ctx.enter_context(nc.Block())
        PEEL = 3

        def run(eng, step):
            for j in range(PEEL):
                step(j, j % 2, j // 2)
            with eng.Fori(0, (NST - PEEL) // 2 - 1) as i:
                for d in range(2):
                    j = PEEL + d
                    step(i * 2 + j, j % 2, i + j // 2)
            for j in range(NST - 2, NST + 1):
                step(j, j % 2, j // 2)

        def has(j):
            return not isinstance(j, int) or 0 <= j < NST

        @block.sync
        def _(sp):
            sp.dma_start(b1_rows[:, :], b1.rearrange("e (c f) -> (e c) f", f=P)).then_inc(s["bias_in"], 16)
            sp.dma_start(b2_all[:, :, :].rearrange("p e d -> p (e d)"),
                         b2.rearrange("e d -> (e d)").partition_broadcast(P)).then_inc(s["bias_in"], 16)

            def step(j, v, n):
                if has(j - 1):
                    for u in range(SUB):
                        sp.wait_ge(s["y_sum"], (j - 1) * SUB + u + 1)
                        sp.dma_start(y_dram[bass.ds((j - 1) * SLOT_T + u * P, P), :], y[:, u, :]).then_inc(stored[u], 16)

            run(sp, step)
            for u in range(SUB):
                sp.wait_ge(stored[u], 16 * NST)

        @block.gpsimd
        def _(pool):
            def step(j, v, n):
                if not has(j):
                    return
                if has(j - 2):
                    pool.wait_ge(s["turned_x"], j - 1)
                    for u in range(SUB):
                        pool.wait_ge(gathered[v][u], 16 * n)
                pool.tensor_copy(at_now[:, v, :], C.token_of[:, bass.ds(j * SUB, SUB)]).then_inc(s["at_done"], 1)
                copied = counted(pool, j + 1)
                for u in range(SUB):
                    pool.wait_ge(C.rows_stored, 16 * C.row_chunks)
                    if u == 0:
                        pool.wait_ge(s["at_done"], copied)
                    pool.indirect_dma_start(out=xg[:, v, u, :], out_offset=None, in_=xn_dram[:, :],
                                            in_offset=bass.IndirectOffsetOnAxis(ap=at_now[:, v, u:u + 1].bitcast(U32), axis=0)
                                            ).then_inc(gathered[v][u], 16)

            run(pool, step)

        @block.tensor
        def _(pe):
            def turn_x(j, v, n):
                wait(pe, s["xlo_done"], j - 1)
                for u in range(SUB):
                    pe.wait_ge(gathered[v][u], 16 * (n + 1))
                    for k in range(KD):
                        mm = pe.transpose(ps_x[:, v, k * SLOT_T + u * P:k * SLOT_T + (u + 1) * P],
                                          xg[:, v, u, k * P:(k + 1) * P], C.ident[:, :])
                mm.then_inc(s["turned_x"], 1)

            def first(j, v):
                pe.wait_ge(s["w1_now_done"], j + 1)
                pe.wait_ge(s["xhi_done"], j + 1)
                pe.wait_ge(s["xlo_done"], j + 1)
                for i in range(HB):
                    wait(pe, s["gelu_done"], HB * (j - 1) + i + 1)
                    for f in (2 * i, 2 * i + 1):
                        parts = [(k, hl, xx) for k in range(KD) for hl, xx in ((0, xhi), (0, xlo), (1, xhi))]
                        for q, (k, hl, xx) in enumerate(parts):
                            mm = pe.matmul(ps_h[:, i, f % 2 * SLOT_T:(f % 2 + 1) * SLOT_T],
                                           w1_now[:, v, k, hl, f * P:(f + 1) * P], xx[:, k, :],
                                           start=(q == 0), stop=(q == len(parts) - 1))
                    mm.then_inc(s["h_done"], 1)

            def second(j, v, e):
                for u in range(SUB):
                    wait(pe, s["y_sum"], SUB * (j - 1) + u + 1)
                    slots = slice(u * P, (u + 1) * P)
                    for f in range(FCH):
                        if u == 0 and f % 2 == 0:
                            pe.wait_ge(s["hhi_done"], HB * j + f // 2 + 1)
                        pe.matmul(ps_y[:, u, :], hhi[:, v, f, slots],
                                  w2s[:, bass.ds(e * FCH + f, 1), 0:2 * D].rearrange("p o f -> p (o f)"),
                                  start=(f == 0), stop=False)
                    for f in range(FCH):
                        if u == 0 and f % 2 == 0:
                            pe.wait_ge(s["hlo_done"], HB * j + f // 2 + 1)
                        mm = pe.matmul(ps_y[:, u, 0:D], hlo[:, v, f, slots],
                                       w2s[:, bass.ds(e * FCH + f, 1), 0:D].rearrange("p o f -> p (o f)"),
                                       start=False, stop=(f == FCH - 1))
                    mm.then_inc(s["y_done"], 1)

            pe.wait_ge(s["bias_in"], 32)
            pe.transpose(ps_y[:, 0, 0:E * FCH], b1_rows[:, :], C.ident[0:E * FCH, 0:E * FCH]).then_inc(s["b1_turned"], 1)
            pe.wait_ge(s["b1_done"], 1)

            def step(j, v, n):
                if isinstance(j, int) and j == 0:
                    turn_x(0, 0, 0)
                if has(j):
                    first(j, v)
                if has(j + 1):
                    turn_x(j + 1, 1 - v, n + v)
                if has(j - 1):
                    second(j - 1, 1 - v, pe.value_load(C.expert[0:1, bass.ds(j - 1, 1)], min_val=0, max_val=E - 1))

            run(pe, step)

        @block.scalar
        def _(act):
            act.wait_ge(s["b1_turned"], 1)
            act.activation(b1T[:, :, :].rearrange("p e c -> p (e c)"), ps_y[:, 0, 0:E * FCH], ACT.Copy).then_inc(s["b1_done"], 1)

            def high_x(j, v):
                act.wait_ge(s["turned_x"], j + 1)
                wait(act, s["h_done"], HB * j)
                act.activation(xhi[:, :, :].rearrange("p k t -> p (k t)"), ps_x[:, v, :], ACT.Copy).then_inc(s["xhi_done"], 1)

            def step(j, v, n):
                if isinstance(j, int) and j == 0:
                    high_x(0, 0)
                if has(j):
                    act.wait_ge(s["b1_now_done"], j + 1)
                    wait(act, s["y_done"], SUB * (j - 1))
                    for i in range(HB):
                        act.wait_ge(s["h_done"], HB * j + i + 1)
                        wait(act, s["hlo_done"], HB * (j - 1) + i + 1)
                        for f in (2 * i, 2 * i + 1):
                            ins = act.activation(h[:, f, :], ps_h[:, i, f % 2 * SLOT_T:(f % 2 + 1) * SLOT_T],
                                                 ACT.Gelu_apprx_tanh, bias=b1_now[:, v, f:f + 1])
                        ins.then_inc(s["gelu_done"], 1)
                        act.wait_ge(s["gelu_done"], HB * j + i + 1)
                        act.activation(hhi[:, v, 2 * i:2 * i + 2, :].rearrange("p f t -> p (f t)"),
                                       h[:, 2 * i:2 * i + 2, :].rearrange("p f t -> p (f t)"),
                                       ACT.Copy).then_inc(s["hhi_done"], 1)
                if has(j + 1):
                    high_x(j + 1, 1 - v)

            run(act, step)

        @block.vector
        def _(dve):
            def weights(j, v, e):
                wait(dve, s["h_done"], HB * (j - 1))
                dve.tensor_copy(w1_now[:, v, :, :, :].rearrange("p k c f -> p (k c f)"),
                                w1s[:, bass.ds(e * KD, KD), :, :].rearrange("p k c f -> p (k c f)")).then_inc(s["w1_now_done"], 1)
                wait(dve, s["gelu_done"], HB * (j - 1))
                dve.tensor_copy(b1_now[:, v, :], b1T[:, bass.ds(e, 1), :].rearrange("p o f -> p (o f)")
                                ).then_inc(s["b1_now_done"], 1)

            def low_x(j, v):
                dve.wait_ge(s["xhi_done"], j + 1)
                wait(dve, s["h_done"], HB * j)
                dve.tensor_tensor(xlo[:, :, :].rearrange("p k t -> p (k t)"), ps_x[:, v, :],
                                  xhi[:, :, :].rearrange("p k t -> p (k t)"), ALU.subtract).then_inc(s["xlo_done"], 1)

            def expert(j):
                return dve.value_load(C.expert[0:1, bass.ds(j, 1)], min_val=0, max_val=E - 1)

            def step(j, v, n):
                if isinstance(j, int) and j == 0:
                    dve.wait_ge(s["b1_done"], 1)
                    weights(0, 0, expert(0))
                    low_x(0, 0)
                if has(j + 1):
                    weights(j + 1, 1 - v, expert(j + 1))
                if has(j):
                    for i in range(HB):
                        dve.wait_ge(s["hhi_done"], HB * j + i + 1)
                        if i == 0:
                            wait(dve, s["y_done"], SUB * (j - 1))
                        dve.tensor_tensor(hlo[:, v, 2 * i:2 * i + 2, :].rearrange("p f t -> p (f t)"),
                                          h[:, 2 * i:2 * i + 2, :].rearrange("p f t -> p (f t)"),
                                          hhi[:, v, 2 * i:2 * i + 2, :].rearrange("p f t -> p (f t)"),
                                          ALU.subtract).then_inc(s["hlo_done"], 1)
                if has(j + 1):
                    low_x(j + 1, 1 - v)
                if has(j - 1):
                    e = expert(j - 1)
                    for u in range(SUB):
                        dve.wait_ge(s["y_done"], SUB * (j - 1) + u + 1)
                        dve.tensor_tensor(yb[:, u, :], ps_y[:, u, D:2 * D],
                                          b2_all[:, bass.ds(e, 1), :].rearrange("p o d -> p (o d)"),
                                          ALU.add).then_inc(s["y_low"], 1)
                        dve.wait_ge(s["y_low"], SUB * (j - 1) + u + 1)
                        if has(j - 2):
                            dve.wait_ge(stored[u], 16 * (j - 1))
                        dve.tensor_tensor(y[:, u, :], ps_y[:, u, 0:D], yb[:, u, :], ALU.add).then_inc(s["y_sum"], 1)

            run(dve, step)


def fold(nc, C, w, w_in, w_out, b_in, scale_of_logits):
    hpg = 2
    ng = HEADS // hpg
    dh = P // hpg
    with ExitStack() as ctx:
        m = Mem(nc, ctx, C.sems, "fold")
        wq, wi = (C.xn4[:, 8 * i:8 * i + 8, :].rearrange("p (k n) d -> p k (n d)", k=KD) for i in range(2))
        wiT, w_of = (C.xn4[:, 8 * i:8 * i + 8, :] for i in range(2, 4))
        wqT = m.sb("wqT", [P, ng, D])
        wk = m.sb("wk", [P, 2, ng * P])
        wv = m.sb("wv", [P, 2, ng * P])
        wo = m.sb("wo", [P, ng, D])
        head_mask = m.sb("head_mask", [P, hpg])
        kblk = m.sb("kblk", [P, B, ng, hpg * KEYS])
        values = m.sb("values", [P, ng, B * KEYS])
        vblk = m.sb("vblk", [P, 2, RCH * P])
        amax = m.sb("amax", [P, 2, FCH])
        inv = m.sb("inv", [P, 2, FCH])
        scale = m.sb("scale", [P, 2, FCH])
        NB = 8
        ps = m.ps("ps", [P, NB, 512])
        wq_in, wk_in, wv_in, wo_in, wi_in, w_of_in, b_in_in = (
            m.sem(n) for n in ("wq_in", "wk_in", "wv_in", "wo_in", "wi_in", "w_of_in", "b_in_in"))
        names = ("mask_step", "zeroed", "filled", "emptied", "high_done", "low_done", "vblk_done", "step", "wi_done", "wo_done")
        s = {n: m.sem(n) for n in names}
        filled, emptied, high_done, low_done = s["filled"], s["emptied"], s["high_done"], s["low_done"]
        block = ctx.enter_context(nc.Block())

        K0 = 0
        V0 = K0 + ng
        TURN0 = V0 + ng
        WI0 = TURN0 + ng // 2
        B0 = WI0 + FCH // 2
        KF, VF = KD * len(SB), RCH // 2
        END0 = B0 + B * (KF + VF)

        @block.sync
        def _(sp):
            for dst, name, sem in ((wk, "wk", wk_in), (wv, "wv", wv_in)):
                for k, (at, n) in enumerate(CTX_K):
                    sp.dma_start(dst[0:n, k, :], w[name][at:at + n, :]).then_inc(sem, 16)
            sp.dma_start(wq[:, :, :], w["wq"].rearrange("(k p) n -> p k n", p=P)).then_inc(wq_in, 16)
            sp.dma_start(w_of[:, :, :], w_out.rearrange("(f p) d -> p f d", p=P)).then_inc(w_of_in, 16)
            sp.dma_start(wi[:, :, :], w_in.rearrange("(k p) f -> p k f", p=P)).then_inc(wi_in, 16)
            sp.dma_start(wo[:, :, :], w["wo"].rearrange("(g p) n -> p g n", p=P)).then_inc(wo_in, 16)
            with nc.allow_non_contiguous_dma(reason="a short bias, one element to a partition"):
                sp.dma_start(C.b_in[:, :], b_in.rearrange("(f p) -> p f", p=P)).then_inc(b_in_in, 16)
            sp.wait_ge(b_in_in, 16)

        @block.gpsimd
        def _(pool):
            pool.memset(head_mask[:, :], 1.0).then_inc(s["mask_step"], 1)
            pool.wait_ge(s["mask_step"], 1)
            pool.affine_select(out=head_mask[:, :], in_=head_mask[:, :], compare_op=ALU.is_ge, fill=0.0, base=0,
                               pattern=[[-dh, hpg]], channel_multiplier=1).then_inc(s["mask_step"], 1)
            pool.wait_ge(s["mask_step"], 2)
            pool.affine_select(out=head_mask[:, :], in_=head_mask[:, :], compare_op=ALU.is_ge, fill=0.0, base=dh - 1,
                               pattern=[[dh, hpg]], channel_multiplier=-1).then_inc(s["mask_step"], 1)

        @block.tensor
        def _(pe):
            def bank(fill):
                if NB <= fill < B0 + NB:
                    pe.wait_ge(emptied, fill - NB + 1)
                elif fill >= B0 + NB:
                    pe.wait_ge(low_done, fill - NB - B0 + 1)
                return fill % NB

            def turn(first, source):
                for i in range(ng // 2):
                    at = bank(first + i)
                    for j in range(2 * KD):
                        g, k = 2 * i + j // KD, j % KD
                        mm = pe.transpose(ps[:, at, j * P:(j + 1) * P], source[:, k, g * P:(g + 1) * P], C.ident[:, :])
                    mm.then_inc(filled, 1)

            for first, weights, sem in ((K0, wk, wk_in), (V0, wv, wv_in)):
                pe.wait_ge(sem, 16 * 2)
                for g in range(ng):
                    at = bank(first + g)
                    for k, (_, n) in enumerate(CTX_K):
                        mm = pe.matmul(ps[:, at, 0:B * KEYS], weights[0:n, k, g * P:(g + 1) * P],
                                       C.ctxT[0:n, k, :, :], start=(k == 0), stop=(k == 1))
                    mm.then_inc(filled, 1)
            pe.wait_ge(wq_in, 16)
            turn(TURN0, wq)
            pe.wait_ge(wi_in, 16)
            turn(WI0, wi)
            pe.wait_ge(wo_in, 16)
            for b in range(B):
                fill = B0 + b * (KF + VF)
                pe.wait_ge(emptied, WI0)
                for k in range(KD):
                    for h0, h1 in SB:
                        at = bank(fill)
                        for g in range(h0 // hpg, h1 // hpg):
                            mm = pe.matmul(ps[:, at, (g * hpg - h0) * KEYS:(g * hpg + hpg - h0) * KEYS],
                                           wqT[:, g, k * P:(k + 1) * P], kblk[:, b, g, :], start=True, stop=True)
                        mm.then_inc(filled, 1)
                        fill += 1
                pe.wait_ge(s["vblk_done"], b + 1)
                for i in range(VF):
                    at = bank(fill)
                    for c in (2 * i, 2 * i + 1):
                        mine = [g for cc, g in blocks_of(hpg) if cc == c]
                        for g in mine:
                            mm = pe.matmul(ps[:, at, c % 2 * D:(c % 2 + 1) * D], vblk[:, g % 2, c * P:(c + 1) * P],
                                           wo[:, g, :], start=(g == mine[0]), stop=(g == mine[-1]))
                    mm.then_inc(filled, 1)
                    fill += 1
            pe.wait_ge(s["wi_done"], 1)
            for k in range(KD):
                for j in range(FCH // 4):
                    at = bank(END0 + k * FCH // 4 + j)
                    for f in range(4 * j, 4 * j + 4):
                        mm = pe.transpose(ps[:, at, f % 4 * P:(f % 4 + 1) * P], wiT[:, f, k * P:(k + 1) * P], C.ident[:, :])
                    mm.then_inc(filled, 1)

        @block.scalar
        def _(act):
            def block_values(b):
                for odd in range(2):
                    for h in range(hpg):
                        ins = act.activation(
                            vblk[:, odd, 0:ROWS].rearrange("p (g o h k) -> p g o h k", o=2, h=hpg,
                                                           k=KEYS)[:, :, odd, h, :],
                            values.rearrange("p (g o) (b k) -> p g o b k", o=2, b=B)[:, :, odd, b, :],
                            ACT.Identity, scale=head_mask[:, h:h + 1])
                ins.then_inc(s["vblk_done"], 1)

            def copy_turned(first, dst, by=1.0):
                for i in range(ng // 2):
                    act.wait_ge(filled, first + i + 1)
                    act.activation(dst[:, 2 * i:2 * i + 2, :].rearrange("p g d -> p (g d)"), ps[:, (first + i) % NB, :],
                                   ACT.Copy, scale=by).then_inc(emptied, 1)

            act.wait_ge(s["mask_step"], 3)
            for g in range(ng):
                act.wait_ge(filled, K0 + g + 1)
                for h in range(hpg):
                    ins = act.activation(kblk[:, :, g, h * KEYS:(h + 1) * KEYS],
                                         ps[:, (K0 + g) % NB, 0:B * KEYS].rearrange("p (b k) -> p b k", b=B),
                                         ACT.Identity, scale=head_mask[:, h:h + 1])
                ins.then_inc(emptied, 1)
            for g in range(ng):
                act.wait_ge(filled, V0 + g + 1)
                act.activation(values[:, g, :], ps[:, (V0 + g) % NB, 0:B * KEYS], ACT.Copy).then_inc(emptied, 1)
            copy_turned(TURN0, wqT, scale_of_logits)
            copy_turned(WI0, wiT)
            act.wait_ge(s["zeroed"], 1)
            act.wait_ge(emptied, WI0)
            block_values(0)
            for b in range(B):
                fill = B0 + b * (KF + VF)
                for k in range(KD):
                    for h0, h1 in SB:
                        act.wait_ge(filled, fill + 1)
                        act.activation(C.k_fold[:, b, k, 0, h0 * KEYS:h1 * KEYS], ps[:, fill % NB, 0:(h1 - h0) * KEYS],
                                       ACT.Copy).then_inc(high_done, 1)
                        fill += 1
                for i in range(VF):
                    act.wait_ge(filled, fill + 1)
                    act.activation(C.v_fold[:, b, 0, 2 * i:2 * i + 2, :].rearrange("p c d -> p (c d)"), ps[:, fill % NB, :],
                                   ACT.Copy).then_inc(high_done, 1)
                    fill += 1
                if b + 1 < B:
                    block_values(b + 1)
            for k in range(KD):
                for j in range(FCH // 4):
                    fill = END0 + k * FCH // 4 + j
                    act.wait_ge(filled, fill + 1)
                    act.activation(C.wi_q[:, k, j * 512:(j + 1) * 512], ps[:, fill % NB, :], ACT.Copy)

        @block.vector
        def _(dve):
            steps = [0]

            def link(ins):
                steps[0] += 1
                ins.then_inc(s["step"], 1)
                dve.wait_ge(s["step"], steps[0])

            def quantise(wt, i, f0, f1, out):
                c = slice(f0, f1)
                link(dve.tensor_reduce(amax[:, i, c], wt[:, c, :], AX, ALU.max, apply_absolute_value=True))
                link(dve.tensor_scalar(amax[:, i, c], amax[:, i, c], 1e-8, None, ALU.max))
                link(dve.reciprocal(inv[:, i, c], amax[:, i, c]))
                link(dve.tensor_scalar(scale[:, i, c], inv[:, i, c], 127.0, None, ALU.mult))
                for f in range(f0, f1):
                    ins = dve.tensor_scalar(wt[:, f, :], wt[:, f, :], scale[:, i, f:f + 1], MAGIC, ALU.mult, ALU.add)
                link(ins)
                link(dve.tensor_scalar(wt[:, c, :], wt[:, c, :], MAGIC, 127.0, ALU.subtract, ALU.min))
                return dve.tensor_scalar(out[:, c, :], wt[:, c, :], -128.0, None, ALU.max)

            dve.memset(vblk[:, :, :], 0.0).then_inc(s["zeroed"], 1)
            dve.wait_ge(w_of_in, 16)
            quantise(w_of, 1, 0, FCH, C.wo_q).then_inc(s["wo_done"], 1)
            dve.reciprocal(C.wo_step[:, :], scale[:, 1, :]).then_inc(s["wo_done"], 1)
            fill = B0
            for b in range(B):
                def low(out, ps_in):
                    dve.wait_ge(high_done, fill - B0 + 1)
                    dve.tensor_tensor(out[1], ps_in, out[0], ALU.subtract).then_inc(low_done, 1)

                for k in range(KD):
                    for h0, h1 in SB:
                        c = slice(h0 * KEYS, h1 * KEYS)
                        low([C.k_fold[:, b, k, hl, c] for hl in range(2)], ps[:, fill % NB, 0:(h1 - h0) * KEYS])
                        fill += 1
                for i in range(VF):
                    low([C.v_fold[:, b, hl, 2 * i:2 * i + 2, :].rearrange("p c d -> p (c d)") for hl in range(2)],
                        ps[:, fill % NB, :])
                    fill += 1
                if 3 * b < FCH:
                    if b == 0:
                        dve.wait_ge(emptied, B0)
                    ins = quantise(wiT, 0, 3 * b, min(FCH, 3 * b + 3), wiT)
                    if 3 * b + 3 >= FCH:
                        ins.then_inc(s["wi_done"], 1)
                        dve.reciprocal(C.wi_step[:, :], scale[:, 0, :])


def folded_attention(nc, C, x1_dram, y_dram, x_out, bo, gate_col, b_next, gate_next):
    RING, GR, LAST, AHEAD = 8, 4, 4, 4
    NSB = len(SB)
    with ExitStack() as ctx:
        m = Mem(nc, ctx, C.sems, "a1")
        k_now = m.sb("k_now", [P, KD, 2, ROWS], BF16)
        v_now = m.sb("v_now", [P, 2, RCH, D], BF16)
        gbo = m.sb("gbo", [P, 2, D])
        x = m.sb("x", [P, RING, D])
        at_now = m.sb("at_now", [P, GR, TOPK], I32)
        yg = m.sb("yg", [P, GR, TOPK, D])
        stats = m.sb("stats", [P, 2, 6])
        mv = m.sb("mv", [P, 2, 2])
        veps = m.sb("veps", [P, 2])
        rstd = m.sb("rstd", [P, 2])
        stats_o = m.sb("stats_o", [P, 2, 6])
        mv_o = m.sb("mv_o", [P, 2, 2])
        veps_o = m.sb("veps_o", [P, 2])
        rstd_o = m.sb("rstd_o", [P, 2])
        xn = m.sb("xn", [P, 2, D])
        xhi = m.sb("xhi", [P, 2, KD, P], BF16)
        xlo = m.sb("xlo", [P, 2, KD, P], BF16)
        nmx = m.sb("nmx", [P, HEADS])
        z = m.sb("z", [P, 2, ROWS])
        ssum = m.sb("ssum", [P, 2, HEADS])
        rsum = m.sb("rsum", [P, 2, HEADS])
        phi = m.sb("phi", [P, RCH, P], BF16)
        plo = m.sb("plo", [P, RCH, P], BF16)
        xo = m.sb("xo", [P, 2, D])
        xob = m.sb("xob", [P, 2, D])
        ps_sc = m.ps("ps_sc", [P, NSB, 512])
        ps_x = m.ps("ps_x", [P, 512])
        ps_p = m.ps("ps_p", [P, 3, 512])
        ps_o = m.ps("ps_o", [P, 512])
        bias_in, gbo_done = m.sem("bias_in"), m.sem("gbo_done")
        x_loaded = [m.sem(f"x_loaded{i}") for i in range(RING)]
        gathered = [[m.sem(f"gathered{r}_{c}") for c in range(TOPK)] for r in range(GR)]
        x_stored = [m.sem(f"x_stored{i}") for i in range(2)]
        names = ("at_done", "half_done", "x2_done", "stats_done", "mean_done", "veps_done", "rstd_done", "xn_done", "turned_x",
                 "xhi_done", "xlo_done", "k_now_done", "v_now_done", "scores_done", "nmx_done", "exp_done",
                 "rsum_done", "norm_done", "turned_p", "phi_done", "plo_done", "o_done", "xo_done", "xob_done", "xb_done",
                 "ostats_done", "omean_done", "oveps_done", "orstd_done", "xn_out", "amax_done")
        s = {n: m.sem(n) for n in names}
        full = [(0, 0, 4, P), (1, 4, 8, P), (2, 8, RCH - 1, P), (2, RCH - 1, RCH, ROWS - (RCH - 1) * P)]
        block = ctx.enter_context(nc.Block())

        def run(eng, slot):
            for t in range(TPB + LAST):
                slot(t, t % TPB, t // TPB)
            with eng.Fori(1, B - 1) as b:
                for t in range(LAST, TPB + LAST):
                    slot(b * TPB + t, t % TPB, b + t // TPB)
            for t in range(LAST, TPB + LAST):
                slot((B - 1) * TPB + t, t % TPB, B - 1 + t // TPB)

        def has(T):
            return not isinstance(T, int) or 0 <= T < TILES

        @block.sync
        def _(sp):
            def load(T, r):
                sp.dma_start(x[:, r, :], x1_dram[bass.ds(T * P, P), :]).then_inc(x_loaded[r], 16)

            for r in range(2):
                load(r, r)
            for i, bias in enumerate((bo, b_next)):
                sp.dma_start(gbo[:, i, :], bias.partition_broadcast(P)).then_inc(bias_in, 16)
            for r in range(2, AHEAD):
                load(r, r)

            def slot(T, t, b):
                if has(T - 3):
                    sp.wait_ge(s["xob_done"], T - 2)
                    sp.dma_start(x_out[bass.ds((T - 3) * P, P), :], xob[:, (t - 3) % 2, :]).then_inc(x_stored[(t - 3) % 2], 16)
                if has(T + AHEAD):
                    load(T + AHEAD, (t + AHEAD) % RING)

            run(sp, slot)
            for i in range(2):
                sp.wait_ge(x_stored[i], 16 * TILES // 2)

        @block.gpsimd
        def _(pool):
            def power(T, u):
                pool.wait_ge(s["veps_done"], T + 1)
                pool.tensor_tensor(rstd[:, u:u + 1], veps[:, u:u + 1], C.half[:, 0:1], ALU.pow).then_inc(s["rstd_done"], 1)

            def gather(T, r, turn):
                if has(T - GR):
                    pool.wait_ge(s["x2_done"], T - GR + 1)
                    for c in range(TOPK):
                        pool.wait_ge(gathered[r][c], 16 * turn)
                pool.tensor_copy(at_now[:, r, :].unsqueeze(2), C.slots[:, :, bass.ds(T, 1)]).then_inc(s["at_done"], 1)
                copied = counted(pool, T + 1)
                for c in range(TOPK):
                    pool.wait_ge(C.slots_stored[c], 16 * NST)
                    if c == 0:
                        pool.wait_ge(s["at_done"], copied)
                    pool.indirect_dma_start(out=yg[:, r, c, :], out_offset=None, in_=y_dram[:, :],
                                            in_offset=bass.IndirectOffsetOnAxis(ap=at_now[:, r, c:c + 1].bitcast(U32), axis=0)
                                            ).then_inc(gathered[r][c], 16)

            for T in range(3):
                gather(T, T, 0)
            power(0, 0)
            pool.wait_ge(bias_in, 32)
            for i, col in enumerate((gate_col, gate_next)):
                pool.tensor_scalar(gbo[:, i, :], gbo[:, i, :], C.gate[:, col:col + 1], None, ALU.mult).then_inc(gbo_done, 1)
            power(1, 1)
            pool.wait_ge(gbo_done, 2)

            def slot(T, t, b):
                if has(T - 1):
                    w = (t - 1) % 2
                    pool.wait_ge(s["rsum_done"], T)
                    zt = z[:, w, :].rearrange("p (h k) -> p h k", k=KEYS)
                    pool.tensor_tensor(zt, zt, rsum[:, w, :].unsqueeze(2).broadcast_to((P, HEADS, KEYS)),
                                       ALU.mult).then_inc(s["norm_done"], 1)
                if has(T):
                    pool.wait_ge(s["xn_done"], T + 1)
                    pool.tensor_tensor(x[:, t, :], x[:, t, :], gbo[:, 0, :], ALU.add).then_inc(s["xb_done"], 1)
                if has(T + 3):
                    gather(T + 3, (t + 3) % GR, b * (TPB // GR) + (t + 3) // GR)
                if has(T - 3):
                    pool.wait_ge(s["oveps_done"], T - 2)
                    v = (t - 3) % 2
                    pool.tensor_tensor(rstd_o[:, v:v + 1], veps_o[:, v:v + 1], C.half[:, 0:1],
                                       ALU.pow).then_inc(s["orstd_done"], 1)
                    pool.wait_ge(s["xo_done"], T - 2)
                    if has(T - 5):
                        turn = b if t >= 3 else b - 1
                        pool.wait_ge(x_stored[v], 16 * (turn * (TPB // 2) + (t - 3) % TPB // 2))
                    pool.tensor_tensor(xob[:, v, :], xo[:, v, :], gbo[:, 1, :], ALU.add).then_inc(s["xob_done"], 1)
                if has(T + 2):
                    power(T + 2, t % 2)

            run(pool, slot)

        @block.tensor
        def _(pe):
            def turn_x(T, u):
                pe.wait_ge(s["xn_done"], T + 1)
                wait(pe, s["xlo_done"], T)
                for k in range(KD):
                    mm = pe.transpose(ps_x[:, k * P:(k + 1) * P], xn[:, u, k * P:(k + 1) * P], C.ident[:, :])
                mm.then_inc(s["turned_x"], 1)

            turn_x(0, 0)

            def slot(T, t, b):
                u = t % 2
                if has(T - 2):
                    pe.wait_ge(s["norm_done"], T - 1)
                    for j, c0, c1, n in full:
                        if c0 < RCH - 1:
                            wait(pe, s["plo_done"], 3 * (T - 3) + j + 1)
                        for c in range(c0, c1):
                            mm = pe.transpose(ps_p[0:n, j, c % 4 * P:(c % 4 + 1) * P], z[:, u, c * P:c * P + n],
                                              C.ident[:, :])
                        if c1 != RCH - 1:
                            mm.then_inc(s["turned_p"], 1)
                if has(T):
                    if t == 0:
                        pe.wait_ge(s["k_now_done"], b + 1)
                    pe.wait_ge(s["xlo_done"], T + 1)
                    for j, (h0, h1) in enumerate(SB):
                        wait(pe, s["exp_done"], NSB * (T - 1) + j + 1)
                        n = (h1 - h0) * KEYS
                        parts = [(xx, k, hl) for k in range(KD) for xx, hl in ((xhi, 0), (xhi, 1), (xlo, 0))]
                        for i, (xx, k, hl) in enumerate(parts):
                            mm = pe.matmul(ps_sc[:, j, 0:n], xx[:, u, k, :], k_now[:, k, hl, h0 * KEYS:h1 * KEYS],
                                           start=(i == 0), stop=(i == len(parts) - 1))
                        mm.then_inc(s["scores_done"], 1)
                if has(T + 1):
                    turn_x(T + 1, (t + 1) % 2)
                if has(T - 2):
                    if t == 2:
                        pe.wait_ge(s["v_now_done"], b + 1)
                    wait(pe, s["xo_done"], T - 2)
                    for j, c0, c1, n in full:
                        if c0 < RCH - 1:
                            pe.wait_ge(s["plo_done"], 3 * (T - 2) + j + 1)
                        for c in range(c0, c1):
                            for pp, hl in ((phi, 0), (phi, 1), (plo, 0)):
                                last = c == RCH - 1 and pp is plo
                                mm = pe.matmul(ps_o[:, 0:D], pp[0:n, c, :], v_now[0:n, hl, c, :],
                                               start=(c == 0 and pp is phi and hl == 0), stop=last)
                    mm.then_inc(s["o_done"], 1)

            run(pe, slot)

        @block.scalar
        def _(act):
            def high_x(T, u):
                act.wait_ge(s["turned_x"], T + 1)
                wait(act, s["scores_done"], NSB * (T - 1))
                act.activation(xhi[:, u, :, :].rearrange("p k t -> p (k t)"), ps_x[:, 0:D],
                               ACT.Copy).then_inc(s["xhi_done"], 1)

            high_x(0, 0)

            def slot(T, t, b):
                u = t % 2
                if has(T - 2):
                    wait(act, s["o_done"], T - 2)
                    for j, c0, c1, n in full:
                        if c0 < RCH - 1:
                            act.wait_ge(s["turned_p"], 3 * (T - 2) + j + 1)
                        ins = act.activation(phi[0:n, c0:c1, :].rearrange("p c t -> p (c t)"),
                                             ps_p[0:n, j, c0 % 4 * P:(c0 % 4 + c1 - c0) * P], ACT.Copy)
                        if c1 != RCH - 1:
                            ins.then_inc(s["phi_done"], 1)
                def exponentials(j):
                    act.wait_ge(s["nmx_done"], NSB * T + j + 1)
                    if j == 0:
                        wait(act, s["rsum_done"], T - 1)
                    for h in range(*SB[j]):
                        ins = act.activation(z[:, u, h * KEYS:(h + 1) * KEYS],
                                             ps_sc[:, j, (h - SB[j][0]) * KEYS:(h - SB[j][0] + 1) * KEYS], ACT.Exp,
                                             bias=nmx[:, h:h + 1], accum_out=ssum[:, u, h:h + 1])
                    ins.then_inc(s["exp_done"], 1)

                if has(T):
                    exponentials(0)
                if has(T + 1):
                    high_x(T + 1, (t + 1) % 2)
                if has(T):
                    exponentials(1)
                    exponentials(2)

            run(act, slot)

        @block.vector
        def _(dve):
            def x2_first(T, r, turn):
                dve.wait_ge(x_loaded[r], 16 * (turn + 1))
                g = r % GR
                for c in range(TOPK):
                    dve.wait_ge(gathered[g][c], 16 * (turn * (RING // GR) + r // GR + 1))
                dve.scalar_tensor_tensor(out=x[:, r, :], in0=yg[:, g, 0, :], scalar=C.top[:, 0, bass.ds(T, 1)],
                                         in1=x[:, r, :], op0=ALU.mult, op1=ALU.add).then_inc(s["half_done"], 1)

            def x2_second(T, r):
                dve.wait_ge(s["half_done"], T + 1)
                dve.scalar_tensor_tensor(out=x[:, r, :], in0=yg[:, r % GR, 1, :], scalar=C.top[:, 1, bass.ds(T, 1)],
                                         in1=x[:, r, :], op0=ALU.mult, op1=ALU.add).then_inc(s["x2_done"], 1)

            def ln_stats(T, u, r):
                dve.wait_ge(s["x2_done"], T + 1)
                dve.bn_stats(stats[:, u, :], x[:, r, :]).then_inc(s["stats_done"], 1)
                dve.wait_ge(s["stats_done"], T + 1)

            def ln_mean(T, u):
                dve.bn_aggr(mv[:, u, :], stats[:, u, :]).then_inc(s["mean_done"], 1)
                dve.wait_ge(s["mean_done"], T + 1)
                dve.tensor_scalar(veps[:, u:u + 1], mv[:, u, 1:2], EPS, None, ALU.add).then_inc(s["veps_done"], 1)

            def ln(T, u, r):
                dve.wait_ge(s["rstd_done"], T + 1)
                wait(dve, s["turned_x"], T - 1)
                dve.tensor_scalar(xn[:, u, :], x[:, r, :], mv[:, u, 0:1], rstd[:, u:u + 1], ALU.subtract,
                                  ALU.mult).then_inc(s["xn_done"], 1)

            def low_x(T, u):
                dve.wait_ge(s["xhi_done"], T + 1)
                dve.tensor_tensor(xlo[:, u, :, :].rearrange("p k t -> p (k t)"), ps_x[:, 0:D],
                                  xhi[:, u, :, :].rearrange("p k t -> p (k t)"), ALU.subtract).then_inc(s["xlo_done"], 1)

            def keys(T, b):
                wait(dve, s["scores_done"], NSB * T)
                dve.tensor_copy(k_now[:, :, :, :].rearrange("p k c n -> p (k c n)"),
                                C.k_fold[:, bass.ds(b, 1), :, :, :].rearrange("p o k c n -> p (o k c n)")
                                ).then_inc(s["k_now_done"], 1)

            def values(T, b):
                wait(dve, s["o_done"], T)
                dve.tensor_copy(v_now[:, :, :, :].rearrange("p h c d -> p (h c d)"),
                                C.v_fold[:, bass.ds(b, 1), :, :, :].rearrange("p o h c d -> p (o h c d)")
                                ).then_inc(s["v_now_done"], 1)

            keys(0, 0)
            for T in range(2):
                x2_first(T, T, 0)
                x2_second(T, T)
                ln_stats(T, T, T)
                ln_mean(T, T)
            ln(0, 0, 0)
            low_x(0, 0)

            def slot(T, t, b):
                u = t % 2
                v = (t - 3) % 2
                r2 = (t + 2) % RING
                if has(T - 3):
                    dve.wait_ge(s["o_done"], T - 2)
                    dve.wait_ge(s["xb_done"], T - 2)
                    wait(dve, s["xob_done"], T - 4)
                    dve.scalar_tensor_tensor(out=xo[:, v, :], in0=ps_o[:, 0:D], scalar=C.gate[:, gate_col:gate_col + 1],
                                             in1=x[:, (t - 3) % RING, :], op0=ALU.mult,
                                             op1=ALU.add).then_inc(s["xo_done"], 1)
                if has(T - 1):
                    w = (t - 1) % 2
                    dve.wait_ge(s["exp_done"], NSB * T)
                    if has(T - 3):
                        dve.wait_ge(s["norm_done"], T - 2)
                    dve.reciprocal(rsum[:, w, :], ssum[:, w, :]).then_inc(s["rsum_done"], 1)
                if t == 2 and has(T):
                    values(T - 2, b)
                if has(T - 3):
                    dve.wait_ge(s["xo_done"], T - 2)
                    dve.bn_stats(stats_o[:, v, :], xo[:, v, :]).then_inc(s["ostats_done"], 1)
                if has(T + 1):
                    ln(T + 1, (t + 1) % 2, (t + 1) % RING)
                if has(T - 2):
                    wait(dve, s["o_done"], T - 2)
                for bank, (h0, h1) in enumerate(SB):
                    if has(T - 2):
                        for j, c0, c1, n in full:
                            if j == bank:
                                if c0 < RCH - 1:
                                    dve.wait_ge(s["phi_done"], 3 * (T - 2) + j + 1)
                                ins = dve.tensor_tensor(plo[0:n, c0:c1, :].rearrange("p c t -> p (c t)"),
                                                        ps_p[0:n, j, c0 % 4 * P:(c0 % 4 + c1 - c0) * P],
                                                        phi[0:n, c0:c1, :].rearrange("p c t -> p (c t)"), ALU.subtract)
                        ins.then_inc(s["plo_done"], 1)
                    if has(T):
                        dve.wait_ge(s["scores_done"], T * NSB + bank + 1)
                        if bank == 0:
                            wait(dve, s["exp_done"], NSB * T)
                            if has(T - 3):
                                dve.wait_ge(s["ostats_done"], T - 2)
                        dve.tensor_reduce(nmx[:, h0:h1],
                                          ps_sc[:, bank, 0:(h1 - h0) * KEYS].rearrange("p (h k) -> p h k", k=KEYS), AX,
                                          ALU.max, negate=True).then_inc(s["nmx_done"], 1)
                if t == TPB - 1 and has(T + 1):
                    keys(T + 1, b + 1)
                if has(T - 3):
                    if not has(T):
                        dve.wait_ge(s["ostats_done"], T - 2)
                    dve.bn_aggr(mv_o[:, v, :], stats_o[:, v, :]).then_inc(s["omean_done"], 1)
                if has(T + 2):
                    x2_first(T + 2, r2, b + (t + 2) // RING)
                if has(T - 3):
                    dve.wait_ge(s["omean_done"], T - 2)
                    dve.tensor_scalar(veps_o[:, v:v + 1], mv_o[:, v, 1:2], EPS, None, ALU.add).then_inc(s["oveps_done"], 1)
                if has(T + 1):
                    low_x(T + 1, (t + 1) % 2)
                if has(T + 2):
                    x2_second(T + 2, r2)
                    ln_stats(T + 2, u, r2)
                if has(T - 4):
                    w = (t - 4) % 2
                    dve.wait_ge(s["orstd_done"], T - 3)
                    dve.tensor_scalar(C.xn4[:, bass.ds(T - 4, 1), :].rearrange("p o d -> p (o d)"), xo[:, w, :],
                                      mv_o[:, w, 0:1], rstd_o[:, w:w + 1], ALU.subtract, ALU.mult).then_inc(s["xn_out"], 1)
                if has(T + 2):
                    ln_mean(T + 2, u)
                if has(T - 4):
                    dve.wait_ge(s["xn_out"], T - 3)
                    dve.tensor_reduce(C.xn4_max[:, bass.ds(T - 4, 1)],
                                      C.xn4[:, bass.ds(T - 4, 1), :].rearrange("p o d -> p (o d)"), AX, ALU.max,
                                      apply_absolute_value=True).then_inc(s["amax_done"], 1)

            run(dve, slot)




def ffn(nc, C, x3_dram, out_dram):
    G = 4
    NG = TILES // G
    GT = G * P
    with ExitStack() as octx:
        o = Mem(nc, octx, C.sems, "ffn")
        hid = o.sb("hid", [P, FCH, B * N])
        in_step = o.sb("in_step", [P, FCH])
        out_step = o.sb("out_step", [P, FCH])
        h_scale = o.sb("h_scale", [P, 2])

        def steps_of(dve, sem, count, amax_all, out, tmp):
            for ins in (lambda: dve.tensor_scalar(tmp[:, 0:1], amax_all[:, 0:1], 1e-8, None, ALU.max),
                        lambda: dve.reciprocal(tmp[:, 1:2], tmp[:, 0:1]),
                        lambda: dve.tensor_scalar(out[:, 0:1], tmp[:, 1:2], 32767.0, None, ALU.mult),
                        lambda: dve.reciprocal(out[:, 1:2], out[:, 0:1])):
                ins().then_inc(sem, 1)
                count += 1
                dve.wait_ge(sem, count)
            return count

        with ExitStack() as ctx:
            m = Mem(nc, ctx, C.sems, "f1")
            xn = C.xn4
            amax1 = m.sb("amax1", [P, 2])
            amax_all = m.sb("amax_all", [P, 2])
            amax = m.sb("amax", [P, NG, FCH])
            tmp = m.sb("tmp", [P, 2])
            x_scale = m.sb("x_scale", [P, 2])
            xr = m.sb("xr", [P, 2, 2, 2, D])
            xhi = m.sb("xhi", [P, 2, KD, GT], BF16)
            xlo = m.sb("xlo", [P, 2, KD, GT], BF16)
            ps_x = m.ps("ps_x", [P, 2, 2, 512])
            ps_h = m.ps("ps_h", [P, 4, 512])
            names = ("amax1_done", "all_done", "step", "scaled", "rounded", "turned", "hi_done", "lo_done", "h_done", "gelu_done",
                     "amax_done")
            s = {n: m.sem(n) for n in names}
            block = ctx.enter_context(nc.Block())

            def run(eng, step):
                step(0, 0)
                step(1, 1)
                with eng.Fori(0, (NG - 4) // 2) as i:
                    for d in range(2):
                        step(i * 2 + 2 + d, d)
                for g in range(NG - 2, NG + 1):
                    step(g, g % 2)

            def has(g):
                return not isinstance(g, int) or 0 <= g < NG

            @block.gpsimd
            def _(pool):
                pool.wait_ge(s["amax1_done"], 1)
                pool.partition_all_reduce(amax_all[:, 0:1], amax1[:, 0:1], P, RMAX).then_inc(s["all_done"], 1)
                pool.wait_ge(s["amax1_done"], 2)
                pool.partition_all_reduce(amax_all[:, 1:2], amax1[:, 1:2], P, RMAX).then_inc(s["all_done"], 1)

            @block.vector
            def _(dve):
                dve.tensor_reduce(amax1[:, 0:1], C.xn4_max[:, :], AX, ALU.max).then_inc(s["amax1_done"], 1)
                dve.wait_ge(s["all_done"], 1)
                n = steps_of(dve, s["step"], 0, amax_all[:, 0:1], x_scale, tmp)
                dve.tensor_scalar(in_step[:, :], C.wi_step[:, :], x_scale[:, 1:2], None, ALU.mult).then_inc(s["step"], 1)

                def integers(g, v):
                    for p in range(2):
                        pair = xn[:, bass.ds((g * 2 + p) * 2, 2), :]
                        dve.tensor_scalar(pair, pair, x_scale[:, 0:1], MAGIC, ALU.mult, ALU.add).then_inc(s["scaled"], 1)
                    for p in range(2):
                        dve.wait_ge(s["scaled"], g * 2 + p + 1)
                        wait(dve, s["turned"], g * 2 + p - 3)
                        dve.tensor_scalar(xr[:, v, p, :, :], xn[:, bass.ds((g * 2 + p) * 2, 2), :], MAGIC, None,
                                          ALU.subtract).then_inc(s["rounded"], 1)

                def low(g, v):
                    wait(dve, s["h_done"], (g - 1) * FCH)
                    for p in range(2):
                        dve.wait_ge(s["hi_done"], g * 2 + p + 1)
                        c = slice(p * 2 * P, (p + 1) * 2 * P)
                        dve.tensor_tensor(xlo[:, v, :, c], ps_x[:, v, p, :].rearrange("p (k t) -> p k t", k=KD),
                                          xhi[:, v, :, c], ALU.subtract).then_inc(s["lo_done"], 1)

                integers(0, 0)

                def step(g, v):
                    if has(g):
                        low(g, v)
                    if has(g + 1):
                        integers(g + 1, 1 - v)
                    if has(g - 1):
                        for f in range(FCH):
                            dve.wait_ge(s["gelu_done"], (g - 1) * FCH + f + 1)
                            dve.tensor_reduce(amax[:, bass.ds(g - 1, 1), f:f + 1].rearrange("p o f -> p (o f)"),
                                              hid[:, f, bass.ds((g - 1) * GT, GT)], AX, ALU.max,
                                              apply_absolute_value=True).then_inc(s["amax_done"], 1)

                run(dve, step)
                dve.wait_ge(s["amax_done"], NG * FCH)
                dve.tensor_reduce(amax1[:, 1:2], amax[:, :, :].rearrange("p g f -> p (g f)"), AX,
                                  ALU.max).then_inc(s["amax1_done"], 1)
                dve.wait_ge(s["all_done"], 2)
                steps_of(dve, s["step"], n + 1, amax_all[:, 1:2], h_scale, tmp)
                dve.tensor_scalar(out_step[:, :], C.wo_step[:, :], h_scale[:, 1:2], None, ALU.mult)

            @block.tensor
            def _(pe):
                def step(g, v):
                    if has(g):
                        for p in range(2):
                            pe.wait_ge(s["rounded"], g * 2 + p + 1)
                            wait(pe, s["lo_done"], g * 2 + p - 3)
                            for k in range(KD):
                                for r in range(2):
                                    mm = pe.transpose(ps_x[:, v, p, (2 * k + r) * P:(2 * k + r + 1) * P],
                                                      xr[:, v, p, r, k * P:(k + 1) * P], C.ident[:, :])
                            mm.then_inc(s["turned"], 1)
                    if has(g - 1):
                        pe.wait_ge(s["lo_done"], g * 2)
                        for f in range(FCH):
                            wait(pe, s["gelu_done"], (g - 1) * FCH + f - 3)
                            part = [(k, xx) for k in range(KD) for xx in (xhi, xlo)]
                            for i, (k, xx) in enumerate(part):
                                mm = pe.matmul(ps_h[:, f % 4, :], C.wi_q[:, k, f * P:(f + 1) * P], xx[:, 1 - v, k, :],
                                               start=(i == 0), stop=(i == len(part) - 1))
                            mm.then_inc(s["h_done"], 1)

                run(pe, step)

            @block.scalar
            def _(act):
                def step(g, v):
                    if has(g):
                        wait(act, s["h_done"], (g - 1) * FCH)
                        for p in range(2):
                            act.wait_ge(s["turned"], g * 2 + p + 1)
                            act.activation(xhi[:, v, :, p * 2 * P:(p + 1) * 2 * P],
                                           ps_x[:, v, p, :].rearrange("p (k t) -> p k t", k=KD), ACT.Copy).then_inc(s["hi_done"], 1)
                    if has(g - 1):
                        for f in range(FCH):
                            act.wait_ge(s["h_done"], (g - 1) * FCH + f + 1)
                            act.activation(hid[:, f, bass.ds((g - 1) * GT, GT)], ps_h[:, f % 4, :], ACT.Gelu,
                                           bias=C.b_in[:, f:f + 1], scale=in_step[:, f:f + 1]).then_inc(s["gelu_done"], 1)

                act.wait_ge(s["step"], 5)
                run(act, step)

        with ExitStack() as ctx:
            m = Mem(nc, ctx, C.sems, "f3")
            x = C.xn4[:, 0:G, :]
            y = C.xn4[:, G:2 * G, :]
            gated = C.xn4[:, 2 * G:2 * G + 2, :]
            hhi = m.sb("hhi", [P, 2, FCH, GT], BF16)
            hlo = m.sb("hlo", [P, 2, FCH, GT], BF16)
            ON_POOL = 5
            ps = m.ps("ps", [P, 2, G, 512])
            names = ("scaled", "unit_done", "hi_done", "lo_dve", "lo_pool", "o_done", "gated_done", "y_done")
            s = {n: m.sem(n) for n in names}
            x_in = [m.sem(f"x_in{r}") for r in range(G)]
            stored = [m.sem(f"stored{r}") for r in range(G)]
            block = ctx.enter_context(nc.Block())

            def run(eng, step):
                for g in range(4):
                    step(g, g % 2)
                with eng.Fori(0, (NG - 4) // 2) as i:
                    for d in range(2):
                        step(i * 2 + 4 + d, d)
                for g in range(NG, NG + 2):
                    step(g, g % 2)

            def has(g):
                return not isinstance(g, int) or 0 <= g < NG

            @block.sync
            def _(sp):
                def step(g, v):
                    for r in range(G):
                        if has(g - 2):
                            sp.wait_ge(s["y_done"], (g - 2) * G + r + 1)
                            sp.dma_start(out_dram[bass.ds((g - 2) * GT + r * P, P), :], y[:, r, :]).then_inc(stored[r], 16)
                        if has(g - 1):
                            sp.dma_start(x[:, r, :], x3_dram[bass.ds((g - 1) * GT + r * P, P), :]).then_inc(x_in[r], 16)

                run(sp, step)
                for r in range(G):
                    sp.wait_ge(stored[r], 16 * NG)

            @block.gpsimd
            def _(pool):
                def residual(g, r):
                    pool.wait_ge(s["gated_done"], g * G + r + 1)
                    pool.wait_ge(x_in[r], (g + 1) * 16)
                    if has(g - 1):
                        pool.wait_ge(stored[r], g * 16)
                    pool.tensor_tensor(y[:, r, :], gated[:, r % 2, :], x[:, r, :], ALU.add).then_inc(s["y_done"], 1)

                def step(g, v):
                    for f in range(FCH):
                        if has(g) and f < ON_POOL:
                            if f == 0 and has(g - 2):
                                pool.wait_ge(s["o_done"], (g - 1) * G)
                            pool.wait_ge(s["hi_done"], g * FCH + f + 1)
                            pool.tensor_tensor(hlo[:, v, f, :], hid[:, f, bass.ds(g * GT, GT)], hhi[:, v, f, :],
                                               ALU.subtract).then_inc(s["lo_pool"], 1)
                        if has(g - 2) and f < G:
                            residual(g - 2, f)

                run(pool, step)

            @block.scalar
            def _(act):
                def gate(g, v, r):
                    act.wait_ge(s["o_done"], g * G + r + 1)
                    if r >= 2 or has(g - 1):
                        act.wait_ge(s["y_done"], g * G + r - 1)
                    act.activation(gated[:, r % 2, :], ps[:, v, r, 0:D], ACT.Copy,
                                   scale=C.gate[:, 3:4]).then_inc(s["gated_done"], 1)

                def step(g, v):
                    for f in range(FCH):
                        if has(g):
                            if f == 0 and has(g - 2):
                                act.wait_ge(s["o_done"], (g - 1) * G)
                            act.wait_ge(s["unit_done"], g * FCH + f + 1)
                            act.activation(hhi[:, v, f, :], hid[:, f, bass.ds(g * GT, GT)], ACT.Copy).then_inc(s["hi_done"], 1)
                        if has(g - 2) and f % 2:
                            gate(g - 2, v, f // 2)

                run(act, step)

            @block.vector
            def _(dve):
                def scale(g, f):
                    h = hid[:, f, bass.ds(g * GT, GT)]
                    dve.tensor_scalar(h, h, h_scale[:, 0:1], MAGIC, ALU.mult, ALU.add).then_inc(s["scaled"], 1)

                def unit(g, f):
                    h = hid[:, f, bass.ds(g * GT, GT)]
                    dve.wait_ge(s["scaled"], g * FCH + f + 1)
                    dve.tensor_scalar(h, h, MAGIC, out_step[:, f:f + 1], ALU.subtract, ALU.mult).then_inc(s["unit_done"], 1)

                def low(g, v, f):
                    dve.wait_ge(s["hi_done"], g * FCH + f + 1)
                    dve.tensor_tensor(hlo[:, v, f, :], hid[:, f, bass.ds(g * GT, GT)], hhi[:, v, f, :],
                                      ALU.subtract).then_inc(s["lo_dve"], 1)

                def step(g, v):
                    if has(g):
                        scale(g, 0)
                        for f in range(FCH):
                            if f + 1 < FCH:
                                scale(g, f + 1)
                            unit(g, f)
                            if f - 1 >= ON_POOL:
                                low(g, v, f - 1)
                        low(g, v, FCH - 1)

                run(dve, step)

            @block.tensor
            def _(pe):
                def step(g, v):
                    if not has(g - 1):
                        return
                    w = 1 - v
                    for r in range(G):
                        if has(g - 3):
                            pe.wait_ge(s["gated_done"], (g - 3) * G + r + 1)
                        for f in range(FCH):
                            if r == 0:
                                if f < ON_POOL:
                                    pe.wait_ge(s["lo_pool"], (g - 1) * ON_POOL + f + 1)
                                else:
                                    pe.wait_ge(s["lo_dve"], (g - 1) * (FCH - ON_POOL) + f - ON_POOL + 1)
                            for i, part in enumerate((hhi, hlo)):
                                mm = pe.matmul(ps[:, w, r, 0:D], part[:, w, f, r * P:(r + 1) * P], C.wo_q[:, f, :],
                                               start=(f == 0 and i == 0), stop=(f == FCH - 1 and i == 1))
                        mm.then_inc(s["o_done"], 1)

                run(pe, step)


class Consts:
    pass


def program(nc, io, out):
    x1_dram, x3_dram, xn_dram = (nc.dram_tensor(n, (B * N, D), F32).ap() for n in ("x1", "x3", "xn2"))
    y_dram = nc.dram_tensor("y_slots", (NSUB * P, D), F32).ap()
    x_dram = io["x"].rearrange("b n d -> (b n) d")
    out_dram = out.rearrange("b n d -> (b n) d")
    with ExitStack() as ctx:
        C = Consts()
        C.sems = []
        m = Mem(nc, ctx, C.sems, "all")
        C.ident = m.sb("ident", [P, P])
        C.ones = m.sb("ones", [P, P])
        C.half = m.sb("half", [P, TPB])
        C.gate = m.sb("gate", [P, 4])
        C.ctxT = m.sb("ctxT", [P, 2, B, KEYS])
        C.top = m.sb("top", [P, TOPK, TILES])
        C.slots = m.sb("slots", [P, TOPK, TILES], I32)
        C.expert = m.sb("expert", [P, NST], I32)
        C.token_of = m.sb("token_of", [P, NSUB], I32)
        prologue(nc, io, C)
        with ExitStack() as moe:
            mm = Mem(nc, moe, C.sems, "moe")
            split = {"w1": io["L0_ffn_W1"], "w2": io["L0_ffn_W2"],
                     "w1s": mm.sb("w1s", [P, E * KD, 2, F], BF16), "w2s": mm.sb("w2s", [P, E * FCH, 2 * D], BF16)}
            w0 = {"wq": io["L0_xattn_Wq"], "bq": io["L0_xattn_bq"], "wk": io["L0_xattn_Wk"], "bk": io["L0_xattn_bk"],
                  "wv": io["L0_xattn_Wv"], "bv": io["L0_xattn_bv"], "wo": io["L0_xattn_Wo"], "bo": io["L0_xattn_bo"]}
            attention(nc, C, x_dram, x1_dram, w0, 0, split)
            routing(nc, C, x1_dram, xn_dram, io["L0_ffn_Wg"])
            experts(nc, C, xn_dram, y_dram, split, io["L0_ffn_b1"], io["L0_ffn_b2"])
        C.wi_q = m.sb("wi_q", [P, KD, F], BF16)
        C.wo_q = m.sb("wo_q", [P, FCH, D], BF16)
        C.b_in = m.sb("b_in", [P, FCH])
        C.wi_step = m.sb("wi_step", [P, FCH])
        C.wo_step = m.sb("wo_step", [P, FCH])
        C.xn4 = m.sb("xn4", [P, TILES, D])
        C.xn4_max = m.sb("xn4_max", [P, TILES])
        inner = HEADS * 64
        w1 = {"wq": io["L1_xattn_w_q"], "wk": io["L1_xattn_w_kv"][:, 0:inner], "wv": io["L1_xattn_w_kv"][:, inner:2 * inner],
              "wo": io["L1_xattn_w_out"]}
        with ExitStack() as folded:
            mm = Mem(nc, folded, C.sems, "folded")
            C.k_fold = mm.sb("k_fold", [P, B, KD, 2, ROWS], BF16)
            C.v_fold = mm.sb("v_fold", [P, B, 2, RCH, D], BF16)
            fold(nc, C, w1, io["L1_ffn_W_in"], io["L1_ffn_W_out"], io["L1_ffn_b_in"], 64 ** -0.5)
            clear_semaphores(nc, C)
            folded_attention(nc, C, x1_dram, y_dram, x3_dram, io["L1_xattn_b_out"], 1,
                             io["L1_ffn_b_out"], 3)
        ffn(nc, C, x3_dram, out_dram)


_INS = ["x", "ctx_768", "g_xattn", "g_ffn", "L0_xattn_Wq", "L0_xattn_bq", "L0_xattn_Wk", "L0_xattn_bk", "L0_xattn_Wv",
        "L0_xattn_bv", "L0_xattn_Wo", "L0_xattn_bo", "L0_ffn_Wg", "L0_ffn_W1", "L0_ffn_b1", "L0_ffn_W2", "L0_ffn_b2",
        "L1_xattn_w_q", "L1_xattn_w_kv", "L1_xattn_w_out", "L1_xattn_b_out", "L1_ffn_W_in", "L1_ffn_b_in", "L1_ffn_W_out",
        "L1_ffn_b_out"]


def kernel(**inputs):
    import numpy as _np
    import concourse.bacc as _bacc
    from concourse import mybir as _mybir
    from concourse.bass_utils import run_bass_kernel_spmd as _run

    nc = _bacc.Bacc("TRN2", target_bir_lowering=False, num_devices=1)
    arrays, io = {}, {}
    for name in _INS:
        a = _np.ascontiguousarray(inputs[name])
        arrays[f"in_{name}_dram"] = a
        io[name] = nc.dram_tensor(f"in_{name}_dram", a.shape, _mybir.dt.from_np(a.dtype), kind="ExternalInput").ap()
    out = nc.dram_tensor("out_0_dram", (B, N, D), F32, kind="ExternalOutput").ap()
    program(nc, io, out)
    r = _run(nc, [arrays], core_ids=[0])
    return r.results[0]["out_0_dram"]
```
